# Optimizing a Trainium2 kernel written in Bass

```python
import numpy as np
import jax
import jax.numpy as jnp

def _softmax(x, axis=-1):
    return jax.nn.softmax(x, axis=axis)

def _gelu(x):
    return jax.nn.gelu(x, approximate=True)

def _silu(x):
    return jax.nn.silu(x)

def _sigmoid(x):
    return jax.nn.sigmoid(x)

def _layernorm(x, axis=-1, eps=1e-05):
    m = jnp.mean(x, axis=axis, keepdims=True)
    v = jnp.var(x, axis=axis, keepdims=True)
    return (x - m) / jnp.sqrt(v + eps)

def _scatter_add(tgt, idx, src, axis=0):
    return tgt.at[idx].add(src)

def _segment_sum(src, seg, n):
    return jax.ops.segment_sum(src, seg, n)
kernel_name = 'mk_xattn_seq_d4_seqx_r8_9da980'

def setup_inputs(seed: int=0):
    np.random.seed(seed)
    _w = jnp.asarray

    def _rec_inputs():
        import jax
        import jax.numpy as jnp
        _rk = jax.random.key(seed)
        x = 7.22e-05 + 1 * jax.random.normal(jax.random.fold_in(_rk, 1), (16, 128, 256), jnp.float32)
        _lenS = 128 - jax.random.randint(jax.random.fold_in(_rk, 7), (16,), 0, max(1, 128 // 4) + 1, jnp.int32)
        _lenS2 = 128 - jax.random.randint(jax.random.fold_in(_rk, 8), (16,), 0, max(1, 128 // 4) + 1, jnp.int32)
        _ctx_1024P = jax.random.normal(jax.random.fold_in(_rk, 11), (16, 16, 128), jnp.float32)
        _ctx_1024c = jax.random.dirichlet(jax.random.fold_in(_rk, 511), 0.3 * jnp.ones((16,), jnp.float32), (16, 128))
        _ctx_1024t = jnp.einsum('bsk,bkd->bsd', _ctx_1024c, _ctx_1024P)
        _ctx_1024t = _ctx_1024t * jax.lax.rsqrt(jnp.mean(jnp.square(_ctx_1024t)) + 1e-12) * 0.953939
        ctx_1024 = -0.000514642 + 1.00011 * (_ctx_1024t + 0.3 * jax.random.normal(jax.random.fold_in(_rk, 611), (16, 128, 128), jnp.float32))
        pos_1xS = jnp.broadcast_to(jnp.arange(128, dtype=jnp.int32), (1, 128))
        _validS = jnp.arange(128)[None, :] < _lenS[:, None]
        _validS2 = jnp.arange(128)[None, :] < _lenS2[:, None]
        _causal = jnp.tril(jnp.ones((128, 128), dtype=bool))
        mask_BxS_ik0 = jnp.where(jnp.broadcast_to(_validS[:, :], (16, 128)), 0, 1).astype(jnp.int32)
        mask_BxS2_bk0 = jnp.logical_not(jnp.broadcast_to(_validS2[:, :], (16, 128)))
        return (x, ctx_1024, pos_1xS, mask_BxS_ik0, mask_BxS2_bk0)
    x, ctx_1024, pos_1xS, mask_BxS_ik0, mask_BxS2_bk0 = _rec_inputs()

    def _L0_xattn_setup():
        import jax, jax.numpy as jnp
        import numpy as np
        H = 256
        NH = 16
        HD = H // NH
        CH = 128
        CC = 128
        CHD = CC // NH
        I = 688
        B = 2
        L = 256
        LE = 128
        EPS = 1e-06

        def rms_norm(x, w):
            xf = x.astype(jnp.float32)
            var = jnp.mean(xf * xf, axis=-1, keepdims=True)
            return (w * (xf * jax.lax.rsqrt(var + EPS))).astype(x.dtype)

        def expert_mask(tt):
            vm = jnp.zeros(tt.shape, dtype=bool)
            vm = vm.at[:, :-1].set((tt[:, :-1] == 1) & (tt[:, 1:] == 1))
            return vm

        def rotate_half(x):
            d = x.shape[-1] // 2
            return jnp.concatenate([-x[..., d:], x[..., :d]], axis=-1)

        def apply_rotary(q, k, position_ids, seq_len):
            inv = 1.0 / 10000.0 ** (jnp.arange(0, HD, 2, dtype=jnp.float32) / HD)
            t = jnp.arange(seq_len, dtype=jnp.float32)
            freqs = jnp.outer(t, inv)
            emb = jnp.concatenate([freqs, freqs], axis=-1)
            cos = jnp.cos(emb)[position_ids][:, None].astype(q.dtype)
            sin = jnp.sin(emb)[position_ids][:, None].astype(q.dtype)
            return (q * cos + rotate_half(q) * sin, k * cos + rotate_half(k) * sin)

        def sdpa(q, k, v, causal):
            scale = 1.0 / np.sqrt(q.shape[-1])
            scores = jnp.einsum('bhqd,bhkd->bhqk', q * scale, k)
            if causal:
                mask = jnp.tril(jnp.ones((q.shape[-2], k.shape[-2]), dtype=bool))
                scores = jnp.where(mask, scores, jnp.finfo(jnp.float32).min)
            p = jax.nn.softmax(scores.astype(jnp.float32), axis=-1).astype(q.dtype)
            return jnp.einsum('bhqk,bhkd->bhqd', p, v)

        def heads(x, nh, hd):
            b, l, _ = x.shape
            return x.reshape(b, l, nh, hd).transpose(0, 2, 1, 3)
        key = jax.random.key(seed)
        ks = jax.random.split(key, 20)
        s = 0.02
        f32 = jnp.float32
        return {'hidden_states': jax.random.normal(ks[0], (B, L, H), f32), 'encoder_outputs': jax.random.normal(ks[1], (B, LE, CH), f32), 'token_type_ids': jax.random.randint(ks[2], (B, L), 0, 2, jnp.int32), 'position_ids': jnp.arange(L, dtype=jnp.int32)[None, :], 'ln_in_w': jnp.ones((H,), f32), 'ln_post_attn_w': jnp.ones((H,), f32), 'ln_post_cross_w': jnp.ones((H,), f32), 'v_qkv': jax.random.normal(ks[3], (H, 3 * H), f32) * s, 'l_qkv': jax.random.normal(ks[4], (H, 3 * H), f32) * s, 'v_dense': jax.random.normal(ks[5], (H, H), f32) * s, 'l_dense': jax.random.normal(ks[6], (H, H), f32) * s, 'cq_w': jax.random.normal(ks[7], (H, CC), f32) * s, 'ckv_w': jax.random.normal(ks[8], (CH, 2 * CC), f32) * s, 'cdense_w': jax.random.normal(ks[9], (CC, H), f32) * s, 'v_gate': jax.random.normal(ks[10], (H, I), f32) * s, 'v_up': jax.random.normal(ks[11], (H, I), f32) * s, 'v_down': jax.random.normal(ks[12], (I, H), f32) * s, 'l_gate': jax.random.normal(ks[13], (H, I), f32) * s, 'l_up': jax.random.normal(ks[14], (H, I), f32) * s, 'l_down': jax.random.normal(ks[15], (I, H), f32) * s}
    _L0_xattn_all = _L0_xattn_setup()
    _L0_xattn_in = {k: v for k, v in _L0_xattn_all.items() if k in ('ln_in_w', 'ln_post_attn_w', 'ln_post_cross_w', 'v_qkv', 'l_qkv', 'v_dense', 'l_dense', 'cq_w', 'ckv_w', 'cdense_w', 'v_gate', 'v_up', 'v_down', 'l_gate', 'l_up', 'l_down')}
    del _L0_xattn_all

    def _L1_xattn_setup():
        import jax, jax.numpy as jnp
        import numpy as np
        DIM = 256
        DIM_MEDIA = 128
        HEADS = 16
        DIM_HEAD = 64
        INNER = HEADS * DIM_HEAD
        FF_INNER = 4 * DIM
        B, N_TOK, N_LAT = (4, 256, 64)
        EPS = 1e-05

        def layernorm(x, g, b):
            mu = jnp.mean(x, axis=-1, keepdims=True)
            var = jnp.var(x, axis=-1, keepdims=True)
            return (x - mu) * jax.lax.rsqrt(var + EPS) * g + b
        key = jax.random.key(seed)
        ks = jax.random.split(key, 12)
        x = jax.random.normal(ks[0], (B, N_TOK, DIM), dtype=jnp.float32)
        media = jax.random.normal(ks[1], (B, N_LAT, DIM_MEDIA), dtype=jnp.float32)
        media_mask = jax.random.randint(ks[2], (B, N_LAT), 0, 2).astype(bool)
        media_mask = media_mask.at[:, 0].set(True)
        s = lambda d: 1.0 / np.sqrt(d)
        Wq = jax.random.normal(ks[3], (DIM, INNER), dtype=jnp.float32) * s(DIM)
        Wkv = jax.random.normal(ks[4], (DIM_MEDIA, 2 * INNER), dtype=jnp.float32) * s(DIM_MEDIA)
        Wo = jax.random.normal(ks[5], (INNER, DIM), dtype=jnp.float32) * s(INNER)
        W1 = jax.random.normal(ks[6], (DIM, FF_INNER), dtype=jnp.float32) * s(DIM)
        W2 = jax.random.normal(ks[7], (FF_INNER, DIM), dtype=jnp.float32) * s(FF_INNER)
        return {'x': x, 'media': media, 'media_mask': media_mask, 'ln_q_g': jnp.ones((DIM,), jnp.float32), 'ln_q_b': jnp.zeros((DIM,), jnp.float32), 'Wq': Wq, 'Wkv': Wkv, 'Wo': Wo, 'attn_gate': jax.random.normal(ks[8], (1,), jnp.float32) * 0.5, 'ln_ff_g': jnp.ones((DIM,), jnp.float32), 'ln_ff_b': jnp.zeros((DIM,), jnp.float32), 'W1': W1, 'W2': W2, 'ff_gate': jax.random.normal(ks[9], (1,), jnp.float32) * 0.5}
    _L1_xattn_all = _L1_xattn_setup()
    _L1_xattn_in = {k: v for k, v in _L1_xattn_all.items() if k in ('ln_q_g', 'ln_q_b', 'Wq', 'Wkv', 'Wo', 'attn_gate', 'ln_ff_g', 'ln_ff_b', 'W1', 'W2', 'ff_gate')}
    del _L1_xattn_all

    def _L2_xattn_setup():
        import jax, jax.numpy as jnp
        import numpy as np
        EPS = 1e-06

        def _rmsnorm(x, w):
            var = jnp.mean(jnp.square(x), axis=-1, keepdims=True)
            return x * jax.lax.rsqrt(var + EPS) * w
        key = jax.random.key(seed)
        ks = jax.random.split(key, 6)
        B, N, M = (4, 512, 256)
        d_model, memory_dim = (256, 128)
        hidden_states = jax.random.normal(ks[0], (B, N, d_model), dtype=jnp.float32)
        memory = jax.random.normal(ks[1], (B, M, memory_dim), dtype=jnp.float32)
        W_mem = jax.random.normal(ks[2], (d_model, memory_dim), dtype=jnp.float32) / np.sqrt(memory_dim)
        W_gate = jax.random.normal(ks[3], (d_model, 2 * d_model), dtype=jnp.float32) / np.sqrt(2 * d_model)
        b_gate = jax.random.normal(ks[4], (d_model,), dtype=jnp.float32) * 0.01
        norm_w = jnp.ones((d_model,), dtype=jnp.float32)
        return {'hidden_states': hidden_states, 'memory': memory, 'W_mem': W_mem, 'W_gate': W_gate, 'b_gate': b_gate, 'norm_w': norm_w}
    _L2_xattn_all = _L2_xattn_setup()
    _L2_xattn_in = {k: v for k, v in _L2_xattn_all.items() if k in ('W_mem', 'W_gate', 'b_gate', 'norm_w')}
    del _L2_xattn_all

    def _L3_xattn_setup():
        import jax, jax.numpy as jnp
        import numpy as np
        EPS = 1e-06

        def _rmsnorm(x, w):
            var = jnp.mean(jnp.square(x), axis=-1, keepdims=True)
            return x * jax.lax.rsqrt(var + EPS) * w
        key = jax.random.key(seed)
        ks = jax.random.split(key, 6)
        B, N, M = (4, 512, 256)
        d_model, memory_dim = (256, 128)
        hidden_states = jax.random.normal(ks[0], (B, N, d_model), dtype=jnp.float32)
        memory = jax.random.normal(ks[1], (B, M, memory_dim), dtype=jnp.float32)
        W_mem = jax.random.normal(ks[2], (d_model, memory_dim), dtype=jnp.float32) / np.sqrt(memory_dim)
        W_gate = jax.random.normal(ks[3], (d_model, 2 * d_model), dtype=jnp.float32) / np.sqrt(2 * d_model)
        b_gate = jax.random.normal(ks[4], (d_model,), dtype=jnp.float32) * 0.01
        norm_w = jnp.ones((d_model,), dtype=jnp.float32)
        return {'hidden_states': hidden_states, 'memory': memory, 'W_mem': W_mem, 'W_gate': W_gate, 'b_gate': b_gate, 'norm_w': norm_w}
    _L3_xattn_all = _L3_xattn_setup()
    _L3_xattn_in = {k: v for k, v in _L3_xattn_all.items() if k in ('W_mem', 'W_gate', 'b_gate', 'norm_w')}
    del _L3_xattn_all
    return {'x': x, 'ctx_1024': ctx_1024, 'pos_1xS': pos_1xS, 'mask_BxS_ik0': mask_BxS_ik0, 'mask_BxS2_bk0': mask_BxS2_bk0, 'L0_xattn_ln_in_w': _L0_xattn_in['ln_in_w'], 'L0_xattn_ln_post_attn_w': _L0_xattn_in['ln_post_attn_w'], 'L0_xattn_ln_post_cross_w': _L0_xattn_in['ln_post_cross_w'], 'L0_xattn_v_qkv': _L0_xattn_in['v_qkv'], 'L0_xattn_l_qkv': _L0_xattn_in['l_qkv'], 'L0_xattn_v_dense': _L0_xattn_in['v_dense'], 'L0_xattn_l_dense': _L0_xattn_in['l_dense'], 'L0_xattn_cq_w': _L0_xattn_in['cq_w'], 'L0_xattn_ckv_w': _L0_xattn_in['ckv_w'], 'L0_xattn_cdense_w': _L0_xattn_in['cdense_w'], 'L0_xattn_v_gate': _L0_xattn_in['v_gate'], 'L0_xattn_v_up': _L0_xattn_in['v_up'], 'L0_xattn_v_down': _L0_xattn_in['v_down'], 'L0_xattn_l_gate': _L0_xattn_in['l_gate'], 'L0_xattn_l_up': _L0_xattn_in['l_up'], 'L0_xattn_l_down': _L0_xattn_in['l_down'], 'L1_xattn_ln_q_g': _L1_xattn_in['ln_q_g'], 'L1_xattn_ln_q_b': _L1_xattn_in['ln_q_b'], 'L1_xattn_Wq': _L1_xattn_in['Wq'], 'L1_xattn_Wkv': _L1_xattn_in['Wkv'], 'L1_xattn_Wo': _L1_xattn_in['Wo'], 'L1_xattn_attn_gate': _L1_xattn_in['attn_gate'], 'L1_xattn_ln_ff_g': _L1_xattn_in['ln_ff_g'], 'L1_xattn_ln_ff_b': _L1_xattn_in['ln_ff_b'], 'L1_xattn_W1': _L1_xattn_in['W1'], 'L1_xattn_W2': _L1_xattn_in['W2'], 'L1_xattn_ff_gate': _L1_xattn_in['ff_gate'], 'L2_xattn_W_mem': _L2_xattn_in['W_mem'], 'L2_xattn_W_gate': _L2_xattn_in['W_gate'], 'L2_xattn_b_gate': _L2_xattn_in['b_gate'], 'L2_xattn_norm_w': _L2_xattn_in['norm_w'], 'L3_xattn_W_mem': _L3_xattn_in['W_mem'], 'L3_xattn_W_gate': _L3_xattn_in['W_gate'], 'L3_xattn_b_gate': _L3_xattn_in['b_gate'], 'L3_xattn_norm_w': _L3_xattn_in['norm_w']}

def reference(x, ctx_1024, pos_1xS, mask_BxS_ik0, mask_BxS2_bk0, L0_xattn_ln_in_w, L0_xattn_ln_post_attn_w, L0_xattn_ln_post_cross_w, L0_xattn_v_qkv, L0_xattn_l_qkv, L0_xattn_v_dense, L0_xattn_l_dense, L0_xattn_cq_w, L0_xattn_ckv_w, L0_xattn_cdense_w, L0_xattn_v_gate, L0_xattn_v_up, L0_xattn_v_down, L0_xattn_l_gate, L0_xattn_l_up, L0_xattn_l_down, L1_xattn_ln_q_g, L1_xattn_ln_q_b, L1_xattn_Wq, L1_xattn_Wkv, L1_xattn_Wo, L1_xattn_attn_gate, L1_xattn_ln_ff_g, L1_xattn_ln_ff_b, L1_xattn_W1, L1_xattn_W2, L1_xattn_ff_gate, L2_xattn_W_mem, L2_xattn_W_gate, L2_xattn_b_gate, L2_xattn_norm_w, L3_xattn_W_mem, L3_xattn_W_gate, L3_xattn_b_gate, L3_xattn_norm_w):
    import jax
    import jax.numpy as jnp

    def _L0_xattn_ref(hidden_states, encoder_outputs, token_type_ids, position_ids, ln_in_w, ln_post_attn_w, ln_post_cross_w, v_qkv, l_qkv, v_dense, l_dense, cq_w, ckv_w, cdense_w, v_gate, v_up, v_down, l_gate, l_up, l_down):
        import jax, jax.numpy as jnp
        import numpy as np
        H = 256
        NH = 16
        HD = H // NH
        CH = 128
        CC = 128
        CHD = CC // NH
        I = 688
        B = 2
        L = 256
        LE = 128
        EPS = 1e-06

        def rms_norm(x, w):
            xf = x.astype(jnp.float32)
            var = jnp.mean(xf * xf, axis=-1, keepdims=True)
            return (w * (xf * jax.lax.rsqrt(var + EPS))).astype(x.dtype)

        def expert_mask(tt):
            vm = jnp.zeros(tt.shape, dtype=bool)
            vm = vm.at[:, :-1].set((tt[:, :-1] == 1) & (tt[:, 1:] == 1))
            return vm

        def rotate_half(x):
            d = x.shape[-1] // 2
            return jnp.concatenate([-x[..., d:], x[..., :d]], axis=-1)

        def apply_rotary(q, k, position_ids, seq_len):
            inv = 1.0 / 10000.0 ** (jnp.arange(0, HD, 2, dtype=jnp.float32) / HD)
            t = jnp.arange(seq_len, dtype=jnp.float32)
            freqs = jnp.outer(t, inv)
            emb = jnp.concatenate([freqs, freqs], axis=-1)
            cos = jnp.cos(emb)[position_ids][:, None].astype(q.dtype)
            sin = jnp.sin(emb)[position_ids][:, None].astype(q.dtype)
            return (q * cos + rotate_half(q) * sin, k * cos + rotate_half(k) * sin)

        def sdpa(q, k, v, causal):
            scale = 1.0 / np.sqrt(q.shape[-1])
            scores = jnp.einsum('bhqd,bhkd->bhqk', q * scale, k)
            if causal:
                mask = jnp.tril(jnp.ones((q.shape[-2], k.shape[-2]), dtype=bool))
                scores = jnp.where(mask, scores, jnp.finfo(jnp.float32).min)
            p = jax.nn.softmax(scores.astype(jnp.float32), axis=-1).astype(q.dtype)
            return jnp.einsum('bhqk,bhkd->bhqd', p, v)

        def heads(x, nh, hd):
            b, l, _ = x.shape
            return x.reshape(b, l, nh, hd).transpose(0, 2, 1, 3)
        b, l, _ = hidden_states.shape
        vm = expert_mask(token_type_ids)[..., None]
        residual = hidden_states
        x = rms_norm(hidden_states, ln_in_w)
        mixed = jnp.where(vm, x @ v_qkv, x @ l_qkv)
        q, k, v = jnp.split(mixed, 3, axis=-1)
        q, k, v = (heads(q, NH, HD), heads(k, NH, HD), heads(v, NH, HD))
        q, k = apply_rotary(q, k, position_ids, l)
        ctx = sdpa(q, k, v, causal=True)
        ctx = ctx.transpose(0, 2, 1, 3).reshape(b, l, H)
        attn_out = jnp.where(vm, ctx @ v_dense, ctx @ l_dense)
        hidden_states = residual + attn_out
        ci = rms_norm(hidden_states, ln_post_cross_w)
        cq = heads(ci @ cq_w, NH, CHD)
        ckv = encoder_outputs @ ckv_w
        ck, cv = jnp.split(ckv, 2, axis=-1)
        ck, cv = (heads(ck, NH, CHD), heads(cv, NH, CHD))
        cctx = sdpa(cq, ck, cv, causal=False)
        cctx = cctx.transpose(0, 2, 1, 3).reshape(b, l, CC)
        hidden_states = hidden_states + cctx @ cdense_w
        mi = rms_norm(hidden_states, ln_post_attn_w)
        v_out = jax.nn.silu(mi @ v_gate) * (mi @ v_up) @ v_down
        l_out = jax.nn.silu(mi @ l_gate) * (mi @ l_up) @ l_down
        hidden_states = hidden_states + jnp.where(vm, v_out, l_out)
        return hidden_states

    def _L1_xattn_ref(x, media, media_mask, ln_q_g, ln_q_b, Wq, Wkv, Wo, attn_gate, ln_ff_g, ln_ff_b, W1, W2, ff_gate):
        import jax, jax.numpy as jnp
        import numpy as np
        DIM = 256
        DIM_MEDIA = 128
        HEADS = 16
        DIM_HEAD = 64
        INNER = HEADS * DIM_HEAD
        FF_INNER = 4 * DIM
        B, N_TOK, N_LAT = (4, 256, 64)
        EPS = 1e-05

        def layernorm(x, g, b):
            mu = jnp.mean(x, axis=-1, keepdims=True)
            var = jnp.var(x, axis=-1, keepdims=True)
            return (x - mu) * jax.lax.rsqrt(var + EPS) * g + b
        scale = DIM_HEAD ** (-0.5)
        qn = layernorm(x, ln_q_g, ln_q_b)
        q = qn @ Wq * scale
        kv = media @ Wkv
        k, v = jnp.split(kv, 2, axis=-1)
        split_heads = lambda t: t.reshape(t.shape[0], t.shape[1], HEADS, DIM_HEAD).transpose(0, 2, 1, 3)
        q, k, v = (split_heads(q), split_heads(k), split_heads(v))
        sim = jnp.einsum('bhid,bhjd->bhij', q, k)
        neg_inf = jnp.finfo(sim.dtype).min
        sim = jnp.where(media_mask[:, None, None, :], sim, neg_inf)
        attn = jax.nn.softmax(sim, axis=-1)
        out = jnp.einsum('bhij,bhjd->bhid', attn, v)
        out = out.transpose(0, 2, 1, 3).reshape(x.shape[0], x.shape[1], INNER)
        attn_out = out @ Wo
        x = x + jnp.tanh(attn_gate) * attn_out
        h = layernorm(x, ln_ff_g, ln_ff_b)
        h = jax.nn.gelu(h @ W1, approximate=False) @ W2
        x = x + jnp.tanh(ff_gate) * h
        return x

    def _L2_xattn_ref(hidden_states, memory, W_mem, W_gate, b_gate, norm_w):
        import jax, jax.numpy as jnp
        import numpy as np
        EPS = 1e-06

        def _rmsnorm(x, w):
            var = jnp.mean(jnp.square(x), axis=-1, keepdims=True)
            return x * jax.lax.rsqrt(var + EPS) * w
        D = hidden_states.shape[-1]
        memory_proj = jnp.einsum('bme,de->bmd', memory, W_mem)
        scores = jnp.einsum('bnd,bmd->bnm', hidden_states, memory_proj) / jnp.sqrt(jnp.float32(D))
        attn = jax.nn.softmax(scores, axis=-1)
        memory_context = jnp.einsum('bnm,bmd->bnd', attn, memory_proj)
        gate_input = jnp.concatenate([hidden_states, memory_context], axis=-1)
        gate = jax.nn.sigmoid(jnp.einsum('bnf,df->bnd', gate_input, W_gate) + b_gate)
        fused = hidden_states + gate * memory_context
        return _rmsnorm(fused, norm_w)

    def _L3_xattn_ref(hidden_states, memory, W_mem, W_gate, b_gate, norm_w):
        import jax, jax.numpy as jnp
        import numpy as np
        EPS = 1e-06

        def _rmsnorm(x, w):
            var = jnp.mean(jnp.square(x), axis=-1, keepdims=True)
            return x * jax.lax.rsqrt(var + EPS) * w
        D = hidden_states.shape[-1]
        memory_proj = jnp.einsum('bme,de->bmd', memory, W_mem)
        scores = jnp.einsum('bnd,bmd->bnm', hidden_states, memory_proj) / jnp.sqrt(jnp.float32(D))
        attn = jax.nn.softmax(scores, axis=-1)
        memory_context = jnp.einsum('bnm,bmd->bnd', attn, memory_proj)
        gate_input = jnp.concatenate([hidden_states, memory_context], axis=-1)
        gate = jax.nn.sigmoid(jnp.einsum('bnf,df->bnd', gate_input, W_gate) + b_gate)
        fused = hidden_states + gate * memory_context
        return _rmsnorm(fused, norm_w)
    x = _L0_xattn_ref(x, ctx_1024, mask_BxS_ik0, pos_1xS, L0_xattn_ln_in_w, L0_xattn_ln_post_attn_w, L0_xattn_ln_post_cross_w, L0_xattn_v_qkv, L0_xattn_l_qkv, L0_xattn_v_dense, L0_xattn_l_dense, L0_xattn_cq_w, L0_xattn_ckv_w, L0_xattn_cdense_w, L0_xattn_v_gate, L0_xattn_v_up, L0_xattn_v_down, L0_xattn_l_gate, L0_xattn_l_up, L0_xattn_l_down)
    x = _L1_xattn_ref(x, ctx_1024, mask_BxS2_bk0, L1_xattn_ln_q_g, L1_xattn_ln_q_b, L1_xattn_Wq, L1_xattn_Wkv, L1_xattn_Wo, L1_xattn_attn_gate, L1_xattn_ln_ff_g, L1_xattn_ln_ff_b, L1_xattn_W1, L1_xattn_W2, L1_xattn_ff_gate)
    x = _L2_xattn_ref(x, ctx_1024, L2_xattn_W_mem, L2_xattn_W_gate, L2_xattn_b_gate, L2_xattn_norm_w)
    x = _L3_xattn_ref(x, ctx_1024, L3_xattn_W_mem, L3_xattn_W_gate, L3_xattn_b_gate, L3_xattn_norm_w)
    return x

_drawn_inputs = setup_inputs


def setup_inputs(seed=0):
    import zlib

    import numpy as np

    out = dict(_drawn_inputs(seed))
    spreads = {'L0_xattn_ln_in_w': (1.0, 0.6),
     'L0_xattn_ln_post_attn_w': (1.0, 0.6),
     'L0_xattn_ln_post_cross_w': (1.0, 0.6),
     'L1_xattn_ln_q_g': (1.0, 0.6),
     'L1_xattn_ln_q_b': (0.0, 0.8),
     'L1_xattn_ln_ff_g': (1.0, 0.6),
     'L1_xattn_ln_ff_b': (0.0, 0.8),
     'L2_xattn_norm_w': (1.0, 0.2),
     'L3_xattn_norm_w': (1.0, 0.2)}
    factors = {'L0_xattn_v_qkv': 8.0,
     'L0_xattn_l_qkv': 2.842,
     'L0_xattn_v_dense': 8.0,
     'L0_xattn_l_dense': 2.901,
     'L0_xattn_cq_w': 64.0,
     'L0_xattn_v_gate': 6.213,
     'L0_xattn_v_up': 6.158,
     'L0_xattn_v_down': 6.277,
     'L1_xattn_W1': 2.818,
     'L2_xattn_b_gate': 64.0,
     'L3_xattn_b_gate': 47.218}
    for name, (base, spread) in spreads.items():
        noise = np.random.default_rng([zlib.crc32(name.encode()), seed]).standard_normal(out[name].shape)
        drawn = base * np.exp(spread * noise) if base else spread * noise
        out[name] = jnp.asarray(drawn.astype(out[name].dtype))
    for name, factor in factors.items():
        out[name] = (out[name] * factor).astype(out[name].dtype)
    return out
```

```python
from contextlib import ExitStack

import numpy as np

import concourse.bass as bass
from concourse import mybir

P = 128
BATCHES, SEQ, DIM, CTX = 16, 128, 256, 128
TOKENS = BATCHES * SEQ
GROUP = 4
GROUPS = BATCHES // GROUP
GT = GROUP * SEQ
FC = DIM // P
HEADS = 16
QUAD = 4
QUADS = GROUP * HEADS // QUAD
HD0, HD0C, HD1 = 16, 8, 64
MLP0, MLP1 = 688, 1024
MT = MLP0 // P
MREST = MLP0 - MT * P
HTILES = 2 * MT + 1
REST_AT = 64
HALF = HD0 // 2
SLOTS = 6
SLOT_PARTS = ((0, 0), (0, 1), (0, 2), (1, 0), (1, 1), (2, 0))
ROPE_BASE = 10000.0
EPS_RMS, EPS_LN = 1e-6, 1e-5
MASKED = -3.38e38

F32, BF16, I32, U8 = mybir.dt.float32, mybir.dt.bfloat16, mybir.dt.int32, mybir.dt.uint8
ALU = mybir.AluOpType
ACT = mybir.ActivationFunctionType
AX_X = mybir.AxisListType.X


def media_head(q, i):
    return 2 * QUAD * (q // 2) + q % 2 + 2 * i


class Signal:

    def __init__(self, sem):
        self.sem, self.start, self.total, self.per_group = sem, 0, 0, 0

    def block(self, per_group, groups=GROUPS, amount=1):
        self.start += self.total
        self.per_group, self.amount = per_group * amount, amount
        self.total = self.per_group * groups

    def upto(self, g, n):
        return g * self.per_group + (self.start + n * self.amount)


def over_groups(eng, body):
    body(0, True)
    with eng.Fori(1, GROUPS) as g:
        body(g, False)


def build(nc, a, out):
    with ExitStack() as ctx:
        persistent(nc, ctx, a, out)


def persistent(nc, ctx, a, out):
    count = [0]

    def sb(name, shape, dt=F32, on=ctx):
        count[0] += 1
        return on.enter_context(nc.sbuf_tensor(f"{name}_{count[0]}", shape, dt))

    def signal(name):
        return Signal(ctx.enter_context(nc.semaphore(name)))

    x_t = sb("x_t", [P, FC, TOKENS])
    expert = sb("expert", [P, 2, TOKENS], BF16)
    rest_mask = sb("rest_mask", [P, TOKENS], BF16)
    key_bias = sb("key_bias", [1, TOKENS], BF16)
    ident = sb("ident", [P, P])
    ident_b = sb("ident_b", [P, P], BF16)
    causal = sb("causal", [P, P], BF16)
    ones_row = sb("ones_row", [1, P], BF16)
    mean_w = sb("mean_w", [P, P])
    rope = sb("rope", [P, 2, 2, SEQ])
    scales = sb("scales", [P, 9, FC])
    eps_cols = sb("eps_cols", [P, 2])
    gates = sb("gates", [P, 2])
    weights_a = sb("weights_a", [P, 8704])
    weights_b = sb("weights_b", [P, 6144])
    pair = [ctx.enter_context(nc.psum_tensor(f"pair{i}", [P, 2, GT], F32)) for i in range(4)]
    bank = [pair[i // 2][:, i % 2, :] for i in range(8)]
    s_pair, t_pair, c_pair, g_pair = pair

    (W_LN_IN, W_LN_CROSS, W_LN_MLP, LNQ_G, LNQ_B, LNF_G, LNF_B, NORM2, NORM3) = range(9)

    names = """loaded stores setup_d setup_a setup_p
        sq_ready mean_ready centre_ready dev_ready rstd_ready xn_ready xv_ready xl_ready
        proj_ready proj_out_d proj_out_a rot_part rot_ready hi_ready res_ready mid_ready lo_ready
        stacked v_ready v_out_a v_out_d ctx_loaded
        scores_ready max_ready p_ready turned_ready pt_ready ctx_ready recip_ready norm_ready
        back_ready back_out mix_ready out_ready x_done act_ready hid_ready hid_free
        memt_ready mem_out bias_half""".split()
    s = {n: signal(n) for n in names}
    w_ready = [signal(f"w_ready{i}") for i in range(7)]

    def wa(at, *shape):
        n = int(np.prod(shape))
        v = weights_a[:, at:at + n]
        return split_free(v, shape), at + n

    def wb(at, *shape):
        n = int(np.prod(shape))
        v = weights_b[:, at:at + n]
        return split_free(v, shape), at + n

    def split_free(v, shape):
        if len(shape) == 1:
            return v
        if len(shape) == 2:
            return v.rearrange("p (a b) -> p a b", b=shape[1])
        return v.rearrange("p (a b c) -> p a b c", b=shape[1], c=shape[2])

    at = 0
    w_qk, at = wa(at, 2, FC, 2 * DIM)
    w_v, at = wa(at, 2, FC, DIM)
    w_dense, at = wa(at, 2, FC, DIM)
    at = 0
    w_cq, at = wb(at, FC, P)
    w_ck, at = wb(at, P)
    w_cv, at = wb(at, P)
    w_cdense, at = wb(at, DIM)
    at = 0
    w_gate, at = wa(at, FC, HTILES * P)
    w_up, at = wa(at, FC, HTILES * P)
    w_down, at = wa(at, HTILES, DIM)
    at = 0
    w_q1, at = wb(at, FC, HEADS * HD1)
    w_k1, at = wb(at, HEADS * HD1)
    w_v1, at = wb(at, HEADS * HD1)
    w_o1, at = wb(at, 8, DIM)
    assert at <= 6144
    at = 0
    w_ff1, at = wa(at, FC, MLP1)
    w_ff2, at = wa(at, 8, DIM)
    fuse_w = []
    for take in (wb, wa):
        w_mem, at = take(0, DIM)
        w_g, at = take(at, 4, DIM)
        b_g, at = take(at, FC)
        fuse_w.append((w_mem, w_g, b_g))

    loads = [
        [(w_qk[:, 0], a["v_qk"].rearrange("(c p) n -> p c n", p=P)), (w_qk[:, 1], a["l_qk"].rearrange("(c p) n -> p c n", p=P)),
         (w_v[:, 0], a["v_v"].rearrange("(c p) n -> p c n", p=P)), (w_v[:, 1], a["l_v"].rearrange("(c p) n -> p c n", p=P)),
         (w_dense[:, 0], a["v_dense"].rearrange("(c p) n -> p c n", p=P)),
         (w_dense[:, 1], a["l_dense"].rearrange("(c p) n -> p c n", p=P))],
        [(w_cq, a["cq"].rearrange("(c p) n -> p c n", p=P)), (w_ck, a["ck"]), (w_cv, a["cv"]), (w_cdense, a["cdense"])],
        [(w_gate, a["gate0"].rearrange("(c p) n -> p c n", p=P)), (w_up, a["up0"].rearrange("(c p) n -> p c n", p=P)),
         (w_down, a["down0"].rearrange("(c p) n -> p c n", p=P))],
        [(w_q1, a["wq"].rearrange("(c p) n -> p c n", p=P)), (w_k1, a["wk"]), (w_v1, a["wv"]),
         (w_o1, a["wo"].rearrange("(c p) n -> p c n", p=P))],
        [(w_ff1, a["w1"].rearrange("(c p) n -> p c n", p=P)), (w_ff2, a["w2"].rearrange("(c p) n -> p c n", p=P))],
        [(fuse_w[0][0], a["mem2"]), (fuse_w[0][1], a["g2"].rearrange("(c p) n -> p c n", p=P)), (fuse_w[0][2], a["b2"])],
        [(fuse_w[1][0], a["mem3"]), (fuse_w[1][1], a["g3"].rearrange("(c p) n -> p c n", p=P)), (fuse_w[1][2], a["b3"])],
    ]
    for w, some in zip(w_ready, loads):
        w.block(len(some), groups=1, amount=16)

    def load_weights(eng, n):
        for dst, src in loads[n]:
            eng.dma_start(dst, src).then_inc(w_ready[n].sem, 16)

    def weights_there(eng, n):
        eng.wait_ge(w_ready[n].sem, w_ready[n].total)

    def tok(view, g):
        return view[..., bass.ds(g * GT, GT)]

    with ExitStack() as own:
        tt = sb("tt", [P, TOKENS], I32, own)
        is_one = sb("is_one", [P, BATCHES, SEQ], F32, own)
        keys = sb("keys", [1, TOKENS // 4], I32, own)
        pos_i = sb("pos_i", [P, SEQ], I32, own)
        pos_f = sb("pos_f", [P, SEQ], F32, own)
        pos_neg = sb("pos_neg", [P, SEQ], F32, own)
        onehot = sb("onehot", [P, SEQ], F32, own)
        consts = sb("consts", [P, 2 * P + 1], F32, own)
        raw_gates = sb("raw_gates", [P, 2], F32, own)
        s["setup_d"].block(15, 1)
        s["setup_p"].block(4, 1)
        s["setup_a"].block(1, 1)
        s["loaded"].block(9, 1, 16)
        s["proj_ready"].block(1, 1)
        with nc.Block() as block:
            @block.sync
            def _(eng):
                for dst, src in ((x_t[:], a["x"]), (tt[:], a["tt"].partition_broadcast(P)),
                                 (consts[:], a["consts"]), (ident[:], a["ident"]),
                                 (pos_i[:], a["pos"].partition_broadcast(P)), (keys[:], a["keys"]),
                                 (scales[:], a["scales"]), (raw_gates[:], a["gates"].partition_broadcast(P)),
                                 (causal[:], a["causal"])):
                    eng.dma_start(dst, src).then_inc(s["loaded"].sem, 16)
                load_weights(eng, 0)
                load_weights(eng, 1)

            @block.gpsimd
            def _(eng):
                eng.memset(mean_w[:], 1.0 / DIM).then_inc(s["setup_p"].sem, 1)
                eng.memset(ones_row[:], 1.0).then_inc(s["setup_p"].sem, 1)
                eng.memset(eps_cols[:, 0:1], EPS_RMS).then_inc(s["setup_p"].sem, 1)
                eng.memset(eps_cols[:, 1:2], EPS_LN).then_inc(s["setup_p"].sem, 1)

            @block.scalar
            def _(eng):
                eng.wait_ge(s["loaded"].sem, s["loaded"].total)
                eng.activation(gates[:], raw_gates[:], ACT.Tanh).then_inc(s["setup_a"].sem, 1)

            @block.vector
            def _(eng):
                done = [0]

                def step(ins):
                    done[0] += 1
                    ins.then_inc(s["setup_d"].sem, 1)
                    eng.wait_ge(s["setup_d"].sem, done[0])

                eng.wait_ge(s["loaded"].sem, s["loaded"].total)
                step(eng.tensor_copy(pos_f[:], pos_i[:]))
                step(eng.tensor_scalar(pos_neg[:], pos_f[:], 0.0, float(SEQ), ALU.is_lt, ALU.mult))
                step(eng.tensor_tensor(pos_f[:], pos_f[:], pos_neg[:], ALU.add))
                step(eng.tensor_scalar(pos_f[:], pos_f[:], 0.0, float(SEQ - 1), ALU.max, ALU.min))
                step(eng.tensor_scalar(onehot[:], pos_f[:], consts[:, 2 * P:2 * P + 1], None, ALU.is_equal))
                step(eng.tensor_copy(ident_b[:], ident[:]))
                step(eng.tensor_scalar(is_one[:].rearrange("p b n -> p (b n)"), tt[:], 1.0, None, ALU.is_equal))
                vis = expert[:, 0, :].rearrange("p (b n) -> p b n", n=SEQ)
                step(eng.tensor_tensor(vis[:, :, 0:SEQ - 1], is_one[:, :, 0:SEQ - 1], is_one[:, :, 1:SEQ], ALU.mult))
                step(eng.memset(vis[:, :, SEQ - 1:SEQ], 0.0))
                step(eng.tensor_scalar(expert[:, 1, :], expert[:, 0, :], -1.0, 1.0, ALU.mult, ALU.add))
                step(eng.tensor_copy(rest_mask[0:REST_AT, :], expert[0:REST_AT, 0, :]))
                step(eng.tensor_copy(rest_mask[REST_AT:P, :], expert[REST_AT:P, 1, :]))
                step(eng.tensor_scalar(key_bias[:], keys[:].bitcast(U8), -1.0, -MASKED, ALU.add, ALU.mult))
                eng.wait_ge(s["proj_ready"].sem, s["proj_ready"].upto(0, 1))
                tables = bank[0][:, 0:2 * SEQ].rearrange("p (a n) -> p a n", a=2)
                step(eng.tensor_scalar(rope[:, 0], tables, HD0 ** -0.5, None, ALU.mult))
                step(eng.tensor_copy(rope[:, 1], tables))

            @block.tensor
            def _(eng):
                eng.wait_ge(s["setup_d"].sem, 5)
                eng.matmul(bank[0][:, 0:SEQ], consts[:, 0:P], onehot[:], start=True, stop=True)
                eng.matmul(bank[0][:, SEQ:2 * SEQ], consts[:, P:2 * P], onehot[:], start=True,
                           stop=True).then_inc(s["proj_ready"].sem, 1)

    class Norm:

        def __init__(self, own, scale, bias=None, src=None):
            self.scale, self.bias, self.src = scale, bias, src
            self.eps_col = eps_cols[:, 0:1] if bias is None else eps_cols[:, 1:2]
            self.sq = sb(f"sq{scale}", [P, FC, GT], F32, own)
            self.xn = sb(f"xn{scale}", [P, FC, GT], F32, own)
            self.dev = sb(f"dev{scale}", [P, GT], F32, own)
            self.rstd = sb(f"rstd{scale}", [P, GT], F32, own)
            if bias is not None:
                self.centred = sb(f"centred{scale}", [P, FC, GT], F32, own)
            for n, k in (("sq_ready", 1), ("mean_ready", 1 if bias is None else 2), ("centre_ready", 0 if bias is None else FC),
                         ("dev_ready", 1), ("rstd_ready", 1), ("xn_ready", FC if bias is None else 2 * FC)):
                s[n].block(k)

        def x(self, g):
            return tok(x_t[:], g) if self.src is None else self.src[:]

        def scalar(self, eng, g):
            if self.bias is not None:
                eng.wait_ge(s["centre_ready"].sem, s["centre_ready"].upto(g, FC))
                eng.activation(self.sq[:], self.centred[:], ACT.Square).then_inc(s["sq_ready"].sem, 1)
            else:
                eng.activation(self.sq[:], self.x(g), ACT.Square).then_inc(s["sq_ready"].sem, 1)
            n = s["mean_ready"].per_group
            eng.wait_ge(s["mean_ready"].sem, s["mean_ready"].upto(g, n))
            eng.activation(self.dev[:], bank[7], ACT.Sqrt, bias=self.eps_col).then_inc(s["dev_ready"].sem, 1)

        def tensor(self, eng, g):
            if self.bias is not None:
                for c in range(FC):
                    mm = eng.matmul(bank[6], mean_w[:], x_t[:, c, bass.ds(g * GT, GT)], start=c == 0, stop=c == FC - 1)
                mm.then_inc(s["mean_ready"].sem, 1)
            eng.wait_ge(s["sq_ready"].sem, s["sq_ready"].upto(g, 1))
            for c in range(FC):
                mm = eng.matmul(bank[7], mean_w[:], self.sq[:, c, :], start=c == 0, stop=c == FC - 1)
            mm.then_inc(s["mean_ready"].sem, 1)

        def vector(self, eng, g):
            if self.bias is not None:
                eng.wait_ge(s["mean_ready"].sem, s["mean_ready"].upto(g, 1))
                for c in range(FC):
                    eng.tensor_tensor(self.centred[:, c, :], x_t[:, c, bass.ds(g * GT, GT)], bank[6],
                                      ALU.subtract).then_inc(s["centre_ready"].sem, 1)
                eng.wait_ge(s["centre_ready"].sem, s["centre_ready"].upto(g, FC))
            eng.wait_ge(s["dev_ready"].sem, s["dev_ready"].upto(g, 1))
            eng.reciprocal(self.rstd[:], self.dev[:]).then_inc(s["rstd_ready"].sem, 1)
            eng.wait_ge(s["rstd_ready"].sem, s["rstd_ready"].upto(g, 1))
            for c in range(FC):
                src = self.centred[:, c, :] if self.bias is not None else self.x(g)[:, c]
                eng.scalar_tensor_tensor(out=self.xn[:, c, :], in0=src, scalar=scales[:, self.scale, c:c + 1],
                                         in1=self.rstd[:], op0=ALU.mult, op1=ALU.mult).then_inc(s["xn_ready"].sem, 1)
            if self.bias is not None:
                for c in range(FC):
                    eng.wait_ge(s["xn_ready"].sem, s["xn_ready"].upto(g, c + 1))
                    eng.tensor_scalar(self.xn[:, c, :], self.xn[:, c, :], scales[:, self.bias, c:c + 1], None,
                                      ALU.add).then_inc(s["xn_ready"].sem, 1)

        def there(self, eng, g):
            eng.wait_ge(s["xn_ready"].sem, s["xn_ready"].upto(g, s["xn_ready"].per_group))

    def product(eng, to, factors):
        for n, (w, x) in enumerate(factors):
            mm = eng.matmul(to, w, x, start=n == 0, stop=n == len(factors) - 1)
        return mm

    class Attention:

        def __init__(self, own, hd, score, bias, value, turns, after, post, head=None):
            self.head = head or (lambda q, i: q * QUAD + i)
            self.hd, self.score, self.bias, self.value = hd, score, bias, value
            self.turns, self.after, self.post = turns, after, post
            self.posts = QUADS // after
            self.width = QUAD * hd
            self.p = sb(f"p{hd}", [P, 2, QUAD, SEQ], F32, own)
            self.pt = sb(f"pt{hd}", [P, 3, QUAD, SEQ], F32, own)
            self.nmax = sb(f"nmax{hd}", [P, 2, QUAD], F32, own)
            self.recip = sb(f"recip{hd}", [P, 2, QUAD], F32, own)
            self.ctx = sb(f"ctx{hd}", [P, 2, turns * P], F32, own)
            for n in ("scores_ready", "max_ready", "p_ready", "turned_ready", "pt_ready", "ctx_ready",
                      "recip_ready", "norm_ready"):
                s[n].block(QUADS)
            s["back_ready"].block(self.posts)

        def steps(self):
            return QUADS + 5

        def tensor(self, eng, g):
            def post(j):
                eng.wait_ge(s["norm_ready"].sem, s["norm_ready"].upto(g, self.after * (j + 1)))
                if j >= 2:
                    self.post_free(eng, g, j - 2)
                for t in range(self.turns):
                    mm = eng.transpose(g_pair[:, j % 2, t * P:(t + 1) * P], self.ctx[:, j % 2, t * P:(t + 1) * P],
                                       ident[:])
                mm.then_inc(s["back_ready"].sem, 1)

            for n in range(self.steps()):
                if n < QUADS:
                    if n >= 2:
                        eng.wait_ge(s["p_ready"].sem, s["p_ready"].upto(g, n - 1))
                    b, q = divmod(n, HEADS // QUAD)
                    self.bias(eng, g, s_pair[:, n % 2, :], b)
                    for h in range(QUAD):
                        w, x = self.score(b, self.head(q, h))
                        mm = eng.matmul(s_pair[:, n % 2, h * SEQ:(h + 1) * SEQ], w, x, start=self.bias is no_bias,
                                        stop=True, skip_group_check=True)
                    mm.then_inc(s["scores_ready"].sem, 1)
                if n >= 3 and n - 3 < QUADS:
                    m = n - 3
                    eng.wait_ge(s["pt_ready"].sem, s["pt_ready"].upto(g, m + 1))
                    if m >= 2:
                        eng.wait_ge(s["norm_ready"].sem, s["norm_ready"].upto(g, m - 1))
                    b, q = divmod(m, HEADS // QUAD)
                    for h in range(QUAD):
                        mm = eng.matmul(c_pair[:, m % 2, h * (self.hd + 1):(h + 1) * (self.hd + 1)],
                                        self.pt[:, m % 3, h, :], self.value(b, self.head(q, h)), start=True, stop=True,
                                        skip_group_check=True)
                    mm.then_inc(s["ctx_ready"].sem, 1)
                if 1 <= n <= QUADS:
                    m = n - 1
                    eng.wait_ge(s["p_ready"].sem, s["p_ready"].upto(g, m + 1))
                    if m >= 2:
                        eng.wait_ge(s["pt_ready"].sem, s["pt_ready"].upto(g, m - 1))
                    for h in range(QUAD):
                        mm = eng.transpose(t_pair[:, m % 2, h * SEQ:(h + 1) * SEQ], self.p[:, m % 2, h, :], ident[:])
                    mm.then_inc(s["turned_ready"].sem, 1)
                if n >= 4 and (n - 4) < QUADS and (n - 4 + 1) % self.after == 0:
                    post((n - 4) // self.after)

        def scalar(self, eng, g):
            for n in range(QUADS):
                eng.wait_ge(s["max_ready"].sem, s["max_ready"].upto(g, n + 1))
                if n >= 2:
                    eng.wait_ge(s["turned_ready"].sem, s["turned_ready"].upto(g, n - 1))
                for h in range(QUAD):
                    e = eng.activation(self.p[:, n % 2, h, :], s_pair[:, n % 2, h * SEQ:(h + 1) * SEQ], ACT.Exp,
                                       bias=self.nmax[:, n % 2, h:h + 1])
                e.then_inc(s["p_ready"].sem, 1)

        def vector(self, eng, g):
            for n in range(self.steps()):
                if n < QUADS:
                    eng.wait_ge(s["scores_ready"].sem, s["scores_ready"].upto(g, n + 1))
                    if n >= 2:
                        eng.wait_ge(s["p_ready"].sem, s["p_ready"].upto(g, n - 1))
                    eng.tensor_reduce(self.nmax[:, n % 2, :], s_pair[:, n % 2, :].rearrange("p (h k) -> p h k", h=QUAD),
                                      AX_X, ALU.max, negate=True).then_inc(s["max_ready"].sem, 1)
                if n >= 3 and n - 3 < QUADS:
                    m = n - 3
                    c = c_pair[:, m % 2, 0:QUAD * (self.hd + 1)].rearrange("p (h d) -> p h d", h=QUAD)
                    j, part = divmod(m, self.after)
                    eng.wait_ge(s["ctx_ready"].sem, s["ctx_ready"].upto(g, m + 1))
                    if m >= 2:
                        eng.wait_ge(s["norm_ready"].sem, s["norm_ready"].upto(g, m - 1))
                    eng.reciprocal(self.recip[:, m % 2, :], c[:, :, self.hd]).then_inc(s["recip_ready"].sem, 1)
                    eng.wait_ge(s["recip_ready"].sem, s["recip_ready"].upto(g, m + 1))
                    if j >= 2:
                        eng.wait_ge(s["back_ready"].sem, s["back_ready"].upto(g, j - 1))
                    eng.tensor_tensor(
                        self.ctx[:, j % 2, part * self.width:(part + 1) * self.width].rearrange("p (h d) -> p h d", h=QUAD),
                        c[:, :, 0:self.hd], self.recip[:, m % 2, :].unsqueeze(2).to_broadcast([P, QUAD, self.hd]),
                        ALU.mult).then_inc(s["norm_ready"].sem, 1)
                if 1 <= n <= QUADS:
                    m = n - 1
                    eng.wait_ge(s["turned_ready"].sem, s["turned_ready"].upto(g, m + 1))
                    if m >= 3:
                        eng.wait_ge(s["ctx_ready"].sem, s["ctx_ready"].upto(g, m - 2))
                    eng.tensor_copy(self.pt[:, m % 3].rearrange("p h k -> p (h k)"),
                                    t_pair[:, m % 2, :]).then_inc(s["pt_ready"].sem, 1)
                if n >= 5 and (n - 5) < QUADS and (n - 5 + 1) % self.after == 0:
                    j = (n - 5) // self.after
                    eng.wait_ge(s["back_ready"].sem, s["back_ready"].upto(g, j + 1))
                    self.post(eng, g, j)

        def post_free(self, eng, g, j):
            per = s["back_out"].per_group // self.posts
            eng.wait_ge(s["back_out"].sem, s["back_out"].upto(g, per * (j + 1)))

    def no_bias(eng, g, to, b):
        pass

    class Split:

        def __init__(self, own, srcs):
            self.srcs, self.n = srcs, len(srcs)
            self.parts = [sb(f"parts{srcs[0].shape[1]}_{i}", [P, 3, 2, GT], BF16, own) for i in range(self.n)]
            self.res = sb(f"res{self.n}", [P, 2, GT], F32, own)
            for n in ("hi_ready", "mid_ready", "lo_ready", "res_ready"):
                s[n].block(self.n)

        def scalar(self, eng, g):
            for i, src in enumerate(self.srcs):
                self.src_there(eng, g, i)
                eng.activation(self.parts[i][:, 0], src[:], ACT.Copy).then_inc(s["hi_ready"].sem, 1)
                eng.wait_ge(s["res_ready"].sem, s["res_ready"].upto(g, i + 1))
                eng.activation(self.parts[i][:, 1], self.res[:], ACT.Copy).then_inc(s["mid_ready"].sem, 1)

        def vector(self, eng, g, i):
            if i:
                eng.wait_ge(s["lo_ready"].sem, s["lo_ready"].upto(g, i))
            eng.wait_ge(s["hi_ready"].sem, s["hi_ready"].upto(g, i + 1))
            eng.tensor_tensor(self.res[:], self.srcs[i][:], self.parts[i][:, 0], ALU.subtract)\
               .then_inc(s["res_ready"].sem, 1)
            eng.wait_ge(s["res_ready"].sem, s["res_ready"].upto(g, i + 1))
            eng.wait_ge(s["mid_ready"].sem, s["mid_ready"].upto(g, i + 1))
            eng.tensor_tensor(self.parts[i][:, 2], self.res[:], self.parts[i][:, 1], ALU.subtract)\
               .then_inc(s["lo_ready"].sem, 1)

        def wait_parts(self, eng, g, i):
            for n in ("hi_ready", "mid_ready", "lo_ready"):
                eng.wait_ge(s[n].sem, s[n].upto(g, i + 1))

    def stack_rows(eng, stack, parts, which, base, rows):
        for slot, pq in enumerate(SLOT_PARTS):
            at = base + slot * rows
            eng.dma_start(stack[at:at + rows, :, :], parts[:, pq[which], :]).then_inc(s["stacked"].sem, 16)

    def residual(eng, g, banks, ready, n):
        eng.wait_ge(ready.sem, ready.upto(g, n))
        for m in range(FC):
            xs = x_t[:, m, bass.ds(g * GT, GT)]
            eng.tensor_tensor(xs, xs, banks[m], ALU.add).then_inc(s["x_done"].sem, 1)

    def group_start(eng, g, first):
        if not first:
            eng.wait_ge(s["x_done"].sem, s["x_done"].upto(g, 0))

    def self_attention():
        with ExitStack() as own:
            norm = Norm(own, W_LN_IN)
            xe = sb("xe", [P, 2, FC, GT], F32, own)
            rot_c = sb("rot_c", [P, 2, GT], F32, own)
            rot_s = sb("rot_s", [P, 2, GT], F32, own)
            rot = [sb(f"rot{i}", [P, 2, GT], F32, own) for i in range(2)]
            split = Split(own, rot)
            q_stack = sb("q_stack", [SLOTS * HD0, HEADS, GT], BF16, own)
            k_stack = sb("k_stack", [SLOTS * HD0, HEADS, GT], BF16, own)
            val = sb("val", [P, GROUP, HEADS, HD0 + 1], F32, own)
            mixed = sb("mixed", [P, 2, FC, GT], F32, own)
            for n, k in (("xv_ready", 1), ("xl_ready", 1), ("proj_ready", 2), ("rot_part", 4), ("rot_ready", 4),
                         ("v_ready", GROUP), ("v_out_a", GROUP // 2), ("v_out_d", GROUP // 2), ("back_out", 2 * GROUP),
                         ("out_ready", 1), ("x_done", FC)):
                s[n].block(k)
            s["stacked"].block(4 * SLOTS, amount=16)
            s["setup_p"].block(1, 1)
            split.src_there = lambda eng, g, i: eng.wait_ge(s["rot_ready"].sem, s["rot_ready"].upto(g, 2 * i + 2))

            def causal_bias(eng, g, to, b):
                eng.matmul(to, ident_b[:], causal[:].unsqueeze(1).to_broadcast([P, QUAD, SEQ]), start=True, stop=False,
                           skip_group_check=True)

            def post(eng, g, j):
                src = g_pair[:, j % 2, 0:FC * P].rearrange("p (c n) -> p c n", c=FC)
                for e in range(2):
                    mask = expert[:, e, bass.ds(g * GT + j * SEQ, SEQ)].unsqueeze(1).to_broadcast([P, FC, SEQ])
                    eng.tensor_tensor(mixed[:, e, :, j * SEQ:(j + 1) * SEQ], src, mask, ALU.mult)\
                       .then_inc(s["back_out"].sem, 1)

            att = Attention(own, HD0,
                            lambda b, h: (q_stack[:, h, b * SEQ:(b + 1) * SEQ], k_stack[:, h, b * SEQ:(b + 1) * SEQ]),
                            causal_bias, lambda b, h: val[:, b, h, :], FC, HEADS // QUAD, post)

            with nc.Block() as block:
                @block.sync
                def _(eng):
                    def body(g, first):
                        for i, stack in enumerate((q_stack, k_stack)):
                            split.wait_parts(eng, g, i)
                            for half in range(2):
                                stack_rows(eng, stack, split.parts[i][:, :, half, :], i, half * SLOTS * HALF, HALF)
                    over_groups(eng, body)

                @block.gpsimd
                def _(eng):
                    eng.memset(val[:], 1.0).then_inc(s["setup_p"].sem, 1)

                    def body(g, first):
                        norm.there(eng, g)
                        group_start(eng, g, first)
                        mask = tok(expert[:, 1, :], g).unsqueeze(1).to_broadcast([P, FC, GT])
                        eng.tensor_tensor(xe[:, 1], norm.xn[:], mask, ALU.mult).then_inc(s["xl_ready"].sem, 1)
                    over_groups(eng, body)

                @block.scalar
                def _(eng):
                    eng.wait_ge(s["setup_p"].sem, s["setup_p"].upto(0, 1))

                    def body(g, first):
                        group_start(eng, g, first)
                        norm.scalar(eng, g)
                        split.scalar(eng, g)
                        for b in range(1, GROUP, 2):
                            eng.wait_ge(s["v_ready"].sem, s["v_ready"].upto(g, b + 1))
                            eng.activation(val[:, b, :, 0:HD0], bank[4 + b][:, 0:DIM].rearrange("p (h d) -> p h d", h=HEADS),
                                           ACT.Copy).then_inc(s["v_out_a"].sem, 1)
                        att.scalar(eng, g)
                    over_groups(eng, body)

                @block.vector
                def _(eng):
                    eng.wait_ge(s["setup_p"].sem, s["setup_p"].upto(0, 1))

                    def body(g, first):
                        group_start(eng, g, first)
                        norm.vector(eng, g)
                        norm.there(eng, g)
                        mask = tok(expert[:, 0, :], g).unsqueeze(1).to_broadcast([P, FC, GT])
                        eng.tensor_tensor(xe[:, 0], norm.xn[:], mask, ALU.mult).then_inc(s["xv_ready"].sem, 1)
                        for i, src in enumerate((s_pair, t_pair)):
                            eng.wait_ge(s["proj_ready"].sem, s["proj_ready"].upto(g, i + 1))
                            if i:
                                eng.wait_ge(s["rot_ready"].sem, s["rot_ready"].upto(g, 2))
                            halves = src[:].rearrange("p a (b n) -> p (a b) n", n=SEQ)
                            for k, to in enumerate((rot_c, rot_s)):
                                eng.tensor_tensor(to[:].rearrange("p a (b n) -> p (a b) n", n=SEQ), halves,
                                                  rope[:, i, k, :].unsqueeze(1).to_broadcast([P, 2 * GROUP, SEQ]),
                                                  ALU.mult).then_inc(s["rot_part"].sem, 1)
                            eng.wait_ge(s["rot_part"].sem, s["rot_part"].upto(g, 2 * i + 2))
                            eng.tensor_tensor(rot[i][:, 0], rot_c[:, 0], rot_s[:, 1], ALU.subtract)\
                               .then_inc(s["rot_ready"].sem, 1)
                            eng.tensor_tensor(rot[i][:, 1], rot_c[:, 1], rot_s[:, 0], ALU.add)\
                               .then_inc(s["rot_ready"].sem, 1)
                            eng.wait_ge(s["rot_ready"].sem, s["rot_ready"].upto(g, 2 * i + 2))
                            split.vector(eng, g, i)
                        for b in range(0, GROUP, 2):
                            eng.wait_ge(s["v_ready"].sem, s["v_ready"].upto(g, b + 1))
                            eng.tensor_copy(val[:, b, :, 0:HD0], bank[4 + b][:, 0:DIM].rearrange("p (h d) -> p h d", h=HEADS))\
                               .then_inc(s["v_out_d"].sem, 1)
                        att.vector(eng, g)
                        residual(eng, g, (bank[0], bank[1]), s["out_ready"], 1)
                    over_groups(eng, body)

                @block.tensor
                def _(eng):
                    weights_there(eng, 0)

                    def body(g, first):
                        group_start(eng, g, first)
                        norm.tensor(eng, g)
                        eng.wait_ge(s["xv_ready"].sem, s["xv_ready"].upto(g, 1))
                        eng.wait_ge(s["xl_ready"].sem, s["xl_ready"].upto(g, 1))
                        for i, to in enumerate((s_pair, t_pair)):
                            for half in range(2):
                                col = (2 * i + half) * P
                                mm = product(eng, to[:, half, :], [(w_qk[:, e, c, col:col + P], xe[:, e, c, :])
                                                                   for e in range(2) for c in range(FC)])
                            mm.then_inc(s["proj_ready"].sem, 1)
                        eng.wait_ge(s["dev_ready"].sem, s["dev_ready"].upto(g, 1))
                        for b in range(GROUP):
                            product(eng, bank[4 + b][:, 0:DIM], [(xe[:, e, c, b * SEQ:(b + 1) * SEQ], w_v[:, e, c, :])
                                                                 for e in range(2) for c in range(FC)])\
                                .then_inc(s["v_ready"].sem, 1)
                        eng.wait_ge(s["stacked"].sem, s["stacked"].upto(g, 4 * SLOTS))
                        eng.wait_ge(s["v_out_a"].sem, s["v_out_a"].upto(g, GROUP // 2))
                        eng.wait_ge(s["v_out_d"].sem, s["v_out_d"].upto(g, GROUP // 2))
                        att.tensor(eng, g)
                        eng.wait_ge(s["back_out"].sem, s["back_out"].upto(g, 2 * GROUP))
                        for m in range(FC):
                            mm = product(eng, bank[m], [(w_dense[:, e, c, m * P:(m + 1) * P], mixed[:, e, c, :])
                                                        for e in range(2) for c in range(FC)])
                        mm.then_inc(s["out_ready"].sem, 1)
                    over_groups(eng, body)

    def cross_attention():
        with ExitStack() as own:
            norm = Norm(own, W_LN_CROSS)
            context = sb("context_c", [P, GT], F32, own)
            qk = sb("qk", [P, 2, GT], F32, own)
            split = Split(own, [qk])
            stack = sb("stack", [SLOTS * HD0C, 2, HEADS, GT], BF16, own)
            val = sb("val_c", [P, GROUP, HEADS, HD0C + 1], F32, own)
            gathered = sb("gathered", [P, GT], F32, own)
            for n, k in (("proj_ready", 2), ("rot_ready", 2), ("v_ready", GROUP), ("v_out_a", GROUP // 2),
                         ("v_out_d", GROUP // 2), ("back_out", GROUP), ("out_ready", 1), ("x_done", FC)):
                s[n].block(k)
            s["stacked"].block(2 * SLOTS, amount=16)
            s["ctx_loaded"].block(1, amount=16)
            s["setup_p"].block(1, 1)
            split.src_there = lambda eng, g, i: eng.wait_ge(s["rot_ready"].sem, s["rot_ready"].upto(g, 2))

            def post(eng, g, j):
                eng.tensor_copy(gathered[:, j * SEQ:(j + 1) * SEQ], g_pair[:, j % 2, 0:SEQ])\
                   .then_inc(s["back_out"].sem, 1)

            att = Attention(own, HD0C,
                            lambda b, h: (stack[:, 0, h, b * SEQ:(b + 1) * SEQ], stack[:, 1, h, b * SEQ:(b + 1) * SEQ]),
                            no_bias, lambda b, h: val[:, b, h, :], 1, HEADS // QUAD, post)

            with nc.Block() as block:
                @block.sync
                def _(eng):
                    load_weights(eng, 2)

                    def body(g, first):
                        group_start(eng, g, first)
                        eng.dma_start(context[:], tok(a["ctx"], g)).then_inc(s["ctx_loaded"].sem, 16)
                        split.wait_parts(eng, g, 0)
                        for i in range(2):
                            stack_rows(eng, stack[:, i], split.parts[0][:, :, i, :], i, 0, HD0C)
                    over_groups(eng, body)

                @block.gpsimd
                def _(eng):
                    eng.memset(val[:], 1.0).then_inc(s["setup_p"].sem, 1)

                @block.scalar
                def _(eng):
                    eng.wait_ge(s["setup_p"].sem, s["setup_p"].upto(0, 1))

                    def body(g, first):
                        group_start(eng, g, first)
                        norm.scalar(eng, g)
                        eng.wait_ge(s["proj_ready"].sem, s["proj_ready"].upto(g, 1))
                        eng.activation(qk[:, 0], bank[0], ACT.Copy, scale=HD0C ** -0.5).then_inc(s["rot_ready"].sem, 1)
                        eng.wait_ge(s["proj_ready"].sem, s["proj_ready"].upto(g, 2))
                        eng.activation(qk[:, 1], bank[1], ACT.Copy).then_inc(s["rot_ready"].sem, 1)
                        split.scalar(eng, g)
                        for b in range(1, GROUP, 2):
                            eng.wait_ge(s["v_ready"].sem, s["v_ready"].upto(g, b + 1))
                            eng.activation(val[:, b, :, 0:HD0C], bank[2 + b][:, 0:P].rearrange("p (h d) -> p h d", h=HEADS),
                                           ACT.Copy).then_inc(s["v_out_a"].sem, 1)
                        att.scalar(eng, g)
                    over_groups(eng, body)

                @block.vector
                def _(eng):
                    eng.wait_ge(s["setup_p"].sem, s["setup_p"].upto(0, 1))

                    def body(g, first):
                        group_start(eng, g, first)
                        norm.vector(eng, g)
                        for b in range(0, GROUP, 2):
                            eng.wait_ge(s["v_ready"].sem, s["v_ready"].upto(g, b + 1))
                            eng.tensor_copy(val[:, b, :, 0:HD0C], bank[2 + b][:, 0:P].rearrange("p (h d) -> p h d", h=HEADS))\
                               .then_inc(s["v_out_d"].sem, 1)
                        split.vector(eng, g, 0)
                        att.vector(eng, g)
                        residual(eng, g, (bank[0], bank[1]), s["out_ready"], 1)
                    over_groups(eng, body)

                @block.tensor
                def _(eng):
                    weights_there(eng, 1)

                    def body(g, first):
                        group_start(eng, g, first)
                        norm.tensor(eng, g)
                        norm.there(eng, g)
                        product(eng, bank[0], [(w_cq[:, c, :], norm.xn[:, c, :]) for c in range(FC)])\
                            .then_inc(s["proj_ready"].sem, 1)
                        eng.wait_ge(s["ctx_loaded"].sem, s["ctx_loaded"].upto(g, 1))
                        product(eng, bank[1], [(w_ck, context[:])]).then_inc(s["proj_ready"].sem, 1)
                        for b in range(GROUP):
                            product(eng, bank[2 + b][:, 0:P], [(context[:, b * SEQ:(b + 1) * SEQ], w_cv)])\
                                .then_inc(s["v_ready"].sem, 1)
                        eng.wait_ge(s["stacked"].sem, s["stacked"].upto(g, 2 * SLOTS))
                        eng.wait_ge(s["v_out_a"].sem, s["v_out_a"].upto(g, GROUP // 2))
                        eng.wait_ge(s["v_out_d"].sem, s["v_out_d"].upto(g, GROUP // 2))
                        att.tensor(eng, g)
                        eng.wait_ge(s["back_out"].sem, s["back_out"].upto(g, GROUP))
                        for m in range(FC):
                            mm = product(eng, bank[m], [(w_cdense[:, m * P:(m + 1) * P], gathered[:])])
                        mm.then_inc(s["out_ready"].sem, 1)
                    over_groups(eng, body)

    def expert_mlp():
        with ExitStack() as own:
            norm = Norm(own, W_LN_MLP)
            xe = sb("xe_m", [P, 2, FC, GT], F32, own)
            act = sb("act_m", [P, 2, GT], F32, own)
            hid = sb("hid_m", [P, 3, GT], F32, own)
            for n, k in (("xv_ready", 1), ("xl_ready", 1), ("proj_ready", HTILES), ("act_ready", HTILES),
                         ("hid_ready", HTILES + 1), ("hid_free", HTILES), ("x_done", FC)):
                s[n].block(k)

            with nc.Block() as block:
                @block.sync
                def _(eng):
                    load_weights(eng, 3)

                @block.gpsimd
                def _(eng):
                    def body(g, first):
                        norm.there(eng, g)
                        group_start(eng, g, first)
                        mask = tok(expert[:, 1, :], g).unsqueeze(1).to_broadcast([P, FC, GT])
                        eng.tensor_tensor(xe[:, 1], norm.xn[:], mask, ALU.mult).then_inc(s["xl_ready"].sem, 1)
                    over_groups(eng, body)

                @block.scalar
                def _(eng):
                    def body(g, first):
                        group_start(eng, g, first)
                        norm.scalar(eng, g)
                        for t in range(HTILES):
                            eng.wait_ge(s["proj_ready"].sem, s["proj_ready"].upto(g, t + 1))
                            if t >= 2:
                                eng.wait_ge(s["hid_ready"].sem, s["hid_ready"].upto(g, t - 1))
                            eng.activation(act[:, t % 2], pair[t % 2][:, 0, :], ACT.Silu).then_inc(s["act_ready"].sem, 1)
                    over_groups(eng, body)

                @block.vector
                def _(eng):
                    def body(g, first):
                        group_start(eng, g, first)
                        norm.vector(eng, g)
                        norm.there(eng, g)
                        mask = tok(expert[:, 0, :], g).unsqueeze(1).to_broadcast([P, FC, GT])
                        eng.tensor_tensor(xe[:, 0], norm.xn[:], mask, ALU.mult).then_inc(s["xv_ready"].sem, 1)
                        for t in range(HTILES):
                            eng.wait_ge(s["act_ready"].sem, s["act_ready"].upto(g, t + 1))
                            if t >= 3:
                                eng.wait_ge(s["hid_free"].sem, s["hid_free"].upto(g, t - 2))
                            eng.tensor_tensor(hid[:, t % 3], act[:, t % 2], pair[t % 2][:, 1, :], ALU.mult)\
                               .then_inc(s["hid_ready"].sem, 1)
                        last = hid[:, (HTILES - 1) % 3]
                        eng.wait_ge(s["hid_ready"].sem, s["hid_ready"].upto(g, HTILES))
                        eng.tensor_tensor(last, last, tok(rest_mask[:], g), ALU.mult).then_inc(s["hid_ready"].sem, 1)
                        residual(eng, g, (bank[4], bank[5]), s["hid_free"], HTILES)
                    over_groups(eng, body)

                @block.tensor
                def _(eng):
                    weights_there(eng, 2)

                    def body(g, first):
                        group_start(eng, g, first)
                        norm.tensor(eng, g)
                        eng.wait_ge(s["xv_ready"].sem, s["xv_ready"].upto(g, 1))
                        eng.wait_ge(s["xl_ready"].sem, s["xl_ready"].upto(g, 1))
                        for t in range(HTILES + 1):
                            if t < HTILES:
                                if t >= 2:
                                    eng.wait_ge(s["hid_ready"].sem, s["hid_ready"].upto(g, t - 1))
                                for w, to in ((w_gate, 0), (w_up, 1)):
                                    mm = product(eng, pair[t % 2][:, to, :],
                                                 [(w[:, c, t * P:(t + 1) * P],
                                                   norm.xn[:, c, :] if t == HTILES - 1 else xe[:, t // MT, c, :])
                                                  for c in range(FC)])
                                mm.then_inc(s["proj_ready"].sem, 1)
                            if t >= 1:
                                k = t - 1
                                eng.wait_ge(s["hid_ready"].sem, s["hid_ready"].upto(g, HTILES + 1 if t == HTILES else t))
                                for m in range(FC):
                                    mm = eng.matmul(bank[4 + m], w_down[:, k, m * P:(m + 1) * P], hid[:, k % 3],
                                                    start=k == 0, stop=k == HTILES - 1)
                                mm.then_inc(s["hid_free"].sem, 1)
                    over_groups(eng, body)

    def media_attention():
        TILES = HEADS * HD1 // P
        VHALF = HEADS // 2
        with ExitStack() as own:
            norm = Norm(own, LNQ_G, LNQ_B)
            context = sb("context_m", [P, GT], F32, own)
            bias_row = sb("bias_row", [1, GT], BF16, own)
            q = sb("q_m", [P, TILES, GT], F32, own)
            k = sb("k_m", [P, TILES, GT], F32, own)
            val = sb("val_m", [P, GROUP, HEADS, HD1 + 1], F32, own)
            jobs = [("q", t) for t in range(TILES)] + [("k", t) for t in range(TILES)] + \
                   [("v", n) for n in range(2 * GROUP)]
            for n, c in (("proj_ready", len(jobs)), ("proj_out_d", len(jobs) // 2), ("proj_out_a", len(jobs) // 2),
                         ("back_out", QUADS), ("out_ready", 1), ("x_done", FC)):
                s[n].block(c)
            s["ctx_loaded"].block(1, amount=16)
            s["setup_p"].block(1, 1)
            s["xl_ready"].block(1)

            def key_mask(eng, g, to, b):
                row = bias_row[0:1, b * SEQ:(b + 1) * SEQ].unsqueeze(1).to_broadcast([1, QUAD, SEQ])
                eng.matmul(to, ones_row[:], row, start=True, stop=False, skip_group_check=True)

            def score(b, h):
                rows = slice(HD1 * (h % 2), HD1 * (h % 2) + HD1)
                return q[rows, h // 2, b * SEQ:(b + 1) * SEQ], k[rows, h // 2, b * SEQ:(b + 1) * SEQ]

            def post(eng, g, j):
                b, part = divmod(j, HEADS // QUAD)
                eng.tensor_copy(q[:, 2 * part:2 * part + 2, b * SEQ:(b + 1) * SEQ],
                                g_pair[:, j % 2, 0:2 * P].rearrange("p (c n) -> p c n", c=2))\
                   .then_inc(s["back_out"].sem, 1)

            att = Attention(own, HD1, score, key_mask, lambda b, h: val[:, b, h, :], 2, 1, post,
                            head=media_head)

            def take(eng, g, n, scalar):
                kind, t = jobs[n]
                eng.wait_ge(s["proj_ready"].sem, s["proj_ready"].upto(g, n + 1))
                src = bank[n % 8]
                if kind == "v":
                    b, half = divmod(t, 2)
                    to = val[:, b, VHALF * half:VHALF * (half + 1), 0:HD1]
                    src = src.rearrange("p (h d) -> p h d", h=VHALF)
                else:
                    to = (q if kind == "q" else k)[:, t, :]
                scale = HD1 ** -0.5 if kind == "q" else 1.0
                if scalar:
                    eng.activation(to, src, ACT.Copy, scale=scale).then_inc(s["proj_out_a"].sem, 1)
                else:
                    eng.tensor_scalar(to, src, scale, None, ALU.mult).then_inc(s["proj_out_d"].sem, 1)

            with nc.Block() as block:
                @block.sync
                def _(eng):
                    load_weights(eng, 4)

                    def body(g, first):
                        group_start(eng, g, first)
                        eng.dma_start(context[:], tok(a["ctx"], g)).then_inc(s["ctx_loaded"].sem, 16)
                    over_groups(eng, body)

                @block.gpsimd
                def _(eng):
                    eng.memset(val[:], 1.0).then_inc(s["setup_p"].sem, 1)

                    def body(g, first):
                        group_start(eng, g, first)
                        eng.tensor_copy(bias_row[:], tok(key_bias[:], g)).then_inc(s["xl_ready"].sem, 1)
                    over_groups(eng, body)

                @block.scalar
                def _(eng):
                    eng.wait_ge(s["setup_p"].sem, s["setup_p"].upto(0, 1))

                    def body(g, first):
                        group_start(eng, g, first)
                        norm.scalar(eng, g)
                        for n in range(1, len(jobs), 2):
                            take(eng, g, n, True)
                        att.scalar(eng, g)
                    over_groups(eng, body)

                @block.vector
                def _(eng):
                    eng.wait_ge(s["setup_p"].sem, s["setup_p"].upto(0, 1))

                    def body(g, first):
                        group_start(eng, g, first)
                        norm.vector(eng, g)
                        for n in range(0, len(jobs), 2):
                            take(eng, g, n, False)
                        att.vector(eng, g)
                        eng.wait_ge(s["out_ready"].sem, s["out_ready"].upto(g, 1))
                        for m in range(FC):
                            xs = x_t[:, m, bass.ds(g * GT, GT)]
                            eng.scalar_tensor_tensor(out=xs, in0=bank[m], scalar=gates[:, 0:1], in1=xs, op0=ALU.mult,
                                                     op1=ALU.add).then_inc(s["x_done"].sem, 1)
                    over_groups(eng, body)

                @block.tensor
                def _(eng):
                    weights_there(eng, 3)

                    def body(g, first):
                        group_start(eng, g, first)
                        norm.tensor(eng, g)
                        norm.there(eng, g)
                        eng.wait_ge(s["ctx_loaded"].sem, s["ctx_loaded"].upto(g, 1))
                        for n, (kind, t) in enumerate(jobs):
                            if n >= 8:
                                out_of = s["proj_out_a"] if n % 2 else s["proj_out_d"]
                                eng.wait_ge(out_of.sem, out_of.upto(g, (n - 8) // 2 + 1))
                            if kind == "q":
                                f = [(w_q1[:, c, t * P:(t + 1) * P], norm.xn[:, c, :]) for c in range(FC)]
                            elif kind == "k":
                                f = [(w_k1[:, t * P:(t + 1) * P], context[:])]
                            else:
                                b, half = divmod(t, 2)
                                f = [(context[:, b * SEQ:(b + 1) * SEQ], w_v1[:, half * GT:(half + 1) * GT])]
                            product(eng, bank[n % 8], f).then_inc(s["proj_ready"].sem, 1)
                        for out_of in (s["proj_out_a"], s["proj_out_d"]):
                            eng.wait_ge(out_of.sem, out_of.upto(g, len(jobs) // 2))
                        eng.wait_ge(s["xl_ready"].sem, s["xl_ready"].upto(g, 1))
                        att.tensor(eng, g)
                        eng.wait_ge(s["back_out"].sem, s["back_out"].upto(g, QUADS))
                        for m in range(FC):
                            mm = product(eng, bank[m], [(w_o1[:, t, m * P:(m + 1) * P], q[:, t, :]) for t in range(TILES)])
                        mm.then_inc(s["out_ready"].sem, 1)
                    over_groups(eng, body)

    def feed_forward():
        TILES = MLP1 // P
        with ExitStack() as own:
            norm = Norm(own, LNF_G, LNF_B)
            hid = sb("hid_f", [P, 3, GT], F32, own)
            for n, k in (("proj_ready", TILES), ("hid_ready", TILES), ("hid_free", TILES), ("x_done", FC)):
                s[n].block(k)

            with nc.Block() as block:
                @block.sync
                def _(eng):
                    load_weights(eng, 5)

                @block.scalar
                def _(eng):
                    def body(g, first):
                        group_start(eng, g, first)
                        norm.scalar(eng, g)
                        for t in range(TILES):
                            eng.wait_ge(s["proj_ready"].sem, s["proj_ready"].upto(g, t + 1))
                            if t >= 3:
                                eng.wait_ge(s["hid_free"].sem, s["hid_free"].upto(g, t - 2))
                            eng.activation(hid[:, t % 3], bank[t % 4], ACT.Gelu).then_inc(s["hid_ready"].sem, 1)
                    over_groups(eng, body)

                @block.vector
                def _(eng):
                    def body(g, first):
                        group_start(eng, g, first)
                        norm.vector(eng, g)
                        eng.wait_ge(s["hid_free"].sem, s["hid_free"].upto(g, TILES))
                        for m in range(FC):
                            xs = x_t[:, m, bass.ds(g * GT, GT)]
                            eng.scalar_tensor_tensor(out=xs, in0=bank[4 + m], scalar=gates[:, 1:2], in1=xs, op0=ALU.mult,
                                                     op1=ALU.add).then_inc(s["x_done"].sem, 1)
                    over_groups(eng, body)

                @block.tensor
                def _(eng):
                    weights_there(eng, 4)

                    def body(g, first):
                        group_start(eng, g, first)
                        norm.tensor(eng, g)
                        norm.there(eng, g)
                        for t in range(TILES + 2):
                            if t < TILES:
                                if t >= 4:
                                    eng.wait_ge(s["hid_ready"].sem, s["hid_ready"].upto(g, t - 3))
                                product(eng, bank[t % 4], [(w_ff1[:, c, t * P:(t + 1) * P], norm.xn[:, c, :])
                                                           for c in range(FC)]).then_inc(s["proj_ready"].sem, 1)
                            if t >= 2:
                                k = t - 2
                                eng.wait_ge(s["hid_ready"].sem, s["hid_ready"].upto(g, k + 1))
                                for m in range(FC):
                                    mm = eng.matmul(bank[4 + m], w_ff2[:, k, m * P:(m + 1) * P], hid[:, k % 3],
                                                    start=k == 0, stop=k == TILES - 1)
                                mm.then_inc(s["hid_free"].sem, 1)
                    over_groups(eng, body)

    def memory_fusion(layer):
        w_mem, w_g, b_g = fuse_w[layer]
        last = layer == 1
        with ExitStack() as own:
            context = sb("context_f", [P, GT], F32, own)
            xq = sb("xq", [P, FC, GT], F32, own)
            mem_t = sb("mem_t", [P, FC, GT], F32, own)
            mem = sb("mem", [P, GROUP, DIM], F32, own)
            p = sb("p_f", [P, GROUP, SEQ], F32, own)
            pn = sb("pn_f", [P, GROUP, SEQ], F32, own)
            pt = sb("pt_f", [P, GROUP, SEQ], F32, own)
            nmax = sb("nmax_f", [P, GROUP], F32, own)
            sums = sb("sums_f", [P, GROUP], F32, own)
            recip = sb("recip_f", [P, GROUP], F32, own)
            mix = sb("mix", [P, FC, GT], F32, own)
            gate = sb("gate_f", [P, FC, GT], F32, own)
            fused = sb("fused", [P, FC, GT], F32, own)
            half_b = sb("half_b", [P, FC], F32, own)
            norm = Norm(own, NORM2 + layer, src=fused)
            for n, k in (("memt_ready", FC), ("mem_out", FC + GROUP), ("v_ready", GROUP), ("scores_ready", 1),
                         ("max_ready", 1), ("p_ready", GROUP), ("recip_ready", 1), ("norm_ready", 1), ("turned_ready", 1),
                         ("pt_ready", 1), ("ctx_ready", FC), ("mix_ready", FC), ("proj_ready", FC), ("act_ready", FC),
                         ("res_ready", 3 * FC), ("x_done", FC), ("rot_ready", 1)):
                s[n].block(k)
            s["ctx_loaded"].block(1, amount=16)
            s["bias_half"].block(1, 1)

            with nc.Block() as block:
                @block.sync
                def _(eng):
                    if not last:
                        load_weights(eng, 6)

                    def body(g, first):
                        group_start(eng, g, first)
                        eng.dma_start(context[:], tok(a["ctx"], g)).then_inc(s["ctx_loaded"].sem, 16)
                    over_groups(eng, body)

                @block.gpsimd
                def _(eng):
                    if last:
                        for g in range(GROUPS):
                            eng.wait_ge(s["x_done"].sem, s["x_done"].upto(g, FC))
                            eng.dma_start(out[:, :, g * GT:(g + 1) * GT], x_t[:, :, g * GT:(g + 1) * GT])\
                               .then_inc(s["stores"].sem, 16)
                        eng.wait_ge(s["stores"].sem, 16 * GROUPS)

                @block.scalar
                def _(eng):
                    weights_there(eng, 5 + layer)
                    eng.activation(half_b[:], b_g, ACT.Copy, scale=0.5).then_inc(s["bias_half"].sem, 1)
                    eng.wait_ge(s["bias_half"].sem, s["bias_half"].upto(0, 1))

                    def body(g, first):
                        group_start(eng, g, first)
                        eng.activation(xq[:], tok(x_t[:], g), ACT.Copy, scale=DIM ** -0.5)\
                           .then_inc(s["rot_ready"].sem, 1)
                        for c in range(FC):
                            eng.wait_ge(s["memt_ready"].sem, s["memt_ready"].upto(g, c + 1))
                            eng.activation(mem_t[:, c, :], bank[c], ACT.Copy).then_inc(s["mem_out"].sem, 1)
                        for b in range(GROUP):
                            eng.wait_ge(s["v_ready"].sem, s["v_ready"].upto(g, b + 1))
                            eng.activation(mem[:, b, :], bank[2 + b][:, 0:DIM], ACT.Copy).then_inc(s["mem_out"].sem, 1)
                        eng.wait_ge(s["max_ready"].sem, s["max_ready"].upto(g, 1))
                        for b in range(GROUP):
                            eng.activation(p[:, b, :], bank[6][:, b * SEQ:(b + 1) * SEQ], ACT.Exp, bias=nmax[:, b:b + 1],
                                           accum_out=sums[:, b:b + 1]).then_inc(s["p_ready"].sem, 1)
                        for m in range(FC):
                            eng.wait_ge(s["proj_ready"].sem, s["proj_ready"].upto(g, m + 1))
                            eng.activation(gate[:, m, :], bank[4 + m], ACT.Tanh, bias=half_b[:, m:m + 1], scale=0.5)\
                               .then_inc(s["act_ready"].sem, 1)
                        eng.wait_ge(s["res_ready"].sem, s["res_ready"].upto(g, 3 * FC))
                        norm.scalar(eng, g)
                    over_groups(eng, body)

                @block.vector
                def _(eng):
                    def body(g, first):
                        group_start(eng, g, first)
                        eng.wait_ge(s["scores_ready"].sem, s["scores_ready"].upto(g, 1))
                        eng.tensor_reduce(nmax[:], bank[6].rearrange("p (b k) -> p b k", b=GROUP), AX_X, ALU.max,
                                          negate=True).then_inc(s["max_ready"].sem, 1)
                        eng.wait_ge(s["p_ready"].sem, s["p_ready"].upto(g, GROUP))
                        eng.reciprocal(recip[:], sums[:]).then_inc(s["recip_ready"].sem, 1)
                        eng.wait_ge(s["recip_ready"].sem, s["recip_ready"].upto(g, 1))
                        eng.tensor_tensor(pn[:], p[:], recip[:].unsqueeze(2).to_broadcast([P, GROUP, SEQ]), ALU.mult)\
                           .then_inc(s["norm_ready"].sem, 1)
                        eng.wait_ge(s["turned_ready"].sem, s["turned_ready"].upto(g, 1))
                        eng.tensor_copy(pt[:].rearrange("p b k -> p (b k)"), bank[7]).then_inc(s["pt_ready"].sem, 1)
                        for m in range(FC):
                            eng.wait_ge(s["ctx_ready"].sem, s["ctx_ready"].upto(g, m + 1))
                            eng.tensor_copy(mix[:, m, :], bank[m]).then_inc(s["mix_ready"].sem, 1)
                        r = s["res_ready"]
                        for m in range(FC):
                            eng.wait_ge(s["act_ready"].sem, s["act_ready"].upto(g, m + 1))
                            eng.tensor_scalar(gate[:, m, :], gate[:, m, :], 0.5, 0.5, ALU.mult, ALU.add).then_inc(r.sem, 1)
                            eng.wait_ge(r.sem, r.upto(g, 3 * m + 1))
                            eng.tensor_tensor(gate[:, m, :], gate[:, m, :], mix[:, m, :], ALU.mult).then_inc(r.sem, 1)
                            eng.wait_ge(r.sem, r.upto(g, 3 * m + 2))
                            eng.tensor_tensor(fused[:, m, :], gate[:, m, :], x_t[:, m, bass.ds(g * GT, GT)], ALU.add)\
                               .then_inc(r.sem, 1)
                        eng.wait_ge(s["dev_ready"].sem, s["dev_ready"].upto(g, 1))
                        eng.reciprocal(norm.rstd[:], norm.dev[:]).then_inc(s["rstd_ready"].sem, 1)
                        eng.wait_ge(s["rstd_ready"].sem, s["rstd_ready"].upto(g, 1))
                        for m in range(FC):
                            eng.scalar_tensor_tensor(out=x_t[:, m, bass.ds(g * GT, GT)], in0=fused[:, m, :],
                                                     scalar=scales[:, norm.scale, m:m + 1], in1=norm.rstd[:], op0=ALU.mult,
                                                     op1=ALU.mult).then_inc(s["x_done"].sem, 1)
                    over_groups(eng, body)

                @block.tensor
                def _(eng):
                    weights_there(eng, 5 + layer)

                    def body(g, first):
                        group_start(eng, g, first)
                        eng.wait_ge(s["ctx_loaded"].sem, s["ctx_loaded"].upto(g, 1))
                        for c in range(FC):
                            product(eng, bank[c], [(w_mem[:, c * P:(c + 1) * P], context[:])])\
                                .then_inc(s["memt_ready"].sem, 1)
                        for b in range(GROUP):
                            product(eng, bank[2 + b][:, 0:DIM], [(context[:, b * SEQ:(b + 1) * SEQ], w_mem)])\
                                .then_inc(s["v_ready"].sem, 1)
                        eng.wait_ge(s["mem_out"].sem, s["mem_out"].upto(g, FC))
                        eng.wait_ge(s["rot_ready"].sem, s["rot_ready"].upto(g, 1))
                        for b in range(GROUP):
                            cols = slice(b * SEQ, (b + 1) * SEQ)
                            mm = product(eng, bank[6][:, cols], [(xq[:, c, cols], mem_t[:, c, cols]) for c in range(FC)])
                        mm.then_inc(s["scores_ready"].sem, 1)
                        eng.wait_ge(s["norm_ready"].sem, s["norm_ready"].upto(g, 1))
                        for b in range(GROUP):
                            mm = eng.transpose(bank[7][:, b * SEQ:(b + 1) * SEQ], pn[:, b, :], ident[:])
                        mm.then_inc(s["turned_ready"].sem, 1)
                        eng.wait_ge(s["pt_ready"].sem, s["pt_ready"].upto(g, 1))
                        eng.wait_ge(s["mem_out"].sem, s["mem_out"].upto(g, FC + GROUP))
                        for m in range(FC):
                            for b in range(GROUP):
                                mm = eng.matmul(bank[m][:, b * SEQ:(b + 1) * SEQ], mem[:, b, m * P:(m + 1) * P],
                                                pt[:, b, :], start=True, stop=True)
                            mm.then_inc(s["ctx_ready"].sem, 1)
                        eng.wait_ge(s["mix_ready"].sem, s["mix_ready"].upto(g, FC))
                        for m in range(FC):
                            product(eng, bank[4 + m],
                                    [(w_g[:, c, m * P:(m + 1) * P], x_t[:, c, bass.ds(g * GT, GT)]) for c in range(FC)] +
                                    [(w_g[:, FC + c, m * P:(m + 1) * P], mix[:, c, :]) for c in range(FC)])\
                                .then_inc(s["proj_ready"].sem, 1)
                        norm.tensor(eng, g)
                    over_groups(eng, body)


    self_attention()

    cross_attention()
    expert_mlp()
    media_attention()
    feed_forward()
    memory_fusion(0)
    memory_fusion(1)


def _laid_out(i):
    f = np.float32

    def chunks(w):
        return np.ascontiguousarray(w)

    def by_dim(w, hd):
        return w.reshape(w.shape[0], HEADS, hd).transpose(0, 2, 1).reshape(w.shape[0], HEADS * hd)

    def by_feature(v):
        return v.reshape(FC, P).T

    def hidden_columns(v, l):
        rest = np.zeros((v.shape[0], P), v.dtype)
        rest[:, 0:MREST] = v[:, MT * P:]
        rest[:, REST_AT:REST_AT + MREST] = l[:, MT * P:]
        return np.concatenate([v[:, :MT * P], l[:, :MT * P], rest], axis=1)

    o = {}
    o["x"] = i["x"].reshape(TOKENS, FC, P).transpose(2, 1, 0)
    o["ctx"] = i["ctx_1024"].reshape(TOKENS, CTX).T
    o["tt"] = i["mask_BxS_ik0"].reshape(TOKENS)
    o["keys"] = i["mask_BxS2_bk0"].reshape(1, TOKENS).view(np.int32)
    o["pos"] = i["pos_1xS"].reshape(SEQ)
    for e in "vl":
        qkv = i[f"L0_xattn_{e}_qkv"]
        o[f"{e}_qk"] = np.concatenate([by_dim(qkv[:, :DIM], HD0), by_dim(qkv[:, DIM:2 * DIM], HD0)], axis=1)
        o[f"{e}_v"] = qkv[:, 2 * DIM:]
        o[f"{e}_dense"] = i[f"L0_xattn_{e}_dense"]
    o["cq"] = by_dim(i["L0_xattn_cq_w"], HD0C)
    o["ck"] = by_dim(i["L0_xattn_ckv_w"][:, :P], HD0C)
    o["cv"] = i["L0_xattn_ckv_w"][:, P:]
    o["cdense"] = i["L0_xattn_cdense_w"]
    o["gate0"] = hidden_columns(i["L0_xattn_v_gate"], i["L0_xattn_l_gate"])
    o["up0"] = hidden_columns(i["L0_xattn_v_up"], i["L0_xattn_l_up"])
    o["down0"] = hidden_columns(i["L0_xattn_v_down"].T, i["L0_xattn_l_down"].T).T
    order = [media_head(q, h) for q in range(HEADS // QUAD) for h in range(QUAD)]
    o["wq"] = i["L1_xattn_Wq"]
    o["wo"] = i["L1_xattn_Wo"].reshape(HEADS, HD1, DIM)[order].reshape(HEADS * HD1, DIM)
    o["wk"], o["wv"] = i["L1_xattn_Wkv"][:, :HEADS * HD1], i["L1_xattn_Wkv"][:, HEADS * HD1:]
    o["w1"], o["w2"] = i["L1_xattn_W1"], i["L1_xattn_W2"]
    for n in "23":
        o[f"mem{n}"] = i[f"L{n}_xattn_W_mem"].T
        o[f"g{n}"] = i[f"L{n}_xattn_W_gate"].T
        o[f"b{n}"] = by_feature(i[f"L{n}_xattn_b_gate"])
    o["scales"] = np.stack([by_feature(i[n]) for n in (
        "L0_xattn_ln_in_w", "L0_xattn_ln_post_cross_w", "L0_xattn_ln_post_attn_w", "L1_xattn_ln_q_g", "L1_xattn_ln_q_b",
        "L1_xattn_ln_ff_g", "L1_xattn_ln_ff_b", "L2_xattn_norm_w", "L3_xattn_norm_w")], axis=1)
    o["gates"] = np.concatenate([i["L1_xattn_attn_gate"], i["L1_xattn_ff_gate"]])

    inv = (1.0 / ROPE_BASE ** (np.arange(0, HD0, 2, dtype=f) / f(HD0))).astype(f)
    angle = np.outer(np.arange(SEQ, dtype=f), inv).astype(f)
    o["consts"] = np.concatenate([np.repeat(np.cos(angle), HEADS, axis=1), np.repeat(np.sin(angle), HEADS, axis=1),
                                  np.arange(P, dtype=f)[:, None]], axis=1).astype(f)
    o["ident"] = np.eye(P, dtype=f)
    above = np.arange(P)[None, :] > np.arange(P)[:, None]
    o["causal"] = np.where(above, MASKED, 0.0).astype(mybir.dt.np(BF16))
    return {n: np.ascontiguousarray(v) for n, v in o.items()}


def kernel(**inputs):
    import concourse.bacc as bacc
    from concourse.bass_utils import run_bass_kernel_spmd

    arrays = _laid_out({n: np.asarray(v) for n, v in inputs.items()})
    nc = bacc.Bacc("TRN2", target_bir_lowering=False, num_devices=1)
    aps = {n: nc.dram_tensor(f"in_{n}", v.shape, mybir.dt.from_np(v.dtype), kind="ExternalInput").ap()
           for n, v in arrays.items()}
    out = nc.dram_tensor("out_x", (P, FC, TOKENS), F32, kind="ExternalOutput").ap()
    build(nc, aps, out)
    got = run_bass_kernel_spmd(nc, [{f"in_{n}": v for n, v in arrays.items()}], core_ids=[0]).results[0]["out_x"]
    return got.transpose(2, 1, 0).reshape(BATCHES, SEQ, DIM)
```

```python
from contextlib import ExitStack

import numpy as np

import concourse.bass as bass
from concourse import mybir

P = 128
BATCHES, SEQ, DIM, CTX = 16, 128, 256, 128
TOKENS = BATCHES * SEQ
GROUP = 4
GROUPS = BATCHES // GROUP
GT = GROUP * SEQ
FC = DIM // P
HEADS = 16
QUAD = 4
QUADS = GROUP * HEADS // QUAD
HD0, HD0C, HD1 = 16, 8, 64
MLP0, MLP1 = 688, 1024
MT = MLP0 // P
MREST = MLP0 - MT * P
HTILES = 2 * MT + 1
REST_AT = 64
HALF = HD0 // 2
SLOTS = 6
SLOT_PARTS = ((0, 0), (0, 1), (0, 2), (1, 0), (1, 1), (2, 0))
ROPE_BASE = 10000.0
EPS_RMS, EPS_LN = 1e-6, 1e-5
MASKED = -3.38e38

F32, BF16, I32, U8 = mybir.dt.float32, mybir.dt.bfloat16, mybir.dt.int32, mybir.dt.uint8
ALU = mybir.AluOpType
ACT = mybir.ActivationFunctionType
AX_X = mybir.AxisListType.X


def media_head(q, i):
    return 2 * QUAD * (q // 2) + q % 2 + 2 * i


class Signal:

    def __init__(self, sem):
        self.sem, self.start, self.total, self.per_group = sem, 0, 0, 0

    def block(self, per_group, groups=GROUPS, amount=1):
        self.start += self.total
        self.per_group, self.amount = per_group * amount, amount
        self.total = self.per_group * groups

    def upto(self, g, n):
        return g * self.per_group + (self.start + n * self.amount)


def over_groups(eng, body):
    body(0, True)
    with eng.Fori(1, GROUPS) as g:
        body(g, False)


def ahead_over_groups(eng, start, body):
    start()
    with eng.Fori(0, GROUPS - 1) as g:
        body(g, True)
    body(GROUPS - 1, False)


def build(nc, a, out):
    with ExitStack() as ctx:
        persistent(nc, ctx, a, out)


def persistent(nc, ctx, a, out):
    count = [0]

    def sb(name, shape, dt=F32, on=ctx):
        count[0] += 1
        return on.enter_context(nc.sbuf_tensor(f"{name}_{count[0]}", shape, dt))

    def signal(name):
        return Signal(ctx.enter_context(nc.semaphore(name)))

    x_t = sb("x_t", [P, FC, TOKENS])
    expert = sb("expert", [P, 2, TOKENS], BF16)
    rest_mask = sb("rest_mask", [P, TOKENS], BF16)
    key_bias = sb("key_bias", [1, TOKENS], BF16)
    ident = sb("ident", [P, P])
    ident_b = sb("ident_b", [P, P], BF16)
    causal = sb("causal", [P, P], BF16)
    ones_row = sb("ones_row", [1, P], BF16)
    mean_w = sb("mean_w", [P, P])
    rope = sb("rope", [P, 2, 2, SEQ])
    scales = sb("scales", [P, 9, FC])
    eps_cols = sb("eps_cols", [P, 2])
    gates = sb("gates", [P, 2])
    weights_a = sb("weights_a", [P, 8704])
    weights_b = sb("weights_b", [P, 6144])
    pair = [ctx.enter_context(nc.psum_tensor(f"pair{i}", [P, 2, GT], F32)) for i in range(4)]
    bank = [pair[i // 2][:, i % 2, :] for i in range(8)]
    s_pair, t_pair, c_pair, g_pair = pair

    (W_LN_IN, W_LN_CROSS, W_LN_MLP, LNQ_G, LNQ_B, LNF_G, LNF_B, NORM2, NORM3) = range(9)

    names = """loaded stores setup_d setup_a setup_p
        sq_ready mean_ready centre_ready dev_ready rstd_ready xn_ready xv_ready xl_ready
        proj_ready proj_out_d proj_out_a rot_part rot_ready hi_ready res_ready mid_ready lo_ready
        stacked v_ready v_out_a v_out_d ctx_loaded
        scores_ready max_ready p_ready turned_ready pt_ready ctx_ready recip_ready norm_ready
        back_ready back_out mix_ready out_ready x_done act_ready hid_ready hid_free
        memt_ready mem_out bias_half""".split()
    s = {n: signal(n) for n in names}
    w_ready = [signal(f"w_ready{i}") for i in range(7)]

    def wa(at, *shape):
        n = int(np.prod(shape))
        v = weights_a[:, at:at + n]
        return split_free(v, shape), at + n

    def wb(at, *shape):
        n = int(np.prod(shape))
        v = weights_b[:, at:at + n]
        return split_free(v, shape), at + n

    def split_free(v, shape):
        if len(shape) == 1:
            return v
        if len(shape) == 2:
            return v.rearrange("p (a b) -> p a b", b=shape[1])
        return v.rearrange("p (a b c) -> p a b c", b=shape[1], c=shape[2])

    at = 0
    w_qk, at = wa(at, 2, FC, 2 * DIM)
    w_v, at = wa(at, 2, FC, DIM)
    w_dense, at = wa(at, 2, FC, DIM)
    at = 0
    w_cq, at = wb(at, FC, P)
    w_ck, at = wb(at, P)
    w_cv, at = wb(at, P)
    w_cdense, at = wb(at, DIM)
    at = 0
    w_gate, at = wa(at, FC, HTILES * P)
    w_up, at = wa(at, FC, HTILES * P)
    w_down, at = wa(at, HTILES, DIM)
    at = 0
    w_q1, at = wb(at, FC, HEADS * HD1)
    w_k1, at = wb(at, HEADS * HD1)
    w_v1, at = wb(at, HEADS * HD1)
    w_o1, at = wb(at, 8, DIM)
    assert at <= 6144
    at = 0
    w_ff1, at = wa(at, FC, MLP1)
    w_ff2, at = wa(at, 8, DIM)
    fuse_w = []
    for take in (wb, wa):
        w_mem, at = take(0, DIM)
        w_g, at = take(at, 4, DIM)
        b_g, at = take(at, FC)
        fuse_w.append((w_mem, w_g, b_g))

    loads = [
        [(w_qk[:, 0], a["v_qk"].rearrange("(c p) n -> p c n", p=P)), (w_qk[:, 1], a["l_qk"].rearrange("(c p) n -> p c n", p=P)),
         (w_v[:, 0], a["v_v"].rearrange("(c p) n -> p c n", p=P)), (w_v[:, 1], a["l_v"].rearrange("(c p) n -> p c n", p=P)),
         (w_dense[:, 0], a["v_dense"].rearrange("(c p) n -> p c n", p=P)),
         (w_dense[:, 1], a["l_dense"].rearrange("(c p) n -> p c n", p=P))],
        [(w_cq, a["cq"].rearrange("(c p) n -> p c n", p=P)), (w_ck, a["ck"]), (w_cv, a["cv"]), (w_cdense, a["cdense"])],
        [(w_gate, a["gate0"].rearrange("(c p) n -> p c n", p=P)), (w_up, a["up0"].rearrange("(c p) n -> p c n", p=P)),
         (w_down, a["down0"].rearrange("(c p) n -> p c n", p=P))],
        [(w_q1, a["wq"].rearrange("(c p) n -> p c n", p=P)), (w_k1, a["wk"]), (w_v1, a["wv"]),
         (w_o1, a["wo"].rearrange("(c p) n -> p c n", p=P))],
        [(w_ff1, a["w1"].rearrange("(c p) n -> p c n", p=P)), (w_ff2, a["w2"].rearrange("(c p) n -> p c n", p=P))],
        [(fuse_w[0][0], a["mem2"]), (fuse_w[0][1], a["g2"].rearrange("(c p) n -> p c n", p=P)), (fuse_w[0][2], a["b2"])],
        [(fuse_w[1][0], a["mem3"]), (fuse_w[1][1], a["g3"].rearrange("(c p) n -> p c n", p=P)), (fuse_w[1][2], a["b3"])],
    ]
    for w, some in zip(w_ready, loads):
        w.block(len(some), groups=1, amount=16)

    def load_weights(eng, n):
        for dst, src in loads[n]:
            eng.dma_start(dst, src).then_inc(w_ready[n].sem, 16)

    def weights_there(eng, n):
        eng.wait_ge(w_ready[n].sem, w_ready[n].total)

    def tok(view, g):
        return view[..., bass.ds(g * GT, GT)]

    with ExitStack() as own:
        tt = sb("tt", [P, TOKENS], I32, own)
        is_one = sb("is_one", [P, BATCHES, SEQ], F32, own)
        keys = sb("keys", [1, TOKENS // 4], I32, own)
        pos_i = sb("pos_i", [P, SEQ], I32, own)
        pos_f = sb("pos_f", [P, SEQ], F32, own)
        pos_neg = sb("pos_neg", [P, SEQ], F32, own)
        onehot = sb("onehot", [P, SEQ], F32, own)
        consts = sb("consts", [P, 2 * P + 1], F32, own)
        raw_gates = sb("raw_gates", [P, 2], F32, own)
        s["setup_d"].block(15, 1)
        s["setup_p"].block(4, 1)
        s["setup_a"].block(1, 1)
        s["loaded"].block(9, 1, 16)
        s["proj_ready"].block(1, 1)
        with nc.Block() as block:
            @block.sync
            def _(eng):
                for dst, src in ((x_t[:], a["x"]), (tt[:], a["tt"].partition_broadcast(P)),
                                 (consts[:], a["consts"]), (ident[:], a["ident"]),
                                 (pos_i[:], a["pos"].partition_broadcast(P)), (keys[:], a["keys"]),
                                 (scales[:], a["scales"]), (raw_gates[:], a["gates"].partition_broadcast(P)),
                                 (causal[:], a["causal"])):
                    eng.dma_start(dst, src).then_inc(s["loaded"].sem, 16)
                load_weights(eng, 0)
                load_weights(eng, 1)

            @block.gpsimd
            def _(eng):
                eng.memset(mean_w[:], 1.0 / DIM).then_inc(s["setup_p"].sem, 1)
                eng.memset(ones_row[:], 1.0).then_inc(s["setup_p"].sem, 1)
                eng.memset(eps_cols[:, 0:1], EPS_RMS).then_inc(s["setup_p"].sem, 1)
                eng.memset(eps_cols[:, 1:2], EPS_LN).then_inc(s["setup_p"].sem, 1)

            @block.scalar
            def _(eng):
                eng.wait_ge(s["loaded"].sem, s["loaded"].total)
                eng.activation(gates[:], raw_gates[:], ACT.Tanh).then_inc(s["setup_a"].sem, 1)

            @block.vector
            def _(eng):
                done = [0]

                def step(ins):
                    done[0] += 1
                    ins.then_inc(s["setup_d"].sem, 1)
                    eng.wait_ge(s["setup_d"].sem, done[0])

                eng.wait_ge(s["loaded"].sem, s["loaded"].total)
                step(eng.tensor_copy(pos_f[:], pos_i[:]))
                step(eng.tensor_scalar(pos_neg[:], pos_f[:], 0.0, float(SEQ), ALU.is_lt, ALU.mult))
                step(eng.tensor_tensor(pos_f[:], pos_f[:], pos_neg[:], ALU.add))
                step(eng.tensor_scalar(pos_f[:], pos_f[:], 0.0, float(SEQ - 1), ALU.max, ALU.min))
                step(eng.tensor_scalar(onehot[:], pos_f[:], consts[:, 2 * P:2 * P + 1], None, ALU.is_equal))
                step(eng.tensor_copy(ident_b[:], ident[:]))
                step(eng.tensor_scalar(is_one[:].rearrange("p b n -> p (b n)"), tt[:], 1.0, None, ALU.is_equal))
                vis = expert[:, 0, :].rearrange("p (b n) -> p b n", n=SEQ)
                step(eng.tensor_tensor(vis[:, :, 0:SEQ - 1], is_one[:, :, 0:SEQ - 1], is_one[:, :, 1:SEQ], ALU.mult))
                step(eng.memset(vis[:, :, SEQ - 1:SEQ], 0.0))
                step(eng.tensor_scalar(expert[:, 1, :], expert[:, 0, :], -1.0, 1.0, ALU.mult, ALU.add))
                step(eng.tensor_copy(rest_mask[0:REST_AT, :], expert[0:REST_AT, 0, :]))
                step(eng.tensor_copy(rest_mask[REST_AT:P, :], expert[REST_AT:P, 1, :]))
                step(eng.tensor_scalar(key_bias[:], keys[:].bitcast(U8), -1.0, -MASKED, ALU.add, ALU.mult))
                eng.wait_ge(s["proj_ready"].sem, s["proj_ready"].upto(0, 1))
                tables = bank[0][:, 0:2 * SEQ].rearrange("p (a n) -> p a n", a=2)
                step(eng.tensor_scalar(rope[:, 0], tables, HD0 ** -0.5, None, ALU.mult))
                step(eng.tensor_copy(rope[:, 1], tables))

            @block.tensor
            def _(eng):
                eng.wait_ge(s["setup_d"].sem, 5)
                eng.matmul(bank[0][:, 0:SEQ], consts[:, 0:P], onehot[:], start=True, stop=True)
                eng.matmul(bank[0][:, SEQ:2 * SEQ], consts[:, P:2 * P], onehot[:], start=True,
                           stop=True).then_inc(s["proj_ready"].sem, 1)

    class Norm:

        def __init__(self, own, scale, bias=None, src=None, banks=(6, 7), ahead=False, apart=False):
            self.scale, self.bias, self.src, self.ahead = scale, bias, src, ahead
            self.eps_col = eps_cols[:, 0:1] if bias is None else eps_cols[:, 1:2]
            self.mean_bank, self.square_bank = bank[banks[0]], bank[banks[1]]
            self.sq = sb("sq", [P, FC, GT], F32, own)
            self.xn = sb("xn", [P, FC, GT], F32, own)
            self.pre = sb("pre", [P, FC, GT], F32, own) if apart else self.xn
            self.dev = sb("dev", [P, GT], F32, own)
            self.rstd = sb("rstd", [P, GT], F32, own)
            for n, k in (("sq_ready", 1), ("mean_ready", 1 if bias is None else 2), ("centre_ready", 0 if bias is None else FC),
                         ("dev_ready", 1), ("rstd_ready", 1), ("xn_ready", FC if bias is None else 2 * FC)):
                s[n].block(k)

        def x(self, g):
            return tok(x_t[:], g) if self.src is None else self.src[:]

        def square(self, eng, g):
            if self.bias is None:
                eng.activation(self.sq[:], self.x(g), ACT.Square).then_inc(s["sq_ready"].sem, 1)
            else:
                eng.wait_ge(s["centre_ready"].sem, s["centre_ready"].upto(g, FC))
                eng.activation(self.sq[:], self.pre[:], ACT.Square).then_inc(s["sq_ready"].sem, 1)

        def root(self, eng, g):
            n = s["mean_ready"].per_group
            eng.wait_ge(s["mean_ready"].sem, s["mean_ready"].upto(g, n))
            if self.ahead:
                eng.wait_ge(s["rstd_ready"].sem, s["rstd_ready"].upto(g, 0))
            eng.activation(self.dev[:], self.square_bank, ACT.Sqrt, bias=self.eps_col).then_inc(s["dev_ready"].sem, 1)

        def mean(self, eng, g):
            for c in range(FC):
                mm = eng.matmul(self.mean_bank, mean_w[:], x_t[:, c, bass.ds(g * GT, GT)], start=c == 0, stop=c == FC - 1)
            mm.then_inc(s["mean_ready"].sem, 1)

        def tensor(self, eng, g):
            eng.wait_ge(s["sq_ready"].sem, s["sq_ready"].upto(g, 1))
            for c in range(FC):
                mm = eng.matmul(self.square_bank, mean_w[:], self.sq[:, c, :], start=c == 0, stop=c == FC - 1)
            mm.then_inc(s["mean_ready"].sem, 1)

        def centre(self, eng, g):
            eng.wait_ge(s["mean_ready"].sem, s["mean_ready"].upto(g, 1))
            for c in range(FC):
                eng.tensor_tensor(self.pre[:, c, :], x_t[:, c, bass.ds(g * GT, GT)], self.mean_bank,
                                  ALU.subtract).then_inc(s["centre_ready"].sem, 1)
            eng.wait_ge(s["centre_ready"].sem, s["centre_ready"].upto(g, FC))

        def reciprocal(self, eng, g):
            eng.wait_ge(s["dev_ready"].sem, s["dev_ready"].upto(g, 1))
            eng.reciprocal(self.rstd[:], self.dev[:]).then_inc(s["rstd_ready"].sem, 1)

        def scaled(self, eng, g):
            eng.wait_ge(s["rstd_ready"].sem, s["rstd_ready"].upto(g, 1))
            for c in range(FC):
                src = self.pre[:, c, :] if self.bias is not None else self.x(g)[:, c]
                eng.scalar_tensor_tensor(out=self.pre[:, c, :], in0=src, scalar=scales[:, self.scale, c:c + 1],
                                         in1=self.rstd[:], op0=ALU.mult, op1=ALU.mult).then_inc(s["xn_ready"].sem, 1)

        def biased(self, eng, g):
            for c in range(FC):
                eng.wait_ge(s["xn_ready"].sem, s["xn_ready"].upto(g, c + 1))
                eng.tensor_scalar(self.xn[:, c, :], self.pre[:, c, :], scales[:, self.bias, c:c + 1], None,
                                  ALU.add).then_inc(s["xn_ready"].sem, 1)

        def pool(self, eng, g):
            eng.wait_ge(s["rstd_ready"].sem, s["rstd_ready"].upto(g, 1))
            for c in range(FC):
                eng.tensor_tensor(self.pre[:, c, :], self.pre[:, c, :], self.rstd[:], ALU.mult).then_inc(s["xn_ready"].sem, 1)
            for c in range(FC):
                eng.wait_ge(s["xn_ready"].sem, s["xn_ready"].upto(g, c + 1))
                eng.tensor_scalar(self.xn[:, c, :], self.pre[:, c, :], scales[:, self.scale, c:c + 1],
                                  scales[:, self.bias, c:c + 1], ALU.mult, ALU.add).then_inc(s["xn_ready"].sem, 1)

        def vector(self, eng, g):
            self.reciprocal(eng, g)
            self.scaled(eng, g)
            if self.bias is not None:
                self.biased(eng, g)

        def there(self, eng, g):
            eng.wait_ge(s["xn_ready"].sem, s["xn_ready"].upto(g, s["xn_ready"].per_group))

    def product(eng, to, factors):
        for n, (w, x) in enumerate(factors):
            mm = eng.matmul(to, w, x, start=n == 0, stop=n == len(factors) - 1)
        return mm

    def no_bias(eng, g, to, b):
        pass

    class Attention:

        def __init__(self, own, hd, score, bias, value, turns, unit, post, head=None):
            self.head = head or (lambda q, i: q * QUAD + i)
            self.hd, self.score, self.bias, self.value = hd, score, bias, value
            self.turns, self.unit, self.post = turns, unit, post
            self.quads = GROUPS * QUADS
            self.units = self.quads // unit
            self.c_banks = [4] if unit > 1 else [4, 5]
            self.g_banks = [5] if unit > 1 else self.c_banks
            self.p = sb("p", [P, 3, QUAD, SEQ], F32, own)
            self.pt = sb("pt", [P, 3, QUAD, SEQ], F32, own)
            self.nmax = sb("nmax", [P, 2, QUAD], F32, own)
            self.recip = sb("recip", [P, unit * QUAD], F32, own)
            self.ctx = sb("ctx", [P, 2, turns * P], F32, own)
            for n in ("scores_ready", "max_ready", "p_ready", "turned_ready", "pt_ready", "ctx_ready"):
                s[n].block(self.quads, 1)
            for n in ("recip_ready", "norm_ready", "back_ready"):
                s[n].block(self.units, 1)

        def wait(self, eng, name, n):
            eng.wait_ge(s[name].sem, s[name].upto(0, n))

        def where(self, n):
            return n // QUADS, n % QUADS // (HEADS // QUAD), n % (HEADS // QUAD)

        def tensor(self, eng, between):
            for n in range(self.quads + 5):
                if n < self.quads:
                    if n >= 2:
                        self.wait(eng, "p_ready", n - 1)
                    g, b, q = self.where(n)
                    self.bias(eng, g, s_pair[:, n % 2, :], b)
                    for h in range(QUAD):
                        w, x = self.score(g, b, self.head(q, h))
                        mm = eng.matmul(s_pair[:, n % 2, h * SEQ:(h + 1) * SEQ], w, x, start=self.bias is no_bias,
                                        stop=True, skip_group_check=True)
                    mm.then_inc(s["scores_ready"].sem, 1)
                between(eng, n, 0)
                m = n - 4
                if 0 <= m < self.quads:
                    self.wait(eng, "pt_ready", m + 1)
                    u, part = divmod(m, self.unit)
                    last = u - len(self.c_banks)
                    if part == 0 and last >= 0:
                        if self.g_banks is self.c_banks:
                            eng.wait_ge(s["back_out"].sem, s["back_out"].upto(0, (last + 1) * self.takes))
                        else:
                            self.wait(eng, "norm_ready", last + 1)
                    g, b, q = self.where(m)
                    to = bank[self.c_banks[u % len(self.c_banks)]]
                    for h in range(QUAD):
                        at = (part * QUAD + h) * (self.hd + 1)
                        mm = eng.matmul(to[:, at:at + self.hd + 1], self.pt[:, m % 3, h, :],
                                        self.value(g, b, self.head(q, h)), start=True, stop=True, skip_group_check=True)
                    mm.then_inc(s["ctx_ready"].sem, 1)
                between(eng, n, 1)
                m = n - 2
                if 0 <= m < self.quads:
                    self.wait(eng, "p_ready", m + 1)
                    if m >= 2:
                        self.wait(eng, "pt_ready", m - 1)
                    for h in range(QUAD):
                        mm = eng.transpose(t_pair[:, m % 2, h * SEQ:(h + 1) * SEQ], self.p[:, m % 3, h, :], ident[:])
                    mm.then_inc(s["turned_ready"].sem, 1)
                between(eng, n, 2)
                m = n - 5
                if 0 <= m < self.quads and (m + 1) % self.unit == 0:
                    u = m // self.unit
                    self.wait(eng, "norm_ready", u + 1)
                    if u and self.g_banks is not self.c_banks:
                        eng.wait_ge(s["back_out"].sem, s["back_out"].upto(0, u * self.takes))
                    for t in range(self.turns):
                        mm = eng.transpose(bank[self.g_banks[u % len(self.g_banks)]][:, t * P:(t + 1) * P],
                                           self.ctx[:, u % 2, t * P:(t + 1) * P], ident[:])
                    mm.then_inc(s["back_ready"].sem, 1)

        def scalar(self, eng, between):
            for n in range(self.quads + 5):
                if n < self.quads:
                    self.wait(eng, "max_ready", n + 1)
                    if n >= 3:
                        self.wait(eng, "turned_ready", n - 2)
                    for h in range(QUAD):
                        e = eng.activation(self.p[:, n % 3, h, :], s_pair[:, n % 2, h * SEQ:(h + 1) * SEQ], ACT.Exp,
                                           bias=self.nmax[:, n % 2, h:h + 1])
                    e.then_inc(s["p_ready"].sem, 1)
                between(eng, n, 0)

        def vector(self, eng, between):
            for n in range(self.quads + 5):
                if n < self.quads:
                    self.wait(eng, "scores_ready", n + 1)
                    if n >= 2:
                        self.wait(eng, "p_ready", n - 1)
                    eng.tensor_reduce(self.nmax[:, n % 2, :], s_pair[:, n % 2, :].rearrange("p (h k) -> p h k", h=QUAD),
                                      AX_X, ALU.max, negate=True).then_inc(s["max_ready"].sem, 1)
                between(eng, n, 0)
                m = n - 4
                if 0 <= m < self.quads and (m + 1) % self.unit == 0:
                    u = m // self.unit
                    heads = self.unit * QUAD
                    c = bank[self.c_banks[u % len(self.c_banks)]][:, 0:heads * (self.hd + 1)]
                    c = c.rearrange("p (h d) -> p h d", h=heads)
                    self.wait(eng, "ctx_ready", m + 1)
                    if u:
                        self.wait(eng, "norm_ready", u)
                    eng.reciprocal(self.recip[:], c[:, :, self.hd]).then_inc(s["recip_ready"].sem, 1)
                    self.wait(eng, "recip_ready", u + 1)
                    if u >= 2:
                        self.wait(eng, "back_ready", u - 1)
                    eng.tensor_tensor(self.ctx[:, u % 2, :].rearrange("p (h d) -> p h d", h=heads), c[:, :, 0:self.hd],
                                      self.recip[:].unsqueeze(2).to_broadcast([P, heads, self.hd]), ALU.mult)\
                       .then_inc(s["norm_ready"].sem, 1)
                between(eng, n, 1)
                m = n - 2
                if 0 <= m < self.quads:
                    self.wait(eng, "turned_ready", m + 1)
                    if m >= 3:
                        self.wait(eng, "ctx_ready", m - 2)
                    eng.tensor_copy(self.pt[:, m % 3].rearrange("p h k -> p (h k)"),
                                    t_pair[:, m % 2, :]).then_inc(s["pt_ready"].sem, 1)
                between(eng, n, 2)
                m = n - 5
                if 0 <= m < self.quads and (m + 1) % self.unit == 0:
                    u = m // self.unit
                    self.wait(eng, "back_ready", u + 1)
                    self.post(eng, u)

    class Split:

        def __init__(self, own, src, n):
            self.src, self.n = src, n
            self.parts = [sb("parts", [P, 3, 2, GT], BF16, own) for _ in range(n)]
            self.res = sb("res", [P, 2, GT], F32, own)
            for k in ("hi_ready", "mid_ready", "lo_ready", "res_ready"):
                s[k].block(n)

        def high(self, eng, g, i):
            self.src_there(eng, g, i)
            if g:
                eng.wait_ge(s["stacked"].sem, s["stacked"].upto(g, 0))
            eng.activation(self.parts[i][:, 0], self.src[:], ACT.Copy).then_inc(s["hi_ready"].sem, 1)

        def rest(self, eng, g, i):
            eng.wait_ge(s["hi_ready"].sem, s["hi_ready"].upto(g, i + 1))
            eng.tensor_tensor(self.res[:], self.src[:], self.parts[i][:, 0], ALU.subtract).then_inc(s["res_ready"].sem, 1)

        def middle(self, eng, g, i):
            eng.wait_ge(s["res_ready"].sem, s["res_ready"].upto(g, i + 1))
            eng.activation(self.parts[i][:, 1], self.res[:], ACT.Copy).then_inc(s["mid_ready"].sem, 1)

        def low(self, eng, g, i):
            eng.wait_ge(s["mid_ready"].sem, s["mid_ready"].upto(g, i + 1))
            eng.tensor_tensor(self.parts[i][:, 2], self.res[:], self.parts[i][:, 1], ALU.subtract)\
               .then_inc(s["lo_ready"].sem, 1)

        def part_there(self, eng, g, i, part):
            ready = s[("hi_ready", "mid_ready", "lo_ready")[part]]
            eng.wait_ge(ready.sem, ready.upto(g, i + 1))

    def stack_rows(eng, stack, parts, which, part, base, rows):
        for slot, has in enumerate(SLOT_PARTS):
            if has[which] == part:
                at = base + slot * rows
                eng.dma_start(stack[at:at + rows, :, :], parts[:, part]).then_inc(s["stacked"].sem, 16)

    def residual(eng, g, banks, ready, n):
        eng.wait_ge(ready.sem, ready.upto(g, n))
        for m in range(FC):
            xs = x_t[:, m, bass.ds(g * GT, GT)]
            eng.tensor_tensor(xs, xs, banks[m], ALU.add).then_inc(s["x_done"].sem, 1)

    def group_start(eng, g, first):
        if not first:
            eng.wait_ge(s["x_done"].sem, s["x_done"].upto(g, 0))

    def around(front, back=None):
        def between(eng, n, slot):
            g, at = divmod(n, QUADS)
            if back and g >= 1:
                back(eng, g - 1, at, slot)
            if g + 1 < GROUPS:
                front(eng, g + 1, at, slot)
        return between

    def first_front(eng, front):
        for at in range(QUADS):
            for slot in range(3):
                front(eng, 0, at, slot)

    def self_attention():
        with ExitStack() as own:
            norm = Norm(own, W_LN_IN, ahead=True)
            xe = sb("xe", [P, 2, FC, GT], F32, own)
            rot_c = sb("rot_c", [P, 2, GT], F32, own)
            rot_s = sb("rot_s", [P, 2, GT], F32, own)
            rot = sb("rot", [P, 2, GT], F32, own)
            split = Split(own, rot, 2)
            spare_a = weights_a[0:SLOTS * HD0, 4096:4096 + HEADS * GT // 2].bitcast(BF16).rearrange("p (h n) -> p h n", h=HEADS)
            spare_b = weights_b[0:SLOTS * HD0, 1024:1024 + HEADS * GT // 2].bitcast(BF16).rearrange("p (h n) -> p h n", h=HEADS)
            q_stack = [sb("q_stack", [SLOTS * HD0, HEADS, GT], BF16, own)[:], spare_a]
            k_stack = [sb("k_stack", [SLOTS * HD0, HEADS, GT], BF16, own)[:], spare_b]
            val = sb("val", [P, 2, GROUP, HEADS, HD0 + 1], F32, own)
            mixed = sb("mixed", [P, 2, FC, GT], F32, own)
            for n, k in (("xv_ready", 1), ("xl_ready", 1), ("proj_ready", 4), ("rot_part", 8), ("rot_ready", 4),
                         ("v_ready", GROUP), ("v_out_a", GROUP // 2), ("v_out_d", GROUP // 2), ("back_out", 2 * GROUP),
                         ("out_ready", FC), ("x_done", FC)):
                s[n].block(k)
            s["stacked"].block(4 * SLOTS, amount=16)
            s["setup_p"].block(1, 1)

            def causal_bias(eng, g, to, b):
                eng.matmul(to, ident_b[:], causal[:].unsqueeze(1).to_broadcast([P, QUAD, SEQ]), start=True, stop=False,
                           skip_group_check=True)

            def post(eng, u):
                g, b = divmod(u, GROUP)
                if b == 0 and g:
                    eng.wait_ge(s["out_ready"].sem, s["out_ready"].upto(g - 1, FC))
                src = bank[5][:, 0:FC * P].rearrange("p (c n) -> p c n", c=FC)
                for e in range(2):
                    mask = expert[:, e, u * SEQ:(u + 1) * SEQ].unsqueeze(1).to_broadcast([P, FC, SEQ])
                    eng.tensor_tensor(mixed[:, e, :, b * SEQ:(b + 1) * SEQ], src, mask, ALU.mult)\
                       .then_inc(s["back_out"].sem, 1)

            def score(g, b, h):
                cols = slice(b * SEQ, (b + 1) * SEQ)
                return q_stack[g % 2][:, h, cols], k_stack[g % 2][:, h, cols]

            att = Attention(own, HD0, score, causal_bias, lambda g, b, h: val[:, g % 2, b, h, :], FC, HEADS // QUAD, post)
            att.takes = 2

            def project(eng, g, i, half):
                if i == 0 and half == 0:
                    eng.wait_ge(s["xv_ready"].sem, s["xv_ready"].upto(g, 1))
                    eng.wait_ge(s["xl_ready"].sem, s["xl_ready"].upto(g, 1))
                if i == 0 and g:
                    if g >= 2:
                        eng.wait_ge(s["x_done"].sem, s["x_done"].upto(g - 2, half + 1))
                if i == 1:
                    eng.wait_ge(s["rot_part"].sem, s["rot_part"].upto(g, 2 * half + 2))
                col = (2 * i + half) * P
                product(eng, bank[6 + half], [(w_qk[:, e, c, col:col + P], xe[:, e, c, :])
                                              for e in range(2) for c in range(FC)]).then_inc(s["proj_ready"].sem, 1)

            def values(eng, g, first):
                if first == 0:
                    eng.wait_ge(s["rot_part"].sem, s["rot_part"].upto(g, 8))
                for b in (first, first + 1):
                    if first:
                        out_of = s["v_out_a"] if b % 2 else s["v_out_d"]
                        eng.wait_ge(out_of.sem, out_of.upto(g, 1))
                    product(eng, bank[6 + b % 2][:, 0:DIM], [(xe[:, e, c, b * SEQ:(b + 1) * SEQ], w_v[:, e, c, :])
                                                             for e in range(2) for c in range(FC)])\
                        .then_inc(s["v_ready"].sem, 1)

            def mean(eng, g):
                if g:
                    eng.wait_ge(s["v_out_a"].sem, s["v_out_a"].upto(g - 1, GROUP // 2))
                norm.tensor(eng, g)

            def output(eng, g, m):
                if m == 0:
                    eng.wait_ge(s["back_out"].sem, s["back_out"].upto(g, 2 * GROUP))
                    eng.wait_ge(s["v_out_d"].sem, s["v_out_d"].upto(min(g + 1, GROUPS - 1), GROUP // 2))
                    eng.wait_ge(s["v_out_a"].sem, s["v_out_a"].upto(min(g + 1, GROUPS - 1), GROUP // 2))
                    if g + 2 < GROUPS:
                        eng.wait_ge(s["dev_ready"].sem, s["dev_ready"].upto(g + 2, 1))
                product(eng, bank[6 + m], [(w_dense[:, e, c, m * P:(m + 1) * P], mixed[:, e, c, :])
                                           for e in range(2) for c in range(FC)]).then_inc(s["out_ready"].sem, 1)

            def pe_front(eng, g, at, slot):
                if slot == 0:
                    if at == 1:
                        mean(eng, g)
                    elif 7 <= at < 11:
                        project(eng, g, (at - 7) // 2, (at - 7) % 2)
                    elif at in (12, 14):
                        values(eng, g, at - 12)
                elif (at, slot) == (15, 2):
                    eng.wait_ge(s["stacked"].sem, s["stacked"].upto(g, 4 * SLOTS))
                    for out_of in (s["v_out_a"], s["v_out_d"]):
                        eng.wait_ge(out_of.sem, out_of.upto(g, GROUP // 2))

            def pe_back(eng, g, at, slot):
                if at in (5, 6) and slot == 0:
                    output(eng, g, at - 5)

            def rotated(eng, g, i, half):
                eng.wait_ge(s["proj_ready"].sem, s["proj_ready"].upto(g, 2 * i + half + 1))
                if half == 0 and (g or i):
                    eng.wait_ge(s["rot_ready"].sem, s["rot_ready"].upto(g, 2 * i))
                for k, to in enumerate((rot_c, rot_s)):
                    eng.tensor_tensor(to[:, half].rearrange("p (b n) -> p b n", n=SEQ),
                                      bank[6 + half].rearrange("p (b n) -> p b n", n=SEQ),
                                      rope[:, i, k, :].unsqueeze(1).to_broadcast([P, GROUP, SEQ]),
                                      ALU.mult).then_inc(s["rot_part"].sem, 1)

            def take_values(eng, g, b):
                eng.wait_ge(s["v_ready"].sem, s["v_ready"].upto(g, b + 1))
                to, src = val[:, g % 2, b, :, 0:HD0], bank[6 + b % 2][:, 0:DIM].rearrange("p (h d) -> p h d", h=HEADS)
                if b % 2:
                    eng.activation(to, src, ACT.Copy).then_inc(s["v_out_a"].sem, 1)
                else:
                    eng.tensor_copy(to, src).then_inc(s["v_out_d"].sem, 1)

            def add(eng, g, m):
                eng.wait_ge(s["out_ready"].sem, s["out_ready"].upto(g, m + 1))
                xs = x_t[:, m, g * GT:(g + 1) * GT]
                eng.tensor_tensor(xs, xs, bank[6 + m], ALU.add).then_inc(s["x_done"].sem, 1)

            def dve_front(eng, g, at, slot):
                if (at, slot) == (2, 2):
                    norm.reciprocal(eng, g)
                elif (at, slot) == (3, 2):
                    if g:
                        eng.wait_ge(s["xv_ready"].sem, s["xv_ready"].upto(g - 1, 1))
                        eng.wait_ge(s["xl_ready"].sem, s["xl_ready"].upto(g - 1, 1))
                    norm.scaled(eng, g)
                elif 8 <= at < 12 and slot == 1:
                    rotated(eng, g, (at - 8) // 2, (at - 8) % 2)
                elif at in (12, 14) and slot == 2:
                    take_values(eng, g, at - 12)

            def dve_back(eng, g, at, slot):
                if at in (6, 7) and slot == 2:
                    add(eng, g, at - 6)

            def act_front(eng, g, at, slot):
                if slot == 0:
                    if at == 0:
                        norm.square(eng, g)
                    elif at == 1:
                        norm.root(eng, g)
                    elif at in (10, 12):
                        split.high(eng, g, (at - 10) // 2)
                    elif at in (11, 13):
                        split.middle(eng, g, (at - 10) // 2)
                    if at in (13, 15):
                        take_values(eng, g, at - 12)

            split.src_there = lambda eng, g, i: eng.wait_ge(s["rot_ready"].sem, s["rot_ready"].upto(g, 2 * i + 2))

            with nc.Block() as block:
                @block.sync
                def _(eng):
                    for g in range(GROUPS):
                        for i, stack in enumerate((q_stack, k_stack)):
                            if g >= 2 and i == 0:
                                att.wait(eng, "scores_ready", QUADS * (g - 1))
                            for part in range(3):
                                split.part_there(eng, g, i, part)
                                for half in range(2):
                                    stack_rows(eng, stack[g % 2], split.parts[i][:, :, half, :], i, part,
                                               half * SLOTS * HALF, HALF)

                @block.gpsimd
                def _(eng):
                    eng.memset(val[:], 1.0).then_inc(s["setup_p"].sem, 1)
                    for g in range(GROUPS):
                        norm.there(eng, g)
                        if g:
                            eng.wait_ge(s["v_ready"].sem, s["v_ready"].upto(g - 1, GROUP))
                        for e, ready in enumerate((s["xv_ready"], s["xl_ready"])):
                            mask = expert[:, e, g * GT:(g + 1) * GT].unsqueeze(1).to_broadcast([P, FC, GT])
                            eng.tensor_tensor(xe[:, e], norm.xn[:], mask, ALU.mult).then_inc(ready.sem, 1)
                        for i in range(2):
                            eng.wait_ge(s["rot_part"].sem, s["rot_part"].upto(g, 4 * i + 4))
                            if g or i:
                                eng.wait_ge(s["hi_ready"].sem, s["hi_ready"].upto(g, i))
                                eng.wait_ge(s["res_ready"].sem, s["res_ready"].upto(g, i))
                            eng.tensor_tensor(rot[:, 0], rot_c[:, 0], rot_s[:, 1], ALU.subtract).then_inc(s["rot_ready"].sem, 1)
                            eng.tensor_tensor(rot[:, 1], rot_c[:, 1], rot_s[:, 0], ALU.add).then_inc(s["rot_ready"].sem, 1)
                            eng.wait_ge(s["rot_ready"].sem, s["rot_ready"].upto(g, 2 * i + 2))
                            split.rest(eng, g, i)
                            split.low(eng, g, i)

                @block.scalar
                def _(eng):
                    eng.wait_ge(s["setup_p"].sem, s["setup_p"].upto(0, 1))
                    first_front(eng, act_front)
                    att.scalar(eng, around(act_front))

                @block.vector
                def _(eng):
                    eng.wait_ge(s["setup_p"].sem, s["setup_p"].upto(0, 1))
                    first_front(eng, dve_front)
                    att.vector(eng, around(dve_front, dve_back))
                    for m in range(FC):
                        add(eng, GROUPS - 1, m)

                @block.tensor
                def _(eng):
                    weights_there(eng, 0)
                    first_front(eng, pe_front)
                    att.tensor(eng, around(pe_front, pe_back))
                    for m in range(FC):
                        output(eng, GROUPS - 1, m)

    def cross_attention():
        with ExitStack() as own:
            norm = Norm(own, W_LN_CROSS, ahead=True)
            context = sb("context", [P, GT], F32, own)
            qk = sb("qk", [P, 2, GT], F32, own)
            split = Split(own, qk, 1)
            stack = sb("stack", [SLOTS * HD0C, 2, 2, HEADS, GT], BF16, own)
            val = sb("val", [P, 2, GROUP, HEADS, HD0C + 1], F32, own)
            gathered = sb("gathered", [P, GT], F32, own)
            for n, k in (("proj_ready", 2), ("rot_ready", 2), ("v_ready", 1), ("v_out_d", 1),
                         ("back_out", GROUP), ("out_ready", FC), ("x_done", FC)):
                s[n].block(k)
            s["stacked"].block(2 * SLOTS, amount=16)
            s["ctx_loaded"].block(1, amount=16)
            s["setup_p"].block(1, 1)
            split.src_there = lambda eng, g, i: eng.wait_ge(s["rot_ready"].sem, s["rot_ready"].upto(g, 2))

            def post(eng, u):
                g, b = divmod(u, GROUP)
                if b == 0 and g:
                    eng.wait_ge(s["out_ready"].sem, s["out_ready"].upto(g - 1, FC))
                eng.tensor_copy(gathered[:, b * SEQ:(b + 1) * SEQ], bank[5][:, 0:SEQ]).then_inc(s["back_out"].sem, 1)

            def score(g, b, h):
                cols = slice(b * SEQ, (b + 1) * SEQ)
                return stack[:, g % 2, 0, h, cols], stack[:, g % 2, 1, h, cols]

            att = Attention(own, HD0C, score, no_bias, lambda g, b, h: val[:, g % 2, b, h, :], 1, HEADS // QUAD, post)
            att.takes = 1

            def mean(eng, g):
                if g:
                    eng.wait_ge(s["v_out_d"].sem, s["v_out_d"].upto(g - 1, 1))
                norm.tensor(eng, g)

            def project(eng, g):
                norm.there(eng, g)
                product(eng, bank[6], [(w_cq[:, c, :], norm.xn[:, c, :]) for c in range(FC)])\
                    .then_inc(s["proj_ready"].sem, 1)
                eng.wait_ge(s["ctx_loaded"].sem, s["ctx_loaded"].upto(g, 1))
                eng.wait_ge(s["dev_ready"].sem, s["dev_ready"].upto(g, 1))
                product(eng, bank[7], [(w_ck, context[:])]).then_inc(s["proj_ready"].sem, 1)

            def output(eng, g):
                eng.wait_ge(s["back_out"].sem, s["back_out"].upto(g, GROUP))
                if g + 2 < GROUPS:
                    eng.wait_ge(s["rot_ready"].sem, s["rot_ready"].upto(g + 2, 2))
                for m in range(FC):
                    product(eng, bank[6 + m], [(w_cdense[:, m * P:(m + 1) * P], gathered[:])])\
                        .then_inc(s["out_ready"].sem, 1)

            def values(eng, g):
                eng.wait_ge(s["rot_ready"].sem, s["rot_ready"].upto(g, 2))
                if g >= 2:
                    eng.wait_ge(s["x_done"].sem, s["x_done"].upto(g - 2, FC))
                for b in range(GROUP):
                    mm = product(eng, bank[6][:, b * P:(b + 1) * P], [(context[:, b * SEQ:(b + 1) * SEQ], w_cv)])
                mm.then_inc(s["v_ready"].sem, 1)

            def pe_front(eng, g, at, slot):
                if (at, slot) == (1, 0):
                    mean(eng, g)
                elif (at, slot) == (4, 0):
                    project(eng, g)
                elif (at, slot) == (9, 0):
                    values(eng, g)
                elif (at, slot) == (15, 2):
                    eng.wait_ge(s["stacked"].sem, s["stacked"].upto(g, 2 * SLOTS))
                    eng.wait_ge(s["v_out_d"].sem, s["v_out_d"].upto(g, 1))

            def pe_back(eng, g, at, slot):
                if (at, slot) == (7, 0):
                    output(eng, g)

            def take_values(eng, g):
                eng.wait_ge(s["v_ready"].sem, s["v_ready"].upto(g, 1))
                eng.tensor_copy(val[:, g % 2, :, :, 0:HD0C].rearrange("p b h d -> p (b h) d"),
                                bank[6].rearrange("p (h d) -> p h d", d=HD0C)).then_inc(s["v_out_d"].sem, 1)

            def add(eng, g, m):
                eng.wait_ge(s["out_ready"].sem, s["out_ready"].upto(g, m + 1))
                xs = x_t[:, m, g * GT:(g + 1) * GT]
                eng.tensor_tensor(xs, xs, bank[6 + m], ALU.add).then_inc(s["x_done"].sem, 1)

            def dve_front(eng, g, at, slot):
                if (at, slot) == (2, 2):
                    norm.reciprocal(eng, g)
                elif (at, slot) == (3, 2):
                    if g:
                        eng.wait_ge(s["proj_ready"].sem, s["proj_ready"].upto(g - 1, 1))
                    norm.scaled(eng, g)
                elif (at, slot) == (10, 2):
                    take_values(eng, g)

            def dve_back(eng, g, at, slot):
                if at in (7, 8) and slot == 2:
                    add(eng, g, at - 7)

            def take_projected(eng, g):
                if g:
                    eng.wait_ge(s["res_ready"].sem, s["res_ready"].upto(g - 1, 1))
                eng.wait_ge(s["proj_ready"].sem, s["proj_ready"].upto(g, 1))
                eng.activation(qk[:, 0], bank[6], ACT.Copy, scale=HD0C ** -0.5).then_inc(s["rot_ready"].sem, 1)
                eng.wait_ge(s["proj_ready"].sem, s["proj_ready"].upto(g, 2))
                eng.activation(qk[:, 1], bank[7], ACT.Copy).then_inc(s["rot_ready"].sem, 1)

            def act_front(eng, g, at, slot):
                if slot == 0:
                    if at == 0:
                        norm.square(eng, g)
                    elif at == 1:
                        norm.root(eng, g)
                    elif at == 5:
                        take_projected(eng, g)
                    elif at == 6:
                        split.high(eng, g, 0)
                    elif at == 8:
                        split.middle(eng, g, 0)

            with nc.Block() as block:
                @block.sync
                def _(eng):
                    for g in range(GROUPS):
                        if g:
                            eng.wait_ge(s["v_ready"].sem, s["v_ready"].upto(g - 1, 1))
                        eng.dma_start(context[:], a["ctx"][:, g * GT:(g + 1) * GT]).then_inc(s["ctx_loaded"].sem, 16)
                        if g == 0:
                            load_weights(eng, 2)
                        if g >= 2:
                            att.wait(eng, "scores_ready", QUADS * (g - 1))
                        for part in range(3):
                            split.part_there(eng, g, 0, part)
                            for i in range(2):
                                stack_rows(eng, stack[:, g % 2, i], split.parts[0][:, :, i, :], i, part, 0, HD0C)

                @block.gpsimd
                def _(eng):
                    eng.memset(val[:], 1.0).then_inc(s["setup_p"].sem, 1)
                    for g in range(GROUPS):
                        split.rest(eng, g, 0)
                        split.low(eng, g, 0)

                @block.scalar
                def _(eng):
                    eng.wait_ge(s["setup_p"].sem, s["setup_p"].upto(0, 1))
                    first_front(eng, act_front)
                    att.scalar(eng, around(act_front))

                @block.vector
                def _(eng):
                    eng.wait_ge(s["setup_p"].sem, s["setup_p"].upto(0, 1))
                    first_front(eng, dve_front)
                    att.vector(eng, around(dve_front, dve_back))
                    for m in range(FC):
                        add(eng, GROUPS - 1, m)

                @block.tensor
                def _(eng):
                    weights_there(eng, 1)
                    first_front(eng, pe_front)
                    att.tensor(eng, around(pe_front, pe_back))
                    output(eng, GROUPS - 1)

    def expert_mlp():
        with ExitStack() as own:
            norm = Norm(own, W_LN_MLP, ahead=True)
            xe = sb("xe", [P, 2, FC, GT], F32, own)
            act = sb("act", [P, 2, GT], F32, own)
            hid = sb("hid", [P, 3, GT], F32, own)
            for n, k in (("xv_ready", 1), ("xl_ready", 1), ("proj_ready", HTILES), ("act_ready", HTILES),
                         ("hid_ready", HTILES + 1), ("hid_free", HTILES), ("x_done", FC)):
                s[n].block(k)

            def banks(t):
                return pair[t % 2] if t else pair[3]

            def hidden_there(eng, g, t):
                eng.wait_ge(s["hid_ready"].sem, s["hid_ready"].upto(g, t + 2))

            def gated(eng, g, t):
                eng.wait_ge(s["proj_ready"].sem, s["proj_ready"].upto(g, t + 1))
                if t >= 2:
                    hidden_there(eng, g, t - 2)
                else:
                    eng.wait_ge(s["hid_ready"].sem, s["hid_ready"].upto(g, 0))
                eng.activation(act[:, t % 2], banks(t)[:, 0, :], ACT.Silu).then_inc(s["act_ready"].sem, 1)

            def hidden(eng, g, t):
                eng.wait_ge(s["act_ready"].sem, s["act_ready"].upto(g, t + 1))
                if t >= 3:
                    eng.wait_ge(s["hid_free"].sem, s["hid_free"].upto(g, t - 2))
                elif t == 1:
                    eng.wait_ge(s["hid_free"].sem, s["hid_free"].upto(g, 0))
                eng.tensor_tensor(hid[:, t % 3], act[:, t % 2], banks(t)[:, 1, :], ALU.mult)\
                   .then_inc(s["hid_ready"].sem, 1)
                if t == 0:
                    eng.wait_ge(s["hid_ready"].sem, s["hid_ready"].upto(g, 1))
                    eng.tensor_tensor(hid[:, 0], hid[:, 0], tok(rest_mask[:], g), ALU.mult)\
                       .then_inc(s["hid_ready"].sem, 1)

            def project(eng, g, t):
                if t == 0:
                    norm.there(eng, g)
                    eng.wait_ge(s["dev_ready"].sem, s["dev_ready"].upto(g, 1))
                elif t == 1:
                    eng.wait_ge(s["xv_ready"].sem, s["xv_ready"].upto(g, 1))
                elif t == MT + 1:
                    eng.wait_ge(s["xl_ready"].sem, s["xl_ready"].upto(g, 1))
                if t >= 3:
                    hidden_there(eng, g, t - 2)
                for w, to in ((w_gate, 0), (w_up, 1)):
                    mm = product(eng, banks(t)[:, to, :],
                                 [(w[:, c, t * P:(t + 1) * P], xe[:, (t - 1) // MT, c, :] if t else norm.xn[:, c, :])
                                  for c in range(FC)])
                mm.then_inc(s["proj_ready"].sem, 1)

            def down(eng, g, t):
                hidden_there(eng, g, t)
                if t == 0:
                    eng.wait_ge(s["x_done"].sem, s["x_done"].upto(g, 0))
                for m in range(FC):
                    mm = eng.matmul(bank[4 + m], w_down[:, t, m * P:(m + 1) * P], hid[:, t % 3], start=t == 0,
                                    stop=t == HTILES - 1)
                mm.then_inc(s["hid_free"].sem, 1)

            with nc.Block() as block:
                @block.sync
                def _(eng):
                    load_weights(eng, 3)

                @block.gpsimd
                def _(eng):
                    def masked(g, e, ready):
                        mask = tok(expert[:, e, :], g).unsqueeze(1).to_broadcast([P, FC, GT])
                        eng.tensor_tensor(xe[:, e], norm.xn[:], mask, ALU.mult).then_inc(ready.sem, 1)

                    def start():
                        norm.there(eng, 0)
                        masked(0, 0, s["xv_ready"])
                        masked(0, 1, s["xl_ready"])

                    def body(g, more):
                        if more:
                            norm.there(eng, g + 1)
                            eng.wait_ge(s["proj_ready"].sem, s["proj_ready"].upto(g, MT + 1))
                            masked(g + 1, 0, s["xv_ready"])
                            eng.wait_ge(s["proj_ready"].sem, s["proj_ready"].upto(g, HTILES))
                            masked(g + 1, 1, s["xl_ready"])
                    ahead_over_groups(eng, start, body)

                @block.scalar
                def _(eng):
                    def start():
                        norm.square(eng, 0)
                        norm.root(eng, 0)
                        gated(eng, 0, 0)

                    def body(g, more):
                        for t in range(1, HTILES):
                            gated(eng, g, t)
                            if t == 1 and more:
                                norm.square(eng, g + 1)
                                norm.root(eng, g + 1)
                        if more:
                            gated(eng, g + 1, 0)
                    ahead_over_groups(eng, start, body)

                @block.vector
                def _(eng):
                    def start():
                        norm.vector(eng, 0)
                        hidden(eng, 0, 0)

                    def body(g, more):
                        for t in range(1, HTILES):
                            hidden(eng, g, t)
                            if t == 3 and more:
                                eng.wait_ge(s["proj_ready"].sem, s["proj_ready"].upto(g, 1))
                                eng.wait_ge(s["xv_ready"].sem, s["xv_ready"].upto(g, 1))
                                eng.wait_ge(s["xl_ready"].sem, s["xl_ready"].upto(g, 1))
                                norm.vector(eng, g + 1)
                        if more:
                            hidden(eng, g + 1, 0)
                        residual(eng, g, (bank[4], bank[5]), s["hid_free"], HTILES)
                    ahead_over_groups(eng, start, body)

                @block.tensor
                def _(eng):
                    weights_there(eng, 2)

                    def start():
                        norm.tensor(eng, 0)
                        project(eng, 0, 0)

                    def body(g, more):
                        for t in range(1, HTILES):
                            project(eng, g, t)
                            down(eng, g, t - 1)
                            if t == 2 and more:
                                norm.tensor(eng, g + 1)
                        if more:
                            project(eng, g + 1, 0)
                        down(eng, g, HTILES - 1)
                    ahead_over_groups(eng, start, body)

    def media_attention():
        TILES = HEADS * HD1 // P
        VHALF = HEADS // 2
        with ExitStack() as own:
            norm = Norm(own, LNQ_G, LNQ_B, ahead=True)
            context = sb("context", [P, GT], F32, own)
            bias_row = sb("bias_row", [1, 2, GT], BF16, own)
            spare = weights_a[:, 4096:4096 + TILES * GT].rearrange("p (t n) -> p t n", t=TILES)
            q = [sb("q", [P, TILES, GT], F32, own)[:] for _ in range(2)]
            k = [sb("k", [P, TILES, GT], F32, own)[:], spare]
            val = sb("val", [P, 2, GROUP, HEADS, HD1 + 1], F32, own)
            jobs = [("k", t) for t in range(TILES)] + [("q", t) for t in range(TILES)] + \
                   [("v", n) for n in range(2 * GROUP)]
            for n, c in (("proj_ready", len(jobs)), ("proj_out_d", len(jobs) // 2), ("proj_out_a", len(jobs) // 2),
                         ("back_out", QUADS), ("out_ready", FC), ("x_done", FC), ("xl_ready", 1)):
                s[n].block(c)
            s["ctx_loaded"].block(1, amount=16)
            s["setup_p"].block(1, 1)

            def key_mask(eng, g, to, b):
                row = bias_row[0:1, g % 2, b * SEQ:(b + 1) * SEQ].unsqueeze(1).to_broadcast([1, QUAD, SEQ])
                eng.matmul(to, ones_row[:], row, start=True, stop=False, skip_group_check=True)

            def score(g, b, h):
                rows, cols = slice(HD1 * (h % 2), HD1 * (h % 2) + HD1), slice(b * SEQ, (b + 1) * SEQ)
                return q[g % 2][rows, h // 2, cols], k[g % 2][rows, h // 2, cols]

            def post(eng, u):
                g, (b, part) = u // QUADS, divmod(u % QUADS, HEADS // QUAD)
                eng.tensor_copy(q[g % 2][:, 2 * part:2 * part + 2, b * SEQ:(b + 1) * SEQ],
                                bank[4 + u % 2][:, 0:2 * P].rearrange("p (c n) -> p c n", c=2)).then_inc(s["back_out"].sem, 1)

            att = Attention(own, HD1, score, key_mask, lambda g, b, h: val[:, g % 2, b, h, :], 2, 1, post,
                            head=media_head)
            att.takes = 1

            def taken(eng, g, n):
                out_of = s["proj_out_d"] if n % 2 else s["proj_out_a"]
                eng.wait_ge(out_of.sem, out_of.upto(g, n // 2 + 1))

            def mean(eng, g):
                if g:
                    taken(eng, g - 1, len(jobs) - 2)
                    taken(eng, g - 1, len(jobs) - 1)
                norm.mean(eng, g)

            def project(eng, g, n):
                kind, t = jobs[n]
                if n < 2:
                    eng.wait_ge(s["dev_ready"].sem, s["dev_ready"].upto(g, 1))
                    eng.wait_ge(s["ctx_loaded"].sem, s["ctx_loaded"].upto(g, 1))
                elif n in (AFTER_OUTPUT, AFTER_OUTPUT + 1) and g >= 2:
                    eng.wait_ge(s["x_done"].sem, s["x_done"].upto(g - 2, n - AFTER_OUTPUT + 1))
                else:
                    taken(eng, g, n - 2)
                if kind == "q":
                    norm.there(eng, g)
                    f = [(w_q1[:, c, t * P:(t + 1) * P], norm.xn[:, c, :]) for c in range(FC)]
                elif kind == "k":
                    f = [(w_k1[:, t * P:(t + 1) * P], context[:])]
                else:
                    b, half = divmod(t, 2)
                    f = [(context[:, b * SEQ:(b + 1) * SEQ], w_v1[:, half * GT:(half + 1) * GT])]
                product(eng, bank[6 + n % 2], f).then_inc(s["proj_ready"].sem, 1)

            def output(eng, g, m, part):
                if part == 0:
                    if m == 0:
                        eng.wait_ge(s["back_out"].sem, s["back_out"].upto(g, QUADS))
                    if g + 2 < GROUPS:
                        taken(eng, g + 2, AFTER_OUTPUT - 2 + m)
                for t in range(part * TILES // 2, (part + 1) * TILES // 2):
                    mm = eng.matmul(bank[6 + m], w_o1[:, t, m * P:(m + 1) * P], q[g % 2][:, t, :], start=t == 0,
                                    stop=t == TILES - 1)
                if part:
                    mm.then_inc(s["out_ready"].sem, 1)

            AFTER_OUTPUT = 8
            slots = [(n, c) for n in range(2, 5) for c in range(3)][:AFTER_OUTPUT] + \
                    [(n, c) for n in range(9, 15) for c in range(3)][:len(jobs) - AFTER_OUTPUT]

            def pe_front(eng, g, at, slot):
                if (at, slot) == (0, 0):
                    mean(eng, g)
                elif (at, slot) == (1, 0):
                    norm.tensor(eng, g)
                elif (at, slot) in slots:
                    project(eng, g, slots.index((at, slot)))
                elif (at, slot) == (15, 2):
                    taken(eng, g, len(jobs) - 2)
                    taken(eng, g, len(jobs) - 1)
                    eng.wait_ge(s["xl_ready"].sem, s["xl_ready"].upto(g, 1))

            def pe_back(eng, g, at, slot):
                if 5 <= at <= 8 and slot == 0:
                    output(eng, g, (at - 5) // 2, (at - 5) % 2)

            def take(eng, g, n):
                kind, t = jobs[n]
                eng.wait_ge(s["proj_ready"].sem, s["proj_ready"].upto(g, n + 1))
                src = bank[6 + n % 2]
                if kind == "v":
                    b, half = divmod(t, 2)
                    to = val[:, g % 2, b, VHALF * half:VHALF * (half + 1), 0:HD1]
                    src = src.rearrange("p (h d) -> p h d", h=VHALF)
                else:
                    to = (q if kind == "q" else k)[g % 2][:, t, :]
                scale = HD1 ** -0.5 if kind == "q" else 1.0
                if n % 2:
                    eng.tensor_scalar(to, src, scale, None, ALU.mult).then_inc(s["proj_out_d"].sem, 1)
                else:
                    eng.activation(to, src, ACT.Copy, scale=scale).then_inc(s["proj_out_a"].sem, 1)

            def centre(eng, g):
                if g:
                    eng.wait_ge(s["proj_ready"].sem, s["proj_ready"].upto(g - 1, 2 * TILES))
                norm.centre(eng, g)

            def add(eng, g, m):
                eng.wait_ge(s["out_ready"].sem, s["out_ready"].upto(g, m + 1))
                xs = x_t[:, m, g * GT:(g + 1) * GT]
                eng.scalar_tensor_tensor(out=xs, in0=bank[6 + m], scalar=gates[:, 0:1], in1=xs, op0=ALU.mult,
                                         op1=ALU.add).then_inc(s["x_done"].sem, 1)

            def dve_front(eng, g, at, slot):
                if (at, slot) == (0, 2):
                    centre(eng, g)
                elif (at, slot) == (2, 2):
                    norm.reciprocal(eng, g)
                before = (at, slot - 1) if slot else (at - 1, 2)
                if before in slots and slots.index(before) % 2:
                    take(eng, g, slots.index(before))

            def dve_back(eng, g, at, slot):
                if at in (6, 8) and slot == 2:
                    add(eng, g, (at - 6) // 2)

            def act_front(eng, g, at, slot):
                if (at, slot) == (1, 0):
                    norm.square(eng, g)
                    norm.root(eng, g)
                for n, when in enumerate(slots):
                    if when[0] == at and slot == 0 and n % 2 == 0:
                        take(eng, g, n)

            with nc.Block() as block:
                @block.sync
                def _(eng):
                    for g in range(GROUPS):
                        if g:
                            eng.wait_ge(s["proj_ready"].sem, s["proj_ready"].upto(g - 1, len(jobs)))
                        eng.dma_start(context[:], a["ctx"][:, g * GT:(g + 1) * GT]).then_inc(s["ctx_loaded"].sem, 16)
                        if g == 0:
                            load_weights(eng, 4)

                @block.gpsimd
                def _(eng):
                    eng.memset(val[:], 1.0).then_inc(s["setup_p"].sem, 1)
                    for g in range(GROUPS):
                        if g >= 2:
                            att.wait(eng, "scores_ready", QUADS * (g - 1))
                        eng.tensor_copy(bias_row[:, g % 2], key_bias[:, g * GT:(g + 1) * GT])\
                           .then_inc(s["xl_ready"].sem, 1)
                        norm.pool(eng, g)

                @block.scalar
                def _(eng):
                    eng.wait_ge(s["setup_p"].sem, s["setup_p"].upto(0, 1))
                    first_front(eng, act_front)
                    att.scalar(eng, around(act_front))

                @block.vector
                def _(eng):
                    eng.wait_ge(s["setup_p"].sem, s["setup_p"].upto(0, 1))
                    first_front(eng, dve_front)
                    att.vector(eng, around(dve_front, dve_back))
                    for m in range(FC):
                        add(eng, GROUPS - 1, m)

                @block.tensor
                def _(eng):
                    weights_there(eng, 3)
                    first_front(eng, pe_front)
                    att.tensor(eng, around(pe_front, pe_back))
                    for m in range(FC):
                        for part in range(2):
                            output(eng, GROUPS - 1, m, part)

    def feed_forward():
        TILES = MLP1 // P
        with ExitStack() as own:
            norm = Norm(own, LNF_G, LNF_B, ahead=True, apart=True)
            hid = sb("hid", [P, 4, GT], F32, own)
            for n, k in (("proj_ready", TILES), ("hid_ready", TILES), ("hid_free", TILES), ("x_done", FC)):
                s[n].block(k)

            with nc.Block() as block:
                @block.sync
                def _(eng):
                    load_weights(eng, 5)

                @block.scalar
                def _(eng):
                    def start():
                        norm.square(eng, 0)
                        norm.root(eng, 0)

                    def body(g, more):
                        for t in range(TILES):
                            eng.wait_ge(s["proj_ready"].sem, s["proj_ready"].upto(g, t + 1))
                            eng.wait_ge(s["hid_free"].sem, s["hid_free"].upto(g, max(t - 3, 0)))
                            eng.activation(hid[:, t % 4], bank[t % 4], ACT.Gelu).then_inc(s["hid_ready"].sem, 1)
                            if t == 2 and more:
                                norm.square(eng, g + 1)
                                norm.root(eng, g + 1)
                    ahead_over_groups(eng, start, body)

                @block.vector
                def _(eng):
                    def start():
                        norm.centre(eng, 0)
                        norm.vector(eng, 0)

                    def body(g, more):
                        if more:
                            norm.centre(eng, g + 1)
                            norm.reciprocal(eng, g + 1)
                            norm.scaled(eng, g + 1)
                            eng.wait_ge(s["proj_ready"].sem, s["proj_ready"].upto(g, TILES))
                            norm.biased(eng, g + 1)
                        eng.wait_ge(s["hid_free"].sem, s["hid_free"].upto(g, TILES))
                        for m in range(FC):
                            xs = x_t[:, m, bass.ds(g * GT, GT)]
                            eng.scalar_tensor_tensor(out=xs, in0=bank[4 + m], scalar=gates[:, 1:2], in1=xs, op0=ALU.mult,
                                                     op1=ALU.add).then_inc(s["x_done"].sem, 1)
                    ahead_over_groups(eng, start, body)

                @block.tensor
                def _(eng):
                    weights_there(eng, 4)

                    def start():
                        norm.mean(eng, 0)
                        norm.tensor(eng, 0)

                    def body(g, more):
                        norm.there(eng, g)
                        for t in range(TILES + 2):
                            if t < TILES:
                                if t >= 4:
                                    eng.wait_ge(s["hid_ready"].sem, s["hid_ready"].upto(g, t - 3))
                                product(eng, bank[t % 4], [(w_ff1[:, c, t * P:(t + 1) * P], norm.xn[:, c, :])
                                                           for c in range(FC)]).then_inc(s["proj_ready"].sem, 1)
                            if t >= 2:
                                k = t - 2
                                eng.wait_ge(s["hid_ready"].sem, s["hid_ready"].upto(g, k + 1))
                                if k == 0:
                                    eng.wait_ge(s["x_done"].sem, s["x_done"].upto(g, 0))
                                for m in range(FC):
                                    mm = eng.matmul(bank[4 + m], w_ff2[:, k, m * P:(m + 1) * P], hid[:, k % 4],
                                                    start=k == 0, stop=k == TILES - 1)
                                mm.then_inc(s["hid_free"].sem, 1)
                            if more and t == 0:
                                norm.mean(eng, g + 1)
                            if more and t == 3:
                                norm.tensor(eng, g + 1)
                    ahead_over_groups(eng, start, body)

    def memory_fusion(layer):
        w_mem, w_g, b_g = fuse_w[layer]
        last = layer == 1
        with ExitStack() as own:
            context = sb("context_f", [P, GT], F32, own)
            xq = sb("xq", [P, FC, GT], F32, own)
            mem_t = sb("mem_t", [P, FC, GT], F32, own)
            mem = sb("mem", [P, GROUP, DIM], F32, own)
            p = sb("p_f", [P, GROUP, SEQ], F32, own)
            pn = sb("pn_f", [P, GROUP, SEQ], F32, own)
            pt = sb("pt_f", [P, GROUP, SEQ], F32, own)
            nmax = sb("nmax_f", [P, GROUP], F32, own)
            sums = sb("sums_f", [P, GROUP], F32, own)
            recip = sb("recip_f", [P, GROUP], F32, own)
            mix = sb("mix", [P, FC, GT], F32, own)
            gate = sb("gate_f", [P, FC, GT], F32, own)
            fused = sb("fused", [P, FC, GT], F32, own)
            half_b = sb("half_b", [P, FC], F32, own)
            norm = Norm(own, NORM2 + layer, src=fused)
            for n, k in (("memt_ready", FC), ("mem_out", FC + GROUP), ("v_ready", GROUP), ("scores_ready", 1),
                         ("max_ready", 1), ("p_ready", GROUP), ("recip_ready", 1), ("norm_ready", 1), ("turned_ready", 1),
                         ("pt_ready", 1), ("ctx_ready", FC), ("mix_ready", FC), ("proj_ready", FC), ("act_ready", FC),
                         ("res_ready", 3 * FC), ("x_done", FC), ("rot_ready", 1)):
                s[n].block(k)
            s["ctx_loaded"].block(1, amount=16)
            s["bias_half"].block(1, 1)

            with nc.Block() as block:
                @block.sync
                def _(eng):
                    if not last:
                        load_weights(eng, 6)

                    def body(g, first):
                        group_start(eng, g, first)
                        eng.dma_start(context[:], tok(a["ctx"], g)).then_inc(s["ctx_loaded"].sem, 16)
                    over_groups(eng, body)

                @block.gpsimd
                def _(eng):
                    if last:
                        for g in range(GROUPS):
                            eng.wait_ge(s["x_done"].sem, s["x_done"].upto(g, FC))
                            eng.dma_start(out[:, :, g * GT:(g + 1) * GT], x_t[:, :, g * GT:(g + 1) * GT])\
                               .then_inc(s["stores"].sem, 16)
                        eng.wait_ge(s["stores"].sem, 16 * GROUPS)

                @block.scalar
                def _(eng):
                    weights_there(eng, 5 + layer)
                    eng.activation(half_b[:], b_g, ACT.Copy, scale=0.5).then_inc(s["bias_half"].sem, 1)
                    eng.wait_ge(s["bias_half"].sem, s["bias_half"].upto(0, 1))

                    def body(g, first):
                        group_start(eng, g, first)
                        eng.activation(xq[:], tok(x_t[:], g), ACT.Copy, scale=DIM ** -0.5)\
                           .then_inc(s["rot_ready"].sem, 1)
                        for c in range(FC):
                            eng.wait_ge(s["memt_ready"].sem, s["memt_ready"].upto(g, c + 1))
                            eng.activation(mem_t[:, c, :], bank[c], ACT.Copy).then_inc(s["mem_out"].sem, 1)
                        for b in range(GROUP):
                            eng.wait_ge(s["v_ready"].sem, s["v_ready"].upto(g, b + 1))
                            eng.activation(mem[:, b, :], bank[2 + b][:, 0:DIM], ACT.Copy).then_inc(s["mem_out"].sem, 1)
                        eng.wait_ge(s["max_ready"].sem, s["max_ready"].upto(g, 1))
                        for b in range(GROUP):
                            eng.activation(p[:, b, :], bank[6][:, b * SEQ:(b + 1) * SEQ], ACT.Exp, bias=nmax[:, b:b + 1],
                                           accum_out=sums[:, b:b + 1]).then_inc(s["p_ready"].sem, 1)
                        for m in range(FC):
                            eng.wait_ge(s["proj_ready"].sem, s["proj_ready"].upto(g, m + 1))
                            eng.activation(gate[:, m, :], bank[4 + m], ACT.Tanh, bias=half_b[:, m:m + 1], scale=0.5)\
                               .then_inc(s["act_ready"].sem, 1)
                        eng.wait_ge(s["res_ready"].sem, s["res_ready"].upto(g, 3 * FC))
                        norm.square(eng, g)
                        norm.root(eng, g)
                    over_groups(eng, body)

                @block.vector
                def _(eng):
                    def body(g, first):
                        group_start(eng, g, first)
                        eng.wait_ge(s["scores_ready"].sem, s["scores_ready"].upto(g, 1))
                        eng.tensor_reduce(nmax[:], bank[6].rearrange("p (b k) -> p b k", b=GROUP), AX_X, ALU.max,
                                          negate=True).then_inc(s["max_ready"].sem, 1)
                        eng.wait_ge(s["p_ready"].sem, s["p_ready"].upto(g, GROUP))
                        eng.reciprocal(recip[:], sums[:]).then_inc(s["recip_ready"].sem, 1)
                        eng.wait_ge(s["recip_ready"].sem, s["recip_ready"].upto(g, 1))
                        eng.tensor_tensor(pn[:], p[:], recip[:].unsqueeze(2).to_broadcast([P, GROUP, SEQ]), ALU.mult)\
                           .then_inc(s["norm_ready"].sem, 1)
                        eng.wait_ge(s["turned_ready"].sem, s["turned_ready"].upto(g, 1))
                        eng.tensor_copy(pt[:].rearrange("p b k -> p (b k)"), bank[7]).then_inc(s["pt_ready"].sem, 1)
                        for m in range(FC):
                            eng.wait_ge(s["ctx_ready"].sem, s["ctx_ready"].upto(g, m + 1))
                            eng.tensor_copy(mix[:, m, :], bank[m]).then_inc(s["mix_ready"].sem, 1)
                        r = s["res_ready"]
                        for m in range(FC):
                            eng.wait_ge(s["act_ready"].sem, s["act_ready"].upto(g, m + 1))
                            eng.tensor_scalar(gate[:, m, :], gate[:, m, :], 0.5, 0.5, ALU.mult, ALU.add).then_inc(r.sem, 1)
                            eng.wait_ge(r.sem, r.upto(g, 3 * m + 1))
                            eng.tensor_tensor(gate[:, m, :], gate[:, m, :], mix[:, m, :], ALU.mult).then_inc(r.sem, 1)
                            eng.wait_ge(r.sem, r.upto(g, 3 * m + 2))
                            eng.tensor_tensor(fused[:, m, :], gate[:, m, :], x_t[:, m, bass.ds(g * GT, GT)], ALU.add)\
                               .then_inc(r.sem, 1)
                        eng.wait_ge(s["dev_ready"].sem, s["dev_ready"].upto(g, 1))
                        eng.reciprocal(norm.rstd[:], norm.dev[:]).then_inc(s["rstd_ready"].sem, 1)
                        eng.wait_ge(s["rstd_ready"].sem, s["rstd_ready"].upto(g, 1))
                        for m in range(FC):
                            eng.scalar_tensor_tensor(out=x_t[:, m, bass.ds(g * GT, GT)], in0=fused[:, m, :],
                                                     scalar=scales[:, norm.scale, m:m + 1], in1=norm.rstd[:], op0=ALU.mult,
                                                     op1=ALU.mult).then_inc(s["x_done"].sem, 1)
                    over_groups(eng, body)

                @block.tensor
                def _(eng):
                    weights_there(eng, 5 + layer)

                    def body(g, first):
                        group_start(eng, g, first)
                        eng.wait_ge(s["ctx_loaded"].sem, s["ctx_loaded"].upto(g, 1))
                        for c in range(FC):
                            product(eng, bank[c], [(w_mem[:, c * P:(c + 1) * P], context[:])])\
                                .then_inc(s["memt_ready"].sem, 1)
                        for b in range(GROUP):
                            product(eng, bank[2 + b][:, 0:DIM], [(context[:, b * SEQ:(b + 1) * SEQ], w_mem)])\
                                .then_inc(s["v_ready"].sem, 1)
                        eng.wait_ge(s["mem_out"].sem, s["mem_out"].upto(g, FC))
                        eng.wait_ge(s["rot_ready"].sem, s["rot_ready"].upto(g, 1))
                        for b in range(GROUP):
                            cols = slice(b * SEQ, (b + 1) * SEQ)
                            mm = product(eng, bank[6][:, cols], [(xq[:, c, cols], mem_t[:, c, cols]) for c in range(FC)])
                        mm.then_inc(s["scores_ready"].sem, 1)
                        eng.wait_ge(s["norm_ready"].sem, s["norm_ready"].upto(g, 1))
                        for b in range(GROUP):
                            mm = eng.transpose(bank[7][:, b * SEQ:(b + 1) * SEQ], pn[:, b, :], ident[:])
                        mm.then_inc(s["turned_ready"].sem, 1)
                        eng.wait_ge(s["pt_ready"].sem, s["pt_ready"].upto(g, 1))
                        eng.wait_ge(s["mem_out"].sem, s["mem_out"].upto(g, FC + GROUP))
                        for m in range(FC):
                            for b in range(GROUP):
                                mm = eng.matmul(bank[m][:, b * SEQ:(b + 1) * SEQ], mem[:, b, m * P:(m + 1) * P],
                                                pt[:, b, :], start=True, stop=True)
                            mm.then_inc(s["ctx_ready"].sem, 1)
                        eng.wait_ge(s["mix_ready"].sem, s["mix_ready"].upto(g, FC))
                        for m in range(FC):
                            product(eng, bank[4 + m],
                                    [(w_g[:, c, m * P:(m + 1) * P], x_t[:, c, bass.ds(g * GT, GT)]) for c in range(FC)] +
                                    [(w_g[:, FC + c, m * P:(m + 1) * P], mix[:, c, :]) for c in range(FC)])\
                                .then_inc(s["proj_ready"].sem, 1)
                        norm.tensor(eng, g)
                    over_groups(eng, body)


    self_attention()

    cross_attention()
    expert_mlp()
    media_attention()
    feed_forward()
    memory_fusion(0)
    memory_fusion(1)


def _laid_out(i):
    f = np.float32

    def chunks(w):
        return np.ascontiguousarray(w)

    def by_dim(w, hd):
        return w.reshape(w.shape[0], HEADS, hd).transpose(0, 2, 1).reshape(w.shape[0], HEADS * hd)

    def by_feature(v):
        return v.reshape(FC, P).T

    def hidden_columns(v, l):
        rest = np.zeros((v.shape[0], P), v.dtype)
        rest[:, 0:MREST] = v[:, MT * P:]
        rest[:, REST_AT:REST_AT + MREST] = l[:, MT * P:]
        return np.concatenate([rest, v[:, :MT * P], l[:, :MT * P]], axis=1)

    o = {}
    o["x"] = i["x"].reshape(TOKENS, FC, P).transpose(2, 1, 0)
    o["ctx"] = i["ctx_1024"].reshape(TOKENS, CTX).T
    o["tt"] = i["mask_BxS_ik0"].reshape(TOKENS)
    o["keys"] = i["mask_BxS2_bk0"].reshape(1, TOKENS).view(np.int32)
    o["pos"] = i["pos_1xS"].reshape(SEQ)
    for e in "vl":
        qkv = i[f"L0_xattn_{e}_qkv"]
        o[f"{e}_qk"] = np.concatenate([by_dim(qkv[:, :DIM], HD0), by_dim(qkv[:, DIM:2 * DIM], HD0)], axis=1)
        o[f"{e}_v"] = qkv[:, 2 * DIM:]
        o[f"{e}_dense"] = i[f"L0_xattn_{e}_dense"]
    o["cq"] = by_dim(i["L0_xattn_cq_w"], HD0C)
    o["ck"] = by_dim(i["L0_xattn_ckv_w"][:, :P], HD0C)
    o["cv"] = i["L0_xattn_ckv_w"][:, P:]
    o["cdense"] = i["L0_xattn_cdense_w"]
    o["gate0"] = hidden_columns(i["L0_xattn_v_gate"], i["L0_xattn_l_gate"])
    o["up0"] = hidden_columns(i["L0_xattn_v_up"], i["L0_xattn_l_up"])
    o["down0"] = hidden_columns(i["L0_xattn_v_down"].T, i["L0_xattn_l_down"].T).T
    order = [media_head(q, h) for q in range(HEADS // QUAD) for h in range(QUAD)]
    o["wq"] = i["L1_xattn_Wq"]
    o["wo"] = i["L1_xattn_Wo"].reshape(HEADS, HD1, DIM)[order].reshape(HEADS * HD1, DIM)
    o["wk"], o["wv"] = i["L1_xattn_Wkv"][:, :HEADS * HD1], i["L1_xattn_Wkv"][:, HEADS * HD1:]
    o["w1"], o["w2"] = i["L1_xattn_W1"], i["L1_xattn_W2"]
    for n in "23":
        o[f"mem{n}"] = i[f"L{n}_xattn_W_mem"].T
        o[f"g{n}"] = i[f"L{n}_xattn_W_gate"].T
        o[f"b{n}"] = by_feature(i[f"L{n}_xattn_b_gate"])
    o["scales"] = np.stack([by_feature(i[n]) for n in (
        "L0_xattn_ln_in_w", "L0_xattn_ln_post_cross_w", "L0_xattn_ln_post_attn_w", "L1_xattn_ln_q_g", "L1_xattn_ln_q_b",
        "L1_xattn_ln_ff_g", "L1_xattn_ln_ff_b", "L2_xattn_norm_w", "L3_xattn_norm_w")], axis=1)
    o["gates"] = np.concatenate([i["L1_xattn_attn_gate"], i["L1_xattn_ff_gate"]])

    inv = (1.0 / ROPE_BASE ** (np.arange(0, HD0, 2, dtype=f) / f(HD0))).astype(f)
    angle = np.outer(np.arange(SEQ, dtype=f), inv).astype(f)
    o["consts"] = np.concatenate([np.repeat(np.cos(angle), HEADS, axis=1), np.repeat(np.sin(angle), HEADS, axis=1),
                                  np.arange(P, dtype=f)[:, None]], axis=1).astype(f)
    o["ident"] = np.eye(P, dtype=f)
    above = np.arange(P)[None, :] > np.arange(P)[:, None]
    o["causal"] = np.where(above, MASKED, 0.0).astype(mybir.dt.np(BF16))
    return {n: np.ascontiguousarray(v) for n, v in o.items()}


def kernel(**inputs):
    import concourse.bacc as bacc
    from concourse.bass_utils import run_bass_kernel_spmd

    arrays = _laid_out({n: np.asarray(v) for n, v in inputs.items()})
    nc = bacc.Bacc("TRN2", target_bir_lowering=False, num_devices=1)
    aps = {n: nc.dram_tensor(f"in_{n}", v.shape, mybir.dt.from_np(v.dtype), kind="ExternalInput").ap()
           for n, v in arrays.items()}
    out = nc.dram_tensor("out_x", (P, FC, TOKENS), F32, kind="ExternalOutput").ap()
    build(nc, aps, out)
    got = run_bass_kernel_spmd(nc, [{f"in_{n}": v for n, v in arrays.items()}], core_ids=[0]).results[0]["out_x"]
    return got.transpose(2, 1, 0).reshape(BATCHES, SEQ, DIM)
```

```python
from contextlib import ExitStack

import numpy as np

import concourse.bass as bass
from concourse import mybir

P = 128
BATCHES, SEQ, DIM, CTX = 16, 128, 256, 128
TOKENS = BATCHES * SEQ
GROUP = 4
GROUPS = BATCHES // GROUP
GT = GROUP * SEQ
FC = DIM // P
HEADS = 16
QUAD = 4
QUADS = GROUP * HEADS // QUAD
HD0, HD0C, HD1 = 16, 8, 64
MLP0, MLP1 = 688, 1024
MT = MLP0 // P
MREST = MLP0 - MT * P
HTILES = 2 * MT + 1
REST_AT = 64
HALF = HD0 // 2
SLOTS = 6
SLOT_PARTS = ((0, 0), (0, 1), (0, 2), (1, 0), (1, 1), (2, 0))
ROPE_BASE = 10000.0
EPS_RMS, EPS_LN = 1e-6, 1e-5
MASKED = -3.38e38

F32, F32R, BF16, I32, U8 = (mybir.dt.float32, mybir.dt.float32r, mybir.dt.bfloat16, mybir.dt.int32,
                            mybir.dt.uint8)
ALU = mybir.AluOpType
ACT = mybir.ActivationFunctionType
AX_X = mybir.AxisListType.X


def media_head(q, i):
    return 2 * QUAD * (q // 2) + q % 2 + 2 * i


class Signal:

    def __init__(self, sem):
        self.sem, self.start, self.total, self.per_group = sem, 0, 0, 0

    def block(self, per_group, groups=GROUPS, amount=1):
        self.start += self.total
        self.per_group, self.amount = per_group * amount, amount
        self.total = self.per_group * groups

    def upto(self, g, n):
        return g * self.per_group + (self.start + n * self.amount)


def over_groups(eng, body):
    body(0, True)
    with eng.Fori(1, GROUPS) as g:
        body(g, False)


def ahead_over_groups(eng, start, body):
    start()
    with eng.Fori(0, GROUPS - 1) as g:
        body(g, True)
    body(GROUPS - 1, False)


def build(nc, a, out):
    with ExitStack() as ctx:
        persistent(nc, ctx, a, out)


def persistent(nc, ctx, a, out):
    count = [0]

    def sb(name, shape, dt=F32, on=ctx):
        count[0] += 1
        return on.enter_context(nc.sbuf_tensor(f"{name}_{count[0]}", shape, dt))

    def signal(name):
        return Signal(ctx.enter_context(nc.semaphore(name)))

    x_t = sb("x_t", [P, FC, TOKENS])
    expert = sb("expert", [P, 2, TOKENS], BF16)
    rest_mask = sb("rest_mask", [P, TOKENS], BF16)
    keys = sb("keys", [1, TOKENS // 4], I32)
    ident = sb("ident", [P, P])
    ident_b = sb("ident_b", [P, P], BF16)
    causal = sb("causal", [P, P], BF16)
    ones_row = sb("ones_row", [1, P], BF16)
    mean_w = sb("mean_w", [P, P])
    scales = sb("scales", [P, 9, FC])
    eps_cols = sb("eps_cols", [P, 2])
    norm_xn = sb("norm_xn", [P, FC, GT])
    norm_sq = sb("norm_sq", [P, FC, GT])
    norm_dev = sb("norm_dev", [P, GT])
    norm_rstd = sb("norm_rstd", [P, GT])
    gates = sb("gates", [P, 2])
    weights_a = sb("weights_a", [P, 8448])
    weights_b = sb("weights_b", [P, 6144])
    pair = [ctx.enter_context(nc.psum_tensor(f"pair{i}", [P, 2, GT], F32)) for i in range(4)]
    bank = [pair[i // 2][:, i % 2, :] for i in range(8)]
    s_pair, t_pair, c_pair, g_pair = pair

    (W_LN_IN, W_LN_CROSS, W_LN_MLP, LNQ_G, LNQ_B, LNF_G, LNF_B, NORM2, NORM3) = range(9)

    names = """loaded x_first x_rest stores setup_d setup_a setup_p
        xv_ready xl_ready
        proj_ready proj_out_d proj_out_a rot_part rot_ready hi_ready res_ready mid_ready lo_ready
        stacked v_ready v_out_a v_out_d ctx_loaded
        scores_ready max_ready p_ready turned_ready pt_ready ctx_ready recip_ready norm_ready
        back_ready back_out mix_ready out_ready x_done act_ready hid_ready hid_free
        memt_ready mem_out bias_half xnh_ready xnl_ready high_ready low_ready wh_ready wl_ready""".split()
    s = {n: signal(n) for n in names}
    w_ready = [signal(f"w_ready{i}") for i in range(7)]

    def wa(at, *shape):
        n = int(np.prod(shape))
        v = weights_a[:, at:at + n]
        return split_free(v, shape), at + n

    def wb(at, *shape):
        n = int(np.prod(shape))
        v = weights_b[:, at:at + n]
        return split_free(v, shape), at + n

    def split_free(v, shape):
        if len(shape) == 1:
            return v
        if len(shape) == 2:
            return v.rearrange("p (a b) -> p a b", b=shape[1])
        return v.rearrange("p (a b c) -> p a b c", b=shape[1], c=shape[2])

    at = 0
    w_qk, at = wa(at, 2, FC, 2 * DIM)
    w_v, at = wa(at, 2, FC, DIM)
    w_dense, at = wa(at, 2, FC, DIM)
    at = 0
    w_cq, at = wb(at, FC, P)
    w_ck, at = wb(at, P)
    w_cv, at = wb(at, P)
    w_cdense, at = wb(at, DIM)
    at = 0
    w_gate, at = wa(at, FC, HTILES * P)
    w_up, at = wa(at, FC, HTILES * P)
    w_down, at = wa(at, HTILES, DIM)
    at = 0
    w_q1, at = wb(at, FC, HEADS * HD1)
    w_k1, at = wb(at, HEADS * HD1)
    w_v1, at = wb(at, HEADS * HD1)
    w_o1, at = wb(at, 8, DIM)
    assert at <= 6144
    at = 0
    w_ff1, at = wa(at, FC, MLP1)
    w_ff2, at = wa(at, 8, DIM)
    fuse_w = []
    for take in (wb, wa):
        w_mem, at = take(0, DIM)
        w_g, at = take(at, 4, DIM)
        b_g, at = take(at, FC)
        fuse_w.append((w_mem, w_g, b_g))

    loads = [
        [(w_qk[:, 0], a["v_qk"].rearrange("(c p) n -> p c n", p=P)), (w_qk[:, 1], a["l_qk"].rearrange("(c p) n -> p c n", p=P)),
         (w_v[:, 0], a["v_v"].rearrange("(c p) n -> p c n", p=P)), (w_v[:, 1], a["l_v"].rearrange("(c p) n -> p c n", p=P)),
         (w_dense[:, 0], a["v_dense"].rearrange("(c p) n -> p c n", p=P)),
         (w_dense[:, 1], a["l_dense"].rearrange("(c p) n -> p c n", p=P))],
        [(w_cq, a["cq"].rearrange("(c p) n -> p c n", p=P)), (w_ck, a["ck"]), (w_cv, a["cv"]), (w_cdense, a["cdense"])],
        [(w_gate, a["gate0"].rearrange("(c p) n -> p c n", p=P)), (w_up, a["up0"].rearrange("(c p) n -> p c n", p=P)),
         (w_down, a["down0"].rearrange("(c p) n -> p c n", p=P))],
        [(w_q1, a["wq"].rearrange("(c p) n -> p c n", p=P)), (w_k1, a["wk"]), (w_v1, a["wv"]),
         (w_o1, a["wo"].rearrange("(c p) n -> p c n", p=P))],
        [(w_ff1, a["w1"].rearrange("(c p) n -> p c n", p=P)), (w_ff2, a["w2"].rearrange("(c p) n -> p c n", p=P))],
        [(fuse_w[0][0], a["mem2"]), (fuse_w[0][1], a["g2"].rearrange("(c p) n -> p c n", p=P)), (fuse_w[0][2], a["b2"])],
        [(fuse_w[1][0], a["mem3"]), (fuse_w[1][1], a["g3"].rearrange("(c p) n -> p c n", p=P)), (fuse_w[1][2], a["b3"])],
    ]
    for w, some in zip(w_ready, loads):
        w.block(len(some), groups=1, amount=16)

    def load_weights(eng, n):
        for dst, src in loads[n]:
            eng.dma_start(dst, src).then_inc(w_ready[n].sem, 16)

    def weights_there(eng, n):
        eng.wait_ge(w_ready[n].sem, w_ready[n].total)

    def tok(view, g):
        return view[..., bass.ds(g * GT, GT)]

    class Norm:

        def __init__(self, scale, bias=None, src=None, banks=(6, 7), ahead=False, tight=False, groups=GROUPS):
            self.scale, self.bias, self.src, self.ahead = scale, bias, src, ahead
            self.eps_col = eps_cols[:, 0:1] if bias is None else eps_cols[:, 1:2]
            self.mean_bank, self.square_bank = bank[banks[0]], bank[banks[1]]
            self.tight = tight
            self.xn, self.dev = norm_xn, norm_dev
            self.sq = norm_xn if tight else norm_sq
            self.rstd = norm_dev if tight else norm_rstd

            def own_signal(name, per_group):
                sig = signal(f"{name}_{scale}")
                sig.block(per_group, groups)
                return sig
            self.sq_ready = own_signal("sq_ready", 1)
            self.mean_ready = own_signal("mean_ready", 1 if bias is None else 2)
            self.centre_ready = own_signal("centre_ready", FC) if bias is not None else None
            self.dev_ready = own_signal("dev_ready", 1)
            self.rstd_ready = own_signal("rstd_ready", 1)
            self.xn_ready = own_signal("xn_ready", FC if bias is None else 2 * FC)

        def x(self, g):
            return tok(x_t[:], g) if self.src is None else self.src[:]

        def square(self, eng, g):
            if self.bias is None:
                eng.activation(self.sq[:], self.x(g), ACT.Square).then_inc(self.sq_ready.sem, 1)
            else:
                eng.wait_ge(self.centre_ready.sem, self.centre_ready.upto(g, FC))
                eng.activation(self.sq[:], self.xn[:], ACT.Square).then_inc(self.sq_ready.sem, 1)

        def root(self, eng, g):
            n = self.mean_ready.per_group
            eng.wait_ge(self.mean_ready.sem, self.mean_ready.upto(g, n))
            used = self.xn_ready if self.tight else self.rstd_ready
            if self.ahead:
                eng.wait_ge(used.sem, used.upto(g, 0))
            eng.activation(self.dev[:], self.square_bank, ACT.Sqrt, bias=self.eps_col).then_inc(self.dev_ready.sem, 1)

        def inverse_root(self, eng, g):
            n = self.mean_ready.per_group
            eng.wait_ge(self.mean_ready.sem, self.mean_ready.upto(g, n))
            if g:
                eng.wait_ge(self.xn_ready.sem, self.xn_ready.upto(g, 0))
            eng.activation(self.dev[:], self.square_bank, ACT.Ln, bias=self.eps_col).then_inc(self.dev_ready.sem, 1)
            eng.wait_ge(self.dev_ready.sem, self.dev_ready.upto(g, 1))
            eng.activation(self.rstd[:], self.dev[:], ACT.Exp, scale=-0.5).then_inc(self.rstd_ready.sem, 1)

        def mean(self, eng, g):
            for c in range(FC):
                mm = eng.matmul(self.mean_bank, mean_w[:], x_t[:, c, bass.ds(g * GT, GT)], start=c == 0, stop=c == FC - 1)
            mm.then_inc(self.mean_ready.sem, 1)

        def tensor(self, eng, g):
            eng.wait_ge(self.sq_ready.sem, self.sq_ready.upto(g, 1))
            for c in range(FC):
                mm = eng.matmul(self.square_bank, mean_w[:], self.sq[:, c, :], start=c == 0, stop=c == FC - 1)
            mm.then_inc(self.mean_ready.sem, 1)

        def centre(self, eng, g):
            eng.wait_ge(self.mean_ready.sem, self.mean_ready.upto(g, 1))
            for c in range(FC):
                eng.tensor_tensor(self.xn[:, c, :], x_t[:, c, bass.ds(g * GT, GT)], self.mean_bank,
                                  ALU.subtract).then_inc(self.centre_ready.sem, 1)
            eng.wait_ge(self.centre_ready.sem, self.centre_ready.upto(g, FC))

        def reciprocal(self, eng, g):
            eng.wait_ge(self.dev_ready.sem, self.dev_ready.upto(g, 1))
            eng.reciprocal(self.rstd[:], self.dev[:]).then_inc(self.rstd_ready.sem, 1)

        def scaled(self, eng, g):
            eng.wait_ge(self.rstd_ready.sem, self.rstd_ready.upto(g, 1))
            for c in range(FC):
                src = self.xn[:, c, :] if self.bias is not None else self.x(g)[:, c]
                eng.scalar_tensor_tensor(out=self.xn[:, c, :], in0=src, scalar=scales[:, self.scale, c:c + 1],
                                         in1=self.rstd[:], op0=ALU.mult, op1=ALU.mult).then_inc(self.xn_ready.sem, 1)

        def biased(self, eng, g):
            for c in range(FC):
                eng.wait_ge(self.xn_ready.sem, self.xn_ready.upto(g, c + 1))
                eng.tensor_scalar(self.xn[:, c, :], self.xn[:, c, :], scales[:, self.bias, c:c + 1], None,
                                  ALU.add).then_inc(self.xn_ready.sem, 1)

        def pool(self, eng, g):
            eng.wait_ge(self.rstd_ready.sem, self.rstd_ready.upto(g, 1))
            for c in range(FC):
                eng.tensor_tensor(self.xn[:, c, :], self.xn[:, c, :], self.rstd[:], ALU.mult).then_inc(self.xn_ready.sem, 1)
            for c in range(FC):
                eng.wait_ge(self.xn_ready.sem, self.xn_ready.upto(g, c + 1))
                eng.tensor_scalar(self.xn[:, c, :], self.xn[:, c, :], scales[:, self.scale, c:c + 1],
                                  scales[:, self.bias, c:c + 1], ALU.mult, ALU.add).then_inc(self.xn_ready.sem, 1)

        def vector(self, eng, g):
            self.reciprocal(eng, g)
            self.scaled(eng, g)
            if self.bias is not None:
                self.biased(eng, g)

        def there(self, eng, g):
            eng.wait_ge(self.xn_ready.sem, self.xn_ready.upto(g, self.xn_ready.per_group))

    def product(eng, to, factors):
        for n, (w, x) in enumerate(factors):
            mm = eng.matmul(to, w, x, start=n == 0, stop=n == len(factors) - 1)
        return mm

    def split_product(eng, to, factors, start=True, stop=True):
        passes = [(w[a], x[b]) for w, x in factors for a, b in ((0, 0), (0, 1), (1, 0))]
        for n, (w, x) in enumerate(passes):
            mm = eng.matmul(to, w, x, start=start and n == 0, stop=stop and n == len(passes) - 1)
        return mm

    def no_bias(eng, g, to, b):
        pass

    class Attention:

        def __init__(self, own, score, bias, value, unit, place, add, post, head=None):
            self.head = head or (lambda q, i: q * QUAD + i)
            self.score, self.bias, self.value, self.post = score, bias, value, post
            self.unit, self.place, self.add = unit, place, add
            self.quads = GROUPS * QUADS
            self.units = self.quads // self.unit
            self.p = sb("p", [P, 3, QUAD, SEQ], F32, own)
            self.pt = sb("pt", [P, 3, QUAD, SEQ], F32, own)
            self.nmax = sb("nmax", [P, 2, QUAD], F32, own)
            self.sums = sb("sums", [P, 3, QUAD], F32, own)
            self.recip = sb("recip", [P, 3, QUAD], F32, own)
            for n in ("scores_ready", "max_ready", "p_ready", "recip_ready", "norm_ready", "turned_ready", "pt_ready", "ctx_ready"):
                s[n].block(self.quads, 1)

        def wait(self, eng, name, n):
            eng.wait_ge(s[name].sem, s[name].upto(0, n))

        def where(self, n):
            return n // QUADS, n % QUADS // (HEADS // QUAD), n % (HEADS // QUAD)

        def tensor(self, eng, between):
            for n in range(self.quads + 4):
                if n < self.quads:
                    if n >= 2:
                        self.wait(eng, "p_ready", n - 1)
                    g, b, q = self.where(n)
                    self.bias(eng, g, s_pair[:, n % 2, :], b)
                    for h in range(QUAD):
                        w, x = self.score(g, b, self.head(q, h))
                        mm = eng.matmul(s_pair[:, n % 2, h * SEQ:(h + 1) * SEQ], w, x, start=self.bias is no_bias,
                                        stop=True, skip_group_check=True)
                    mm.then_inc(s["scores_ready"].sem, 1)
                between(eng, n, 0)
                m = n - 4
                if m >= 0:
                    self.wait(eng, "pt_ready", m + 1)
                    u, part = divmod(m, self.unit)
                    if part == 0 and u >= 2:
                        eng.wait_ge(s["back_out"].sem, s["back_out"].upto(0, u - 1))
                    g, b, q = self.where(m)
                    for h in range(QUAD):
                        mm = eng.matmul(self.place(bank[4 + u % 2], m, h), self.value(g, b, q, h), self.pt[:, m % 3, h, :],
                                        start=h == 0 or not self.add, stop=h == QUAD - 1 or not self.add,
                                        skip_group_check=True)
                    mm.then_inc(s["ctx_ready"].sem, 1)
                between(eng, n, 1)
                m = n - 2
                if 0 <= m < self.quads:
                    self.wait(eng, "norm_ready", m + 1)
                    if m >= 2:
                        self.wait(eng, "pt_ready", m - 1)
                    for h in range(QUAD):
                        mm = eng.transpose(t_pair[:, m % 2, h * SEQ:(h + 1) * SEQ], self.p[:, m % 3, h, :], ident[:])
                    mm.then_inc(s["turned_ready"].sem, 1)
                between(eng, n, 2)

        def scalar(self, eng, between):
            for n in range(self.quads + 4):
                if n < self.quads:
                    self.wait(eng, "max_ready", n + 1)
                    if n >= 3:
                        self.wait(eng, "turned_ready", n - 2)
                    for h in range(QUAD):
                        e = eng.activation(self.p[:, n % 3, h, :], s_pair[:, n % 2, h * SEQ:(h + 1) * SEQ], ACT.Exp,
                                           bias=self.nmax[:, n % 2, h:h + 1], accum_out=self.sums[:, n % 3, h:h + 1])
                    e.then_inc(s["p_ready"].sem, 1)
                between(eng, n, 0)

        def pool(self, eng, between):
            for n in range(self.quads + 1):
                m = n - 1
                if m >= 0:
                    self.wait(eng, "recip_ready", m + 1)
                    eng.tensor_tensor(self.p[:, m % 3], self.p[:, m % 3],
                                      self.recip[:, m % 3].unsqueeze(2).to_broadcast([P, QUAD, SEQ]), ALU.mult)\
                       .then_inc(s["norm_ready"].sem, 1)
                between(eng, n, 0)

        def vector(self, eng, between):
            for n in range(self.quads + 4):
                if n < self.quads:
                    self.wait(eng, "scores_ready", n + 1)
                    if n >= 2:
                        self.wait(eng, "p_ready", n - 1)
                    eng.tensor_reduce(self.nmax[:, n % 2, :], s_pair[:, n % 2, :].rearrange("p (h k) -> p h k", h=QUAD),
                                      AX_X, ALU.max, negate=True).then_inc(s["max_ready"].sem, 1)
                m = n - 1
                if 0 <= m < self.quads:
                    self.wait(eng, "p_ready", m + 1)
                    if m >= 3:
                        self.wait(eng, "norm_ready", m - 2)
                    eng.reciprocal(self.recip[:, m % 3], self.sums[:, m % 3]).then_inc(s["recip_ready"].sem, 1)
                between(eng, n, 0)
                m = n - 4
                if m >= 0 and (m + 1) % self.unit == 0:
                    self.wait(eng, "ctx_ready", m + 1)
                    self.post(eng, m // self.unit)
                between(eng, n, 1)
                m = n - 2
                if 0 <= m < self.quads:
                    self.wait(eng, "turned_ready", m + 1)
                    if m >= 3:
                        self.wait(eng, "ctx_ready", m - 2)
                    eng.tensor_copy(self.pt[:, m % 3].rearrange("p h k -> p (h k)"),
                                    t_pair[:, m % 2, :]).then_inc(s["pt_ready"].sem, 1)
                between(eng, n, 2)

    class Split:

        def __init__(self, own, src, n):
            self.src, self.n = src, n
            self.parts = [sb("parts", [P, 3, 2, GT], BF16, own) for _ in range(n)]
            self.res = sb("res", [P, 2, GT], F32, own)
            for k in ("hi_ready", "mid_ready", "lo_ready", "res_ready"):
                s[k].block(n)

        def high(self, eng, g, i):
            self.src_there(eng, g, i)
            if g:
                eng.wait_ge(s["stacked"].sem, s["stacked"].upto(g, 0))
            eng.activation(self.parts[i][:, 0], self.src[:], ACT.Copy).then_inc(s["hi_ready"].sem, 1)

        def rest(self, eng, g, i):
            eng.wait_ge(s["hi_ready"].sem, s["hi_ready"].upto(g, i + 1))
            if g or i:
                eng.wait_ge(s["lo_ready"].sem, s["lo_ready"].upto(g, i))
            eng.tensor_tensor(self.res[:], self.src[:], self.parts[i][:, 0], ALU.subtract).then_inc(s["res_ready"].sem, 1)

        def middle(self, eng, g, i):
            eng.wait_ge(s["res_ready"].sem, s["res_ready"].upto(g, i + 1))
            eng.activation(self.parts[i][:, 1], self.res[:], ACT.Copy).then_inc(s["mid_ready"].sem, 1)

        def low(self, eng, g, i):
            eng.wait_ge(s["mid_ready"].sem, s["mid_ready"].upto(g, i + 1))
            eng.tensor_tensor(self.parts[i][:, 2], self.res[:], self.parts[i][:, 1], ALU.subtract)\
               .then_inc(s["lo_ready"].sem, 1)

        def part_there(self, eng, g, i, part):
            ready = s[("hi_ready", "mid_ready", "lo_ready")[part]]
            eng.wait_ge(ready.sem, ready.upto(g, i + 1))

    def stack_rows(eng, stack, parts, which, part, base, rows):
        for slot, has in enumerate(SLOT_PARTS):
            if has[which] == part:
                at = base + slot * rows
                eng.dma_start(stack[at:at + rows, :, :], parts[:, part]).then_inc(s["stacked"].sem, 16)

    def residual(eng, g, banks, ready, n):
        eng.wait_ge(ready.sem, ready.upto(g, n))
        for m in range(FC):
            xs = x_t[:, m, bass.ds(g * GT, GT)]
            eng.tensor_tensor(xs, xs, banks[m], ALU.add).then_inc(s["x_done"].sem, 1)

    def group_start(eng, g, first):
        if not first:
            eng.wait_ge(s["x_done"].sem, s["x_done"].upto(g, 0))

    AFTER_NORM = 4

    def around(front, back, beyond, own=None):
        def between(eng, n, slot):
            g, at = divmod(n, QUADS)
            if own and g < GROUPS:
                own(eng, g, at, slot)
            if back and g >= 1:
                back(eng, g - 1, at, slot)
            if g + 1 < GROUPS:
                front(eng, g + 1, at, slot)
            elif g < GROUPS:
                beyond(eng, at, slot)
        return between

    def first_front(eng, front, start=0):
        for at in range(start, QUADS):
            for slot in range(3):
                front(eng, 0, at, slot)

    self_norm = Norm(W_LN_IN, ahead=True)
    cross_norm = Norm(W_LN_CROSS, ahead=True)
    mlp_norm = Norm(W_LN_MLP, ahead=True, tight=True)
    media_norm = Norm(LNQ_G, LNQ_B, ahead=True)
    ff_norm = Norm(LNF_G, LNF_B, ahead=True)

    def experts(eng, step, is_one, tt, b0, b1):
        tokens = slice(b0 * SEQ, b1 * SEQ)
        step(eng.tensor_scalar(is_one[:, b0:b1].rearrange("p b n -> p (b n)"), tt[:, tokens], 1.0, None, ALU.is_equal))
        vis = expert[:, 0, tokens].rearrange("p (b n) -> p b n", n=SEQ)
        step(eng.tensor_tensor(vis[:, :, 0:SEQ - 1], is_one[:, b0:b1, 0:SEQ - 1], is_one[:, b0:b1, 1:SEQ], ALU.mult))
        step(eng.memset(vis[:, :, SEQ - 1:SEQ], 0.0))
        step(eng.tensor_scalar(expert[:, 1, tokens], expert[:, 0, tokens], -1.0, 1.0, ALU.mult, ALU.add))

    def set_up(norm, rope):
        with ExitStack() as own:
            tt = sb("tt", [P, TOKENS], I32, own)
            is_one = sb("is_one", [P, BATCHES, SEQ], F32, own)
            pos_i = sb("pos_i", [P, SEQ], I32, own)
            pos_f = sb("pos_f", [P, SEQ], F32, own)
            pos_neg = sb("pos_neg", [P, SEQ], F32, own)
            onehot = sb("onehot", [P, SEQ], F32, own)
            consts = sb("consts", [P, 2 * P + 1], F32, own)
            raw_gates = sb("raw_gates", [P, 2], F32, own)
            s["setup_d"].block(12, 1)
            s["setup_p"].block(8, 1)
            s["setup_a"].block(1, 1)
            s["loaded"].block(8, 1, 16)
            s["x_first"].block(1, 1, 16)
            s["x_rest"].block(1, 1, 16)
            s["proj_ready"].block(1, 1)

            def chain(eng, done):
                count = [done.start]

                def step(ins):
                    count[0] += 1
                    ins.then_inc(done.sem, 1)
                    eng.wait_ge(done.sem, count[0])
                return step

            with nc.Block() as block:
                @block.sync
                def _(eng):
                    for dst, src in ((consts[:], a["consts"]), (pos_i[:], a["pos"].partition_broadcast(P)),
                                     (tt[:], a["tt"].partition_broadcast(P)), (ident[:], a["ident"])):
                        eng.dma_start(dst, src).then_inc(s["loaded"].sem, 16)
                    load_weights(eng, 0)
                    eng.dma_start(x_t[:, :, GT:], a["x"][:, :, GT:]).then_inc(s["x_rest"].sem, 16)
                    load_weights(eng, 1)

                @block.gpsimd
                def _(eng):
                    step = chain(eng, s["setup_p"])
                    step(eng.memset(mean_w[:], 1.0 / DIM))
                    step(eng.memset(ones_row[:], 1.0))
                    step(eng.memset(eps_cols[:, 0:1], EPS_RMS))
                    step(eng.memset(eps_cols[:, 1:2], EPS_LN))
                    eng.wait_ge(s["loaded"].sem, s["loaded"].total)
                    experts(eng, step, is_one, tt, GROUP, BATCHES)

                @block.scalar
                def _(eng):
                    eng.dma_start(x_t[:, :, 0:GT], a["x"][:, :, 0:GT]).then_inc(s["x_first"].sem, 16)
                    for dst, src in ((scales[:], a["scales"]), (raw_gates[:], a["gates"].partition_broadcast(P)),
                                     (causal[:], a["causal"]), (keys[:], a["keys"])):
                        eng.dma_start(dst, src).then_inc(s["loaded"].sem, 16)
                    eng.wait_ge(s["x_first"].sem, s["x_first"].total)
                    norm.square(eng, 0)
                    eng.wait_ge(s["setup_p"].sem, 4)
                    norm.root(eng, 0)
                    eng.wait_ge(s["loaded"].sem, s["loaded"].total)
                    eng.activation(gates[:], raw_gates[:], ACT.Tanh).then_inc(s["setup_a"].sem, 1)

                @block.vector
                def _(eng):
                    step = chain(eng, s["setup_d"])
                    eng.wait_ge(s["loaded"].sem, s["loaded"].total)
                    step(eng.tensor_copy(pos_f[:], pos_i[:]))
                    step(eng.tensor_scalar(pos_neg[:], pos_f[:], 0.0, float(SEQ), ALU.is_lt, ALU.mult))
                    step(eng.tensor_tensor(pos_f[:], pos_f[:], pos_neg[:], ALU.add))
                    step(eng.tensor_scalar(pos_f[:], pos_f[:], 0.0, float(SEQ - 1), ALU.max, ALU.min))
                    step(eng.tensor_scalar(onehot[:], pos_f[:], consts[:, 2 * P:2 * P + 1], None, ALU.is_equal))
                    step(eng.tensor_copy(ident_b[:], ident[:]))
                    experts(eng, step, is_one, tt, 0, GROUP)
                    eng.wait_ge(s["proj_ready"].sem, s["proj_ready"].upto(0, 1))
                    tables = bank[0][:, 0:2 * SEQ].rearrange("p (a n) -> p a n", a=2)
                    step(eng.tensor_scalar(rope[:, 0], tables, HD0 ** -0.5, None, ALU.mult))
                    step(eng.tensor_copy(rope[:, 1], tables))
                    norm.vector(eng, 0)

                @block.tensor
                def _(eng):
                    eng.wait_ge(s["setup_p"].sem, 4)
                    norm.tensor(eng, 0)
                    eng.wait_ge(s["setup_d"].sem, 5)
                    eng.matmul(bank[0][:, 0:SEQ], consts[:, 0:P], onehot[:], start=True, stop=True)
                    eng.matmul(bank[0][:, SEQ:2 * SEQ], consts[:, P:2 * P], onehot[:], start=True,
                               stop=True).then_inc(s["proj_ready"].sem, 1)

    def self_attention():
        with ExitStack() as own:
            norm, next_norm = self_norm, cross_norm
            rope = sb("rope", [P, 2, 2, SEQ], F32, own)
            set_up(norm, rope)
            xe = sb("xe", [P, 2, FC, GT], F32, own)
            rot_c = sb("rot_c", [P, 2, GT], F32, own)
            rot_s = sb("rot_s", [P, 2, GT], F32, own)
            rot = sb("rot", [P, 2, GT], F32, own)
            split = Split(own, rot, 2)
            spare_a = weights_a[0:SLOTS * HD0, 4096:4096 + HEADS * GT // 2].bitcast(BF16).rearrange("p (h n) -> p h n", h=HEADS)
            spare_b = weights_b[0:SLOTS * HD0, 1024:1024 + HEADS * GT // 2].bitcast(BF16).rearrange("p (h n) -> p h n", h=HEADS)
            q_stack = [sb("q_stack", [SLOTS * HD0, HEADS, GT], BF16, own)[:], spare_a]
            k_stack = [sb("k_stack", [SLOTS * HD0, HEADS, GT], BF16, own)[:], spare_b]
            val = sb("val", [P, GROUP, HEADS // QUAD, QUAD, QUAD * HD0], F32, own)
            mixed = sb("mixed", [P, 2, FC, GT], F32, own)
            for n, k in (("xv_ready", 1), ("xl_ready", 1), ("proj_ready", 4), ("rot_part", 8), ("rot_ready", 4),
                         ("v_ready", GROUP), ("v_out_a", GROUP // 2), ("v_out_d", GROUP // 2), ("back_out", GROUP),
                         ("out_ready", FC), ("x_done", FC)):
                s[n].block(k)
            s["stacked"].block(4 * SLOTS, amount=16)
            s["setup_p"].block(1, 1)

            def causal_bias(eng, g, to, b):
                eng.matmul(to, ident_b[:], causal[:].unsqueeze(1).to_broadcast([P, QUAD, SEQ]), start=True, stop=False,
                           skip_group_check=True)

            def post(eng, u):
                g, b = divmod(u, GROUP)
                if b == 0 and g:
                    eng.wait_ge(s["out_ready"].sem, s["out_ready"].upto(g - 1, FC))
                src = bank[4 + u % 2][:, 0:FC * P].rearrange("p (c n) -> p c n", c=FC)
                for e in range(2):
                    mask = expert[:, e, u * SEQ:(u + 1) * SEQ].unsqueeze(1).to_broadcast([P, FC, SEQ])
                    ins = eng.tensor_tensor(mixed[:, e, :, b * SEQ:(b + 1) * SEQ], src, mask, ALU.mult)
                ins.then_inc(s["back_out"].sem, 1)

            def score(g, b, h):
                cols = slice(b * SEQ, (b + 1) * SEQ)
                return q_stack[g % 2][:, h, cols], k_stack[g % 2][:, h, cols]

            def place(to, n, h):
                chunk, part = divmod(n % (HEADS // QUAD), 2)
                width = QUAD * HD0
                return to[part * width:(part + 1) * width, chunk * SEQ:(chunk + 1) * SEQ]

            att = Attention(own, score, causal_bias, lambda g, b, q, h: val[:, b, q, h, :], HEADS // QUAD, place, True,
                            post)

            def project(eng, g, i, half):
                if i == 0 and half == 0:
                    eng.wait_ge(s["xv_ready"].sem, s["xv_ready"].upto(g, 1))
                    eng.wait_ge(s["xl_ready"].sem, s["xl_ready"].upto(g, 1))
                if i == 0 and g:
                    if g >= 2:
                        eng.wait_ge(s["x_done"].sem, s["x_done"].upto(g - 2, half + 1))
                if i == 1:
                    eng.wait_ge(s["rot_part"].sem, s["rot_part"].upto(g, 2 * half + 2))
                col = (2 * i + half) * P
                product(eng, bank[6 + half], [(w_qk[:, e, c, col:col + P], xe[:, e, c, :])
                                              for e in range(2) for c in range(FC)]).then_inc(s["proj_ready"].sem, 1)

            def on_act(b):
                return b in (1, 2)

            def values(eng, g, first):
                if first == 0:
                    eng.wait_ge(s["rot_part"].sem, s["rot_part"].upto(g, 8))
                for b in (first, first + 1):
                    if first:
                        out_of = s["v_out_a"] if on_act(b) else s["v_out_d"]
                        eng.wait_ge(out_of.sem, out_of.upto(g, 1))
                    product(eng, bank[7 if on_act(b) else 6][:, 0:DIM], [(xe[:, e, c, b * SEQ:(b + 1) * SEQ], w_v[:, e, c, :])
                                                             for e in range(2) for c in range(FC)])\
                        .then_inc(s["v_ready"].sem, 1)

            def mean(eng, g, of=norm, group=None):
                if g:
                    eng.wait_ge(s["v_out_a"].sem, s["v_out_a"].upto(g - 1, GROUP // 2))
                of.tensor(eng, g if group is None else group)

            def output(eng, g, m):
                if m == 0:
                    eng.wait_ge(s["back_out"].sem, s["back_out"].upto(g, GROUP))
                    eng.wait_ge(s["v_out_d"].sem, s["v_out_d"].upto(min(g + 1, GROUPS - 1), GROUP // 2))
                    eng.wait_ge(s["v_out_a"].sem, s["v_out_a"].upto(min(g + 1, GROUPS - 1), GROUP // 2))
                    if g + 2 <= GROUPS:
                        ready = norm.dev_ready if g + 2 < GROUPS else next_norm.dev_ready
                        eng.wait_ge(ready.sem, ready.upto((g + 2) % GROUPS, 1))
                product(eng, bank[6 + m], [(w_dense[:, e, c, m * P:(m + 1) * P], mixed[:, e, c, :])
                                           for e in range(2) for c in range(FC)]).then_inc(s["out_ready"].sem, 1)

            def pe_front(eng, g, at, slot):
                if slot == 0:
                    if at == 1:
                        mean(eng, g)
                    elif 7 <= at < 11:
                        project(eng, g, (at - 7) // 2, (at - 7) % 2)
                    elif at in (12, 14):
                        values(eng, g, at - 12)
                elif (at, slot) == (15, 2):
                    eng.wait_ge(s["stacked"].sem, s["stacked"].upto(g, 4 * SLOTS))
                    for out_of in (s["v_out_a"], s["v_out_d"]):
                        eng.wait_ge(out_of.sem, out_of.upto(g, 1))

            def pe_own(eng, g, at, slot):
                if (at, slot) == (8, 0):
                    for out_of in (s["v_out_a"], s["v_out_d"]):
                        eng.wait_ge(out_of.sem, out_of.upto(g, GROUP // 2))

            def pe_back(eng, g, at, slot):
                if at in (5, 6) and slot == 0:
                    output(eng, g, at - 5)

            def rotated(eng, g, i, half):
                eng.wait_ge(s["proj_ready"].sem, s["proj_ready"].upto(g, 2 * i + half + 1))
                if half == 0 and (g or i):
                    eng.wait_ge(s["rot_ready"].sem, s["rot_ready"].upto(g, 2 * i))
                for k, to in enumerate((rot_c, rot_s)):
                    eng.tensor_tensor(to[:, half].rearrange("p (b n) -> p b n", n=SEQ),
                                      bank[6 + half].rearrange("p (b n) -> p b n", n=SEQ),
                                      rope[:, i, k, :].unsqueeze(1).to_broadcast([P, GROUP, SEQ]),
                                      ALU.mult).then_inc(s["rot_part"].sem, 1)

            def combined(eng, g, i):
                eng.wait_ge(s["rot_part"].sem, s["rot_part"].upto(g, 4 * i + 4))
                if g or i:
                    eng.wait_ge(s["hi_ready"].sem, s["hi_ready"].upto(g, i))
                    eng.wait_ge(s["res_ready"].sem, s["res_ready"].upto(g, i))
                eng.tensor_tensor(rot[:, 0], rot_c[:, 0], rot_s[:, 1], ALU.subtract).then_inc(s["rot_ready"].sem, 1)
                eng.tensor_tensor(rot[:, 1], rot_c[:, 1], rot_s[:, 0], ALU.add).then_inc(s["rot_ready"].sem, 1)

            def take_values(eng, g, b):
                eng.wait_ge(s["v_ready"].sem, s["v_ready"].upto(g, b + 1))
                if g:
                    att.wait(eng, "ctx_ready", QUADS * (g - 1) + HEADS // QUAD * (b + 1))
                else:
                    eng.wait_ge(s["setup_p"].sem, s["setup_p"].upto(0, 1))
                src = bank[7 if on_act(b) else 6][:, 0:DIM].rearrange("p (q h d) -> p q h d", h=QUAD, d=HD0)
                for h in range(QUAD):
                    to = val[:, b, :, h, h * HD0:(h + 1) * HD0]
                    if on_act(b):
                        ins = eng.activation(to, src[:, :, h, :], ACT.Copy)
                    else:
                        ins = eng.tensor_copy(to, src[:, :, h, :])
                ins.then_inc(s["v_out_a" if on_act(b) else "v_out_d"].sem, 1)

            def add(eng, g, m):
                eng.wait_ge(s["out_ready"].sem, s["out_ready"].upto(g, m + 1))
                xs = x_t[:, m, g * GT:(g + 1) * GT]
                eng.tensor_tensor(xs, xs, bank[6 + m], ALU.add).then_inc(s["x_done"].sem, 1)

            def dve_front(eng, g, at, slot):
                if (at, slot) == (2, 2):
                    if g:
                        eng.wait_ge(s["xv_ready"].sem, s["xv_ready"].upto(g - 1, 1))
                        eng.wait_ge(s["xl_ready"].sem, s["xl_ready"].upto(g - 1, 1))
                    norm.scaled(eng, g)
                elif 8 <= at < 12 and slot == 1:
                    rotated(eng, g, (at - 8) // 2, (at - 8) % 2)
                elif at in (9, 11) and slot == 2:
                    combined(eng, g, (at - 9) // 2)
                elif at in (10, 12) and slot == 2:
                    split.rest(eng, g, (at - 10) // 2)
                elif at in (12, 14) and slot == 0:
                    split.low(eng, g, (at - 12) // 2)
                elif (at, slot) == (13, 2):
                    take_values(eng, g, 0)

            def dve_own(eng, g, at, slot):
                if (at, slot) == (3, 1):
                    take_values(eng, g, 3)

            def dve_back(eng, g, at, slot):
                if at in (6, 7) and slot == 2:
                    add(eng, g, at - 6)

            def act_front(eng, g, at, slot):
                if slot == 0:
                    if at == 0:
                        if g == 1:
                            eng.wait_ge(s["x_rest"].sem, s["x_rest"].total)
                        norm.square(eng, g)
                    elif at == 1:
                        norm.inverse_root(eng, g)
                    elif at in (10, 12):
                        split.high(eng, g, (at - 10) // 2)
                    elif at in (11, 13):
                        split.middle(eng, g, (at - 10) // 2)
                    if at == 13:
                        take_values(eng, g, 1)

            def act_own(eng, g, at, slot):
                if (at, slot) == (0, 0):
                    take_values(eng, g, 2)

            def pool_front(eng, g, at, slot):
                if at in (3, 4) and slot == 0 and g:
                    norm.there(eng, g)
                    eng.wait_ge(s["v_ready"].sem, s["v_ready"].upto(g - 1, GROUP))
                    masked(eng, g, at - 3)

            def masked(eng, g, e):
                mask = expert[:, e, g * GT:(g + 1) * GT].unsqueeze(1).to_broadcast([P, FC, GT])
                eng.tensor_tensor(xe[:, e], norm.xn[:], mask, ALU.mult).then_inc(s[("xv_ready", "xl_ready")[e]].sem, 1)

            def pe_beyond(eng, at, slot):
                if (at, slot) == (1, 0):
                    mean(eng, GROUPS, next_norm, 0)

            def act_beyond(eng, at, slot):
                if (at, slot) == (0, 0):
                    eng.wait_ge(s["x_done"].sem, s["x_done"].upto(0, FC))
                    for ready in (s["xv_ready"], s["xl_ready"]):
                        eng.wait_ge(ready.sem, ready.upto(GROUPS, 0))
                    eng.wait_ge(norm.rstd_ready.sem, norm.rstd_ready.upto(GROUPS, 0))
                    next_norm.square(eng, 0)
                elif (at, slot) == (1, 0):
                    next_norm.inverse_root(eng, 0)

            def dve_beyond(eng, at, slot):
                if (at, slot) == (2, 2):
                    for ready in (s["xv_ready"], s["xl_ready"]):
                        eng.wait_ge(ready.sem, ready.upto(GROUPS, 0))
                    next_norm.scaled(eng, 0)

            split.src_there = lambda eng, g, i: eng.wait_ge(s["rot_ready"].sem, s["rot_ready"].upto(g, 2 * i + 2))

            with nc.Block() as block:
                @block.sync
                def _(eng):
                    for g in range(GROUPS):
                        for i, stack in enumerate((q_stack, k_stack)):
                            if g >= 2 and i == 0:
                                att.wait(eng, "scores_ready", QUADS * (g - 1))
                            for part in range(3):
                                split.part_there(eng, g, i, part)
                                for half in range(2):
                                    stack_rows(eng, stack[g % 2], split.parts[i][:, :, half, :], i, part,
                                               half * SLOTS * HALF, HALF)

                @block.gpsimd
                def _(eng):
                    masked(eng, 0, 1)
                    eng.memset(val[:], 0.0).then_inc(s["setup_p"].sem, 1)
                    att.pool(eng, around(pool_front, None, lambda *step: None))

                @block.scalar
                def _(eng):
                    first_front(eng, act_front, start=AFTER_NORM)
                    att.scalar(eng, around(act_front, None, act_beyond, act_own))

                @block.vector
                def _(eng):
                    masked(eng, 0, 0)
                    first_front(eng, dve_front, start=AFTER_NORM)
                    att.vector(eng, around(dve_front, dve_back, dve_beyond, dve_own))
                    for m in range(FC):
                        add(eng, GROUPS - 1, m)

                @block.tensor
                def _(eng):
                    weights_there(eng, 0)
                    first_front(eng, pe_front, start=AFTER_NORM)
                    att.tensor(eng, around(pe_front, pe_back, pe_beyond, pe_own))
                    for m in range(FC):
                        output(eng, GROUPS - 1, m)

    def cross_attention():
        with ExitStack() as own:
            norm, next_norm = cross_norm, mlp_norm
            context = sb("context", [P, GT], F32, own)
            qk = sb("qk", [P, 2, GT], F32, own)
            split = Split(own, qk, 1)
            stack = [[sb("stack", [SLOTS * HD0C, HEADS, GT], BF16, own)[:] for _ in range(2)], None]
            stack[1] = [sb("stack", [SLOTS * HD0C, HEADS, GT], BF16, own)[:], None]
            stack[1][1] = weights_b[0:SLOTS * HD0C, 1024:1024 + HEADS * GT // 2].bitcast(BF16)\
                .rearrange("p (h n) -> p h n", h=HEADS)
            val = sb("val", [P, 2, GROUP, HEADS // QUAD, QUAD, QUAD * HD0C], F32, own)
            gathered = sb("gathered", [P, GT], F32, own)
            for n, k in (("proj_ready", 2), ("rot_ready", 2), ("v_ready", 1), ("v_out_d", QUAD),
                         ("back_out", GROUP), ("out_ready", FC), ("x_done", FC)):
                s[n].block(k)
            s["stacked"].block(2 * SLOTS, amount=16)
            s["ctx_loaded"].block(1, amount=16)
            s["setup_p"].block(3, 1)
            split.src_there = lambda eng, g, i: eng.wait_ge(s["rot_ready"].sem, s["rot_ready"].upto(g, 2))

            def post(eng, u):
                g, b = divmod(u, GROUP)
                if b == 0 and g:
                    eng.wait_ge(s["out_ready"].sem, s["out_ready"].upto(g - 1, FC))
                eng.tensor_copy(gathered[:, b * SEQ:(b + 1) * SEQ], bank[4 + u % 2][:, 0:SEQ]).then_inc(s["back_out"].sem, 1)

            def score(g, b, h):
                cols = slice(b * SEQ, (b + 1) * SEQ)
                return stack[g % 2][0][:, h, cols], stack[g % 2][1][:, h, cols]

            def place(to, n, h):
                part = n % (HEADS // QUAD)
                return to[part * QUAD * HD0C:(part + 1) * QUAD * HD0C, 0:SEQ]

            att = Attention(own, score, no_bias, lambda g, b, q, h: val[:, g % 2, b, q, h, :], HEADS // QUAD, place,
                                  True, post)

            def mean(eng, g, of=norm, group=None):
                if g:
                    eng.wait_ge(s["v_out_d"].sem, s["v_out_d"].upto(g - 1, QUAD))
                of.tensor(eng, g if group is None else group)

            def project(eng, g):
                norm.there(eng, g)
                product(eng, bank[6], [(w_cq[:, c, :], norm.xn[:, c, :]) for c in range(FC)])\
                    .then_inc(s["proj_ready"].sem, 1)
                eng.wait_ge(s["ctx_loaded"].sem, s["ctx_loaded"].upto(g, 1))
                eng.wait_ge(norm.dev_ready.sem, norm.dev_ready.upto(g, 1))
                product(eng, bank[7], [(w_ck, context[:])]).then_inc(s["proj_ready"].sem, 1)

            def output(eng, g):
                eng.wait_ge(s["back_out"].sem, s["back_out"].upto(g, GROUP))
                if g + 2 < GROUPS:
                    eng.wait_ge(s["rot_ready"].sem, s["rot_ready"].upto(g + 2, 2))
                elif g + 2 == GROUPS:
                    eng.wait_ge(next_norm.dev_ready.sem, next_norm.dev_ready.upto(0, 1))
                for m in range(FC):
                    product(eng, bank[6 + m], [(w_cdense[:, m * P:(m + 1) * P], gathered[:])])\
                        .then_inc(s["out_ready"].sem, 1)

            def values(eng, g):
                eng.wait_ge(s["rot_ready"].sem, s["rot_ready"].upto(g, 2))
                if g >= 2:
                    eng.wait_ge(s["x_done"].sem, s["x_done"].upto(g - 2, FC))
                for b in range(GROUP):
                    mm = product(eng, bank[6][:, b * P:(b + 1) * P], [(context[:, b * SEQ:(b + 1) * SEQ], w_cv)])
                mm.then_inc(s["v_ready"].sem, 1)

            def pe_front(eng, g, at, slot):
                if (at, slot) == (1, 0):
                    mean(eng, g)
                elif (at, slot) == (4, 0):
                    project(eng, g)
                elif (at, slot) == (10, 0):
                    values(eng, g)
                elif (at, slot) == (15, 2):
                    eng.wait_ge(s["stacked"].sem, s["stacked"].upto(g, 2 * SLOTS))
                    eng.wait_ge(s["v_out_d"].sem, s["v_out_d"].upto(g, QUAD))

            def pe_back(eng, g, at, slot):
                if (at, slot) == (7, 0):
                    output(eng, g)

            def take_values(eng, g):
                eng.wait_ge(s["v_ready"].sem, s["v_ready"].upto(g, 1))
                for h in range(QUAD):
                    to = val[:, g % 2, :, :, h, h * HD0C:(h + 1) * HD0C].rearrange("p b q d -> p (b q) d")
                    src = bank[6].rearrange("p (q h d) -> p q h d", h=QUAD, d=HD0C)[:, :, h, :]
                    eng.tensor_copy(to, src).then_inc(s["v_out_d"].sem, 1)

            def add(eng, g, m):
                eng.wait_ge(s["out_ready"].sem, s["out_ready"].upto(g, m + 1))
                xs = x_t[:, m, g * GT:(g + 1) * GT]
                eng.tensor_tensor(xs, xs, bank[6 + m], ALU.add).then_inc(s["x_done"].sem, 1)

            def dve_front(eng, g, at, slot):
                if (at, slot) == (2, 1):
                    if g:
                        eng.wait_ge(s["proj_ready"].sem, s["proj_ready"].upto(g - 1, 1))
                    norm.scaled(eng, g)
                elif (at, slot) == (7, 2):
                    split.rest(eng, g, 0)
                elif (at, slot) == (9, 2):
                    split.low(eng, g, 0)
                elif (at, slot) == (11, 2):
                    take_values(eng, g)

            def dve_back(eng, g, at, slot):
                if at in (7, 8) and slot == 2:
                    add(eng, g, at - 7)

            def take_projected(eng, g):
                if g:
                    eng.wait_ge(s["res_ready"].sem, s["res_ready"].upto(g - 1, 1))
                eng.wait_ge(s["proj_ready"].sem, s["proj_ready"].upto(g, 1))
                eng.activation(qk[:, 0], bank[6], ACT.Copy, scale=HD0C ** -0.5).then_inc(s["rot_ready"].sem, 1)
                eng.wait_ge(s["proj_ready"].sem, s["proj_ready"].upto(g, 2))
                eng.activation(qk[:, 1], bank[7], ACT.Copy).then_inc(s["rot_ready"].sem, 1)

            def act_front(eng, g, at, slot):
                if slot == 0:
                    if at == 0:
                        norm.square(eng, g)
                    elif at == 1:
                        norm.inverse_root(eng, g)
                    elif at == 5:
                        take_projected(eng, g)
                    elif at == 6:
                        split.high(eng, g, 0)
                    elif at == 8:
                        split.middle(eng, g, 0)


            def pe_beyond(eng, at, slot):
                if (at, slot) == (1, 0):
                    mean(eng, GROUPS, next_norm, 0)

            def act_beyond(eng, at, slot):
                if (at, slot) == (0, 0):
                    eng.wait_ge(s["x_done"].sem, s["x_done"].upto(0, FC))
                    eng.wait_ge(s["proj_ready"].sem, s["proj_ready"].upto(GROUPS - 1, 1))
                    eng.wait_ge(norm.rstd_ready.sem, norm.rstd_ready.upto(GROUPS, 0))
                    next_norm.square(eng, 0)
                elif (at, slot) == (1, 0):
                    next_norm.inverse_root(eng, 0)

            def dve_beyond(eng, at, slot):
                if (at, slot) == (2, 1):
                    eng.wait_ge(s["proj_ready"].sem, s["proj_ready"].upto(GROUPS - 1, 1))
                    next_norm.scaled(eng, 0)

            with nc.Block() as block:
                @block.sync
                def _(eng):
                    for g in range(GROUPS):
                        if g:
                            eng.wait_ge(s["v_ready"].sem, s["v_ready"].upto(g - 1, 1))
                        eng.dma_start(context[:], a["ctx"][:, g * GT:(g + 1) * GT]).then_inc(s["ctx_loaded"].sem, 16)
                        if g == 0:
                            load_weights(eng, 2)
                        if g >= 2:
                            att.wait(eng, "scores_ready", QUADS * (g - 1))
                        for part in range(3):
                            split.part_there(eng, g, 0, part)
                            for i in range(2):
                                stack_rows(eng, stack[g % 2][i], split.parts[0][:, :, i, :], i, part, 0, HD0C)

                @block.gpsimd
                def _(eng):
                    eng.memset(val[:], 0.0).then_inc(s["setup_p"].sem, 1)
                    for e, rows in enumerate((slice(0, REST_AT), slice(REST_AT, P))):
                        eng.wait_ge(s["setup_p"].sem, s["setup_p"].upto(0, 1 + e))
                        eng.tensor_copy(rest_mask[rows, :], expert[rows, e, :]).then_inc(s["setup_p"].sem, 1)
                    eng.wait_ge(s["setup_p"].sem, s["setup_p"].upto(0, 3))
                    att.pool(eng, lambda *step: None)

                @block.scalar
                def _(eng):
                    eng.wait_ge(s["setup_p"].sem, s["setup_p"].upto(0, 1))
                    first_front(eng, act_front, start=AFTER_NORM)
                    att.scalar(eng, around(act_front, None, act_beyond))

                @block.vector
                def _(eng):
                    eng.wait_ge(s["setup_p"].sem, s["setup_p"].upto(0, 1))
                    first_front(eng, dve_front, start=AFTER_NORM)
                    att.vector(eng, around(dve_front, dve_back, dve_beyond))
                    for m in range(FC):
                        add(eng, GROUPS - 1, m)

                @block.tensor
                def _(eng):
                    weights_there(eng, 1)
                    first_front(eng, pe_front, start=AFTER_NORM)
                    att.tensor(eng, around(pe_front, pe_back, pe_beyond))
                    output(eng, GROUPS - 1)

    def expert_mlp():
        with ExitStack() as own:
            norm = mlp_norm
            xn = [sb("xn_part", [P, FC, GT], F32R, own) for _ in range(2)]
            xe = [sb("xe", [P, 2, FC, GT], F32R, own) for _ in range(2)]
            act = norm_sq
            hid = sb("hid", [P, 2, GT], F32, own)
            hid_parts = [sb("hid_part", [P, 3, GT], F32R, own) for _ in range(2)]
            size = FC * HTILES * P
            high_low = [sb("w_part", [P, 3 * size], F32R, own) for _ in range(2)]
            w_parts = []
            for n, shape in enumerate(((FC, HTILES * P), (FC, HTILES * P), (HTILES, DIM))):
                w_parts.append([split_free(part[:, n * size:(n + 1) * size], shape) for part in high_low])
            gate_parts, up_parts, down_parts = w_parts
            PIECES = ((0, 1), (1, 3), (3, MT + 1), (MT + 1, HTILES))
            for n, k in (("xnh_ready", 1), ("xnl_ready", 1), ("xv_ready", 2), ("xl_ready", 2), ("proj_ready", HTILES),
                         ("act_ready", HTILES), ("hid_ready", HTILES + 1), ("high_ready", HTILES), ("low_ready", HTILES),
                         ("hid_free", HTILES), ("x_done", FC)):
                s[n].block(k)
            s["wh_ready"].block(3 * len(PIECES), 1)
            s["wl_ready"].block(3 * len(PIECES), 1)

            def banks(t):
                return pair[t % 2] if t else pair[3]

            def hidden_there(eng, g, t):
                eng.wait_ge(s["hid_ready"].sem, s["hid_ready"].upto(g, t + 2))

            def part_free(eng, g, t, first):
                if t >= 3:
                    eng.wait_ge(s["hid_free"].sem, s["hid_free"].upto(g, t - 2))
                elif t == 1:
                    eng.wait_ge(s["hid_free"].sem, s["hid_free"].upto(g, 0))
                elif t == 0 and not first:
                    eng.wait_ge(s["hid_free"].sem, s["hid_free"].upto(g, 0) - 1)

            def pieces(n):
                a, b = PIECES[n]
                cols = (slice(None), slice(None), slice(a * P, b * P))
                rows = (slice(None), slice(a, b), slice(None))
                for w, (hi, lo), at in ((w_gate, gate_parts, cols), (w_up, up_parts, cols), (w_down, down_parts, rows)):
                    yield w[at], hi[at], lo[at]

            def weights_high(eng, n):
                for w, hi, lo in pieces(n):
                    eng.activation(hi, w, ACT.Copy).then_inc(s["wh_ready"].sem, 1)

            def gated(eng, g, t):
                eng.wait_ge(s["proj_ready"].sem, s["proj_ready"].upto(g, t + 1))
                if t >= 2:
                    hidden_there(eng, g, t - 2)
                else:
                    eng.wait_ge(s["hid_ready"].sem, s["hid_ready"].upto(g, 0))
                eng.activation(act[:, t % 2], banks(t)[:, 0, :], ACT.Silu).then_inc(s["act_ready"].sem, 1)

            def hidden_high(eng, g, t, first=False):
                hidden_there(eng, g, t)
                part_free(eng, g, t, first)
                eng.activation(hid_parts[0][:, t % 3], hid[:, t % 2], ACT.Copy).then_inc(s["high_ready"].sem, 1)

            def normed_high(eng, g):
                norm.there(eng, g)
                eng.wait_ge(s["xl_ready"].sem, s["xl_ready"].upto(g, 0))
                eng.wait_ge(s["xv_ready"].sem, s["xv_ready"].upto(g, 0))
                eng.activation(xn[0][:], norm.xn[:], ACT.Copy).then_inc(s["xnh_ready"].sem, 1)

            def hidden(eng, g, t):
                eng.wait_ge(s["act_ready"].sem, s["act_ready"].upto(g, t + 1))
                eng.wait_ge(s["low_ready"].sem, s["low_ready"].upto(g, max(t - 1, 0)))
                eng.tensor_tensor(hid[:, t % 2], act[:, t % 2], banks(t)[:, 1, :], ALU.mult)\
                   .then_inc(s["hid_ready"].sem, 1)
                if t == 0:
                    eng.wait_ge(s["hid_ready"].sem, s["hid_ready"].upto(g, 1))
                    eng.tensor_tensor(hid[:, 0], hid[:, 0], tok(rest_mask[:], g), ALU.mult)\
                       .then_inc(s["hid_ready"].sem, 1)

            def hidden_low(eng, g, t, first=False):
                eng.wait_ge(s["high_ready"].sem, s["high_ready"].upto(g, t + 1))
                part_free(eng, g, t, first)
                hidden_there(eng, g, t)
                eng.tensor_tensor(hid_parts[1][:, t % 3], hid[:, t % 2], hid_parts[0][:, t % 3].bitcast(F32),
                                  ALU.subtract).then_inc(s["low_ready"].sem, 1)

            def normed_low(eng, g):
                norm.there(eng, g)
                eng.wait_ge(s["xnh_ready"].sem, s["xnh_ready"].upto(g, 1))
                eng.tensor_tensor(xn[1][:], norm.xn[:], xn[0][:].bitcast(F32), ALU.subtract)\
                   .then_inc(s["xnl_ready"].sem, 1)

            def masked(eng, g, e, ready):
                mask = tok(expert[:, e, :], g).unsqueeze(1).to_broadcast([P, FC, GT])
                for part in range(2):
                    eng.tensor_tensor(xe[part][:, e], xn[part][:].bitcast(F32), mask, ALU.mult).then_inc(ready.sem, 1)

            def project(eng, g, t):
                if t == 0:
                    eng.wait_ge(s["xnh_ready"].sem, s["xnh_ready"].upto(g, 1))
                    eng.wait_ge(s["xnl_ready"].sem, s["xnl_ready"].upto(g, 1))
                    eng.wait_ge(norm.dev_ready.sem, norm.dev_ready.upto(g, 1))
                elif t == 1:
                    eng.wait_ge(s["xv_ready"].sem, s["xv_ready"].upto(g, 2))
                elif t == MT + 1:
                    eng.wait_ge(s["xl_ready"].sem, s["xl_ready"].upto(g, 2))
                for n, (a, b) in enumerate(PIECES):
                    if t == a:
                        eng.wait_ge(s["wh_ready"].sem, s["wh_ready"].upto(0, 3 * (n + 1)))
                        eng.wait_ge(s["wl_ready"].sem, s["wl_ready"].upto(0, 3 * (n + 1)))
                if t >= 3:
                    hidden_there(eng, g, t - 2)
                for w, to in ((gate_parts, 0), (up_parts, 1)):
                    mm = split_product(eng, banks(t)[:, to, :],
                                       [([part[:, c, t * P:(t + 1) * P] for part in w],
                                         [part[:, (t - 1) // MT, c, :] for part in xe] if t else [part[:, c, :] for part in xn])
                                        for c in range(FC)])
                mm.then_inc(s["proj_ready"].sem, 1)

            def down(eng, g, t):
                eng.wait_ge(s["high_ready"].sem, s["high_ready"].upto(g, t + 1))
                eng.wait_ge(s["low_ready"].sem, s["low_ready"].upto(g, t + 1))
                if t == 0:
                    eng.wait_ge(s["x_done"].sem, s["x_done"].upto(g, 0))
                for m in range(FC):
                    mm = split_product(eng, bank[4 + m], [([part[:, t, m * P:(m + 1) * P] for part in down_parts],
                                                           [part[:, t % 3] for part in hid_parts])],
                                       start=t == 0, stop=t == HTILES - 1)
                mm.then_inc(s["hid_free"].sem, 1)

            with nc.Block() as block:
                @block.sync
                def _(eng):
                    load_weights(eng, 3)

                @block.gpsimd
                def _(eng):
                    weights_there(eng, 2)

                    def weights_low(n):
                        eng.wait_ge(s["wh_ready"].sem, s["wh_ready"].upto(0, 3 * (n + 1)))
                        for w, hi, lo in pieces(n):
                            eng.tensor_tensor(lo, w, hi.bitcast(F32), ALU.subtract).then_inc(s["wl_ready"].sem, 1)

                    def start():
                        weights_low(0)
                        weights_low(1)
                        weights_low(2)
                        eng.wait_ge(s["xnl_ready"].sem, s["xnl_ready"].upto(0, 1))
                        masked(eng, 0, 1, s["xl_ready"])
                        weights_low(3)

                    def body(g, more):
                        if more:
                            eng.wait_ge(s["xnl_ready"].sem, s["xnl_ready"].upto(g + 1, 1))
                            eng.wait_ge(s["proj_ready"].sem, s["proj_ready"].upto(g, HTILES))
                            masked(eng, g + 1, 1, s["xl_ready"])
                    ahead_over_groups(eng, start, body)

                @block.scalar
                def _(eng):
                    weights_there(eng, 2)

                    def start():
                        weights_high(eng, 0)
                        normed_high(eng, 0)
                        weights_high(eng, 1)
                        weights_high(eng, 2)
                        weights_high(eng, 3)
                        gated(eng, 0, 0)
                        hidden_high(eng, 0, 0, first=True)

                    def body(g, more):
                        for t in range(1, HTILES):
                            gated(eng, g, t)
                            hidden_high(eng, g, t)
                            if t == 1 and more:
                                eng.wait_ge(s["xnl_ready"].sem, s["xnl_ready"].upto(g, 1))
                                norm.square(eng, g + 1)
                                norm.root(eng, g + 1)
                            if t == 4 and more:
                                normed_high(eng, g + 1)
                        if more:
                            gated(eng, g + 1, 0)
                            hidden_high(eng, g + 1, 0)
                    ahead_over_groups(eng, start, body)

                @block.vector
                def _(eng):
                    def start():
                        normed_low(eng, 0)
                        masked_v(0)
                        hidden(eng, 0, 0)
                        hidden_low(eng, 0, 0, first=True)

                    def masked_v(g):
                        eng.wait_ge(s["xnl_ready"].sem, s["xnl_ready"].upto(g, 1))
                        masked(eng, g, 0, s["xv_ready"])

                    def body(g, more):
                        for t in range(1, HTILES):
                            hidden(eng, g, t)
                            hidden_low(eng, g, t)
                            if t == 3 and more:
                                norm.vector(eng, g + 1)
                            if t == 5 and more:
                                eng.wait_ge(s["proj_ready"].sem, s["proj_ready"].upto(g, 1))
                                eng.wait_ge(s["xl_ready"].sem, s["xl_ready"].upto(g, 2))
                                normed_low(eng, g + 1)
                            if t == 7 and more:
                                eng.wait_ge(s["proj_ready"].sem, s["proj_ready"].upto(g, MT + 1))
                                masked_v(g + 1)
                        if more:
                            hidden(eng, g + 1, 0)
                            hidden_low(eng, g + 1, 0)
                        residual(eng, g, (bank[4], bank[5]), s["hid_free"], HTILES)
                    ahead_over_groups(eng, start, body)

                @block.tensor
                def _(eng):
                    def start():
                        project(eng, 0, 0)
                        project(eng, 0, 1)

                    def body(g, more):
                        for t in range(2, HTILES):
                            project(eng, g, t)
                            down(eng, g, t - 2)
                            if t == 3 and more:
                                norm.tensor(eng, g + 1)
                        if more:
                            project(eng, g + 1, 0)
                        down(eng, g, HTILES - 2)
                        down(eng, g, HTILES - 1)
                        if more:
                            project(eng, g + 1, 1)
                    ahead_over_groups(eng, start, body)

    def media_attention():
        TILES = HEADS * HD1 // P
        VHALF = HEADS // 2
        with ExitStack() as own:
            norm, next_norm = media_norm, ff_norm
            context = sb("context", [P, GT], F32, own)
            bias_row = sb("bias_row", [1, 2, GT], BF16, own)
            spare = weights_a[:, 4096:4096 + TILES * GT].rearrange("p (t n) -> p t n", t=TILES)
            q = [sb("q", [P, TILES, GT], F32, own)[:] for _ in range(2)]
            k = [sb("k", [P, TILES, GT], F32, own)[:], spare]
            val = sb("val", [P, 2, GROUP, HEADS, HD1], F32, own)
            jobs = [("k", t) for t in range(TILES)] + [("q", t) for t in range(TILES)] + \
                   [("v", n) for n in range(2 * GROUP)]
            for n, c in (("proj_ready", len(jobs)), ("proj_out_d", len(jobs) // 2), ("proj_out_a", len(jobs) // 2),
                         ("back_out", QUADS // 2), ("out_ready", FC), ("x_done", FC), ("xl_ready", 1)):
                s[n].block(c)
            s["ctx_loaded"].block(1, amount=16)

            def key_mask(eng, g, to, b):
                row = bias_row[0:1, g % 2, b * SEQ:(b + 1) * SEQ].unsqueeze(1).to_broadcast([1, QUAD, SEQ])
                eng.matmul(to, ones_row[:], row, start=True, stop=False, skip_group_check=True)

            def score(g, b, h):
                rows, cols = slice(HD1 * (h % 2), HD1 * (h % 2) + HD1), slice(b * SEQ, (b + 1) * SEQ)
                return q[g % 2][rows, h // 2, cols], k[g % 2][rows, h // 2, cols]

            def post(eng, u):
                g, (b, part) = u // (QUADS // 2), divmod(u % (QUADS // 2), HEADS // QUAD // 2)
                eng.tensor_copy(q[g % 2][:, QUAD * part:QUAD * (part + 1), b * SEQ:(b + 1) * SEQ],
                                bank[4 + u % 2].rearrange("p (t n) -> p t n", t=QUAD)).then_inc(s["back_out"].sem, 1)

            def place(to, n, h):
                return to[HD1 * (n % 2):HD1 * (n % 2 + 1), h * SEQ:(h + 1) * SEQ]

            att = Attention(own, score, key_mask, lambda g, b, q, h: val[:, g % 2, b, media_head(q, h), :], 2, place,
                                  False, post, head=media_head)

            def taken(eng, g, n):
                out_of = s["proj_out_d"] if n % 2 else s["proj_out_a"]
                eng.wait_ge(out_of.sem, out_of.upto(g, n // 2 + 1))

            def mean(eng, g, of=norm, group=None):
                if g:
                    taken(eng, g - 1, len(jobs) - 2)
                    taken(eng, g - 1, len(jobs) - 1)
                of.mean(eng, g if group is None else group)

            def project(eng, g, n):
                kind, t = jobs[n]
                if n < 2:
                    left = norm.dev_ready if n else norm.centre_ready
                    eng.wait_ge(left.sem, left.upto(g, left.per_group))
                    eng.wait_ge(s["ctx_loaded"].sem, s["ctx_loaded"].upto(g, 1))
                elif n in (AFTER_OUTPUT, AFTER_OUTPUT + 1) and g >= 2:
                    eng.wait_ge(s["x_done"].sem, s["x_done"].upto(g - 2, n - AFTER_OUTPUT + 1))
                else:
                    taken(eng, g, n - 2)
                if kind == "q":
                    norm.there(eng, g)
                    f = [(w_q1[:, c, t * P:(t + 1) * P], norm.xn[:, c, :]) for c in range(FC)]
                elif kind == "k":
                    f = [(w_k1[:, t * P:(t + 1) * P], context[:])]
                else:
                    b, half = divmod(t, 2)
                    f = [(context[:, b * SEQ:(b + 1) * SEQ], w_v1[:, half * GT:(half + 1) * GT])]
                product(eng, bank[6 + n % 2], f).then_inc(s["proj_ready"].sem, 1)

            def output(eng, g, m, part):
                if part == 0:
                    if m == 0:
                        eng.wait_ge(s["back_out"].sem, s["back_out"].upto(g, QUADS // 2))
                    if g + 2 < GROUPS:
                        taken(eng, g + 2, AFTER_OUTPUT - 2 + m)
                    elif g + 2 == GROUPS:
                        eng.wait_ge(next_norm.dev_ready.sem, next_norm.dev_ready.upto(0, 1))
                for t in range(part * TILES // 2, (part + 1) * TILES // 2):
                    mm = eng.matmul(bank[6 + m], w_o1[:, t, m * P:(m + 1) * P], q[g % 2][:, t, :], start=t == 0,
                                    stop=t == TILES - 1)
                if part:
                    mm.then_inc(s["out_ready"].sem, 1)

            AFTER_OUTPUT = 8
            slots = [(n, c) for n in range(3, 6) for c in range(3)][1:] + \
                    [(n, c) for n in range(9, 16) for c in range(3)][1:][:len(jobs) - AFTER_OUTPUT]

            def pe_front(eng, g, at, slot):
                if (at, slot) == (0, 0):
                    mean(eng, g)
                elif (at, slot) == (2, 0):
                    norm.tensor(eng, g)
                elif (at, slot) in slots:
                    project(eng, g, slots.index((at, slot)))
                elif (at, slot) == (15, 2):
                    taken(eng, g, len(jobs) - 2)
                    taken(eng, g, len(jobs) - 1)
                    eng.wait_ge(s["xl_ready"].sem, s["xl_ready"].upto(g, 1))

            def pe_back(eng, g, at, slot):
                if 6 <= at <= 9 and slot == 0:
                    output(eng, g, (at - 6) // 2, (at - 6) % 2)

            def take(eng, g, n):
                kind, t = jobs[n]
                eng.wait_ge(s["proj_ready"].sem, s["proj_ready"].upto(g, n + 1))
                src = bank[6 + n % 2]
                if kind == "v":
                    b, half = divmod(t, 2)
                    to = val[:, g % 2, b, VHALF * half:VHALF * (half + 1), :]
                    src = src.rearrange("p (h d) -> p h d", h=VHALF)
                else:
                    to = (q if kind == "q" else k)[g % 2][:, t, :]
                scale = HD1 ** -0.5 if kind == "q" else 1.0
                if n % 2:
                    eng.tensor_scalar(to, src, scale, None, ALU.mult).then_inc(s["proj_out_d"].sem, 1)
                else:
                    eng.activation(to, src, ACT.Copy, scale=scale).then_inc(s["proj_out_a"].sem, 1)

            def centre(eng, g, of=norm, group=None):
                if g:
                    eng.wait_ge(s["proj_ready"].sem, s["proj_ready"].upto(g - 1, 2 * TILES))
                of.centre(eng, g if group is None else group)

            def add(eng, g, m):
                eng.wait_ge(s["out_ready"].sem, s["out_ready"].upto(g, m + 1))
                xs = x_t[:, m, g * GT:(g + 1) * GT]
                eng.scalar_tensor_tensor(out=xs, in0=bank[6 + m], scalar=gates[:, 0:1], in1=xs, op0=ALU.mult,
                                         op1=ALU.add).then_inc(s["x_done"].sem, 1)

            def dve_front(eng, g, at, slot):
                if (at, slot) == (0, 2):
                    centre(eng, g)
                before = (at, slot - 1) if slot else (at - 1, 2)
                if before in slots and slots.index(before) % 2:
                    take(eng, g, slots.index(before))

            def dve_back(eng, g, at, slot):
                if at in (7, 9) and slot == 2:
                    add(eng, g, (at - 7) // 2)

            def act_front(eng, g, at, slot):
                if (at, slot) == (1, 0):
                    norm.square(eng, g)
                elif (at, slot) == (2, 0):
                    norm.inverse_root(eng, g)
                for n, when in enumerate(slots):
                    if when[0] == at and slot == 0 and n % 2 == 0:
                        take(eng, g, n)

            def pe_beyond(eng, at, slot):
                if (at, slot) == (0, 0):
                    eng.wait_ge(s["x_done"].sem, s["x_done"].upto(0, FC))
                    mean(eng, GROUPS, next_norm, 0)
                elif (at, slot) == (2, 0):
                    next_norm.tensor(eng, 0)

            def act_beyond(eng, at, slot):
                if (at, slot) == (1, 0):
                    eng.wait_ge(norm.rstd_ready.sem, norm.rstd_ready.upto(GROUPS, 0))
                    next_norm.square(eng, 0)
                elif (at, slot) == (2, 0):
                    next_norm.inverse_root(eng, 0)

            def dve_beyond(eng, at, slot):
                if (at, slot) == (0, 2):
                    centre(eng, GROUPS, next_norm, 0)

            def pool_front(eng, g, at, slot):
                if (at, slot) == (0, 0):
                    if g >= 2:
                        att.wait(eng, "scores_ready", QUADS * (g - 1))
                    eng.tensor_scalar(bias_row[:, g % 2], keys[:, g * GT // 4:(g + 1) * GT // 4].bitcast(U8), -1.0, -MASKED,
                                      ALU.add, ALU.mult).then_inc(s["xl_ready"].sem, 1)
                    eng.wait_ge(s["xl_ready"].sem, s["xl_ready"].upto(g, 1))
                elif (at, slot) == (4, 0):
                    norm.pool(eng, g)

            def pool_beyond(eng, at, slot):
                if (at, slot) == (4, 0):
                    next_norm.pool(eng, 0)

            with nc.Block() as block:
                @block.sync
                def _(eng):
                    for g in range(GROUPS):
                        if g:
                            eng.wait_ge(s["proj_ready"].sem, s["proj_ready"].upto(g - 1, len(jobs)))
                        eng.dma_start(context[:], a["ctx"][:, g * GT:(g + 1) * GT]).then_inc(s["ctx_loaded"].sem, 16)
                        if g == 0:
                            load_weights(eng, 4)

                @block.gpsimd
                def _(eng):
                    first_front(eng, pool_front)
                    att.pool(eng, around(pool_front, None, pool_beyond))

                @block.scalar
                def _(eng):
                    first_front(eng, act_front)
                    att.scalar(eng, around(act_front, None, act_beyond))

                @block.vector
                def _(eng):
                    first_front(eng, dve_front)
                    att.vector(eng, around(dve_front, dve_back, dve_beyond))
                    for m in range(FC):
                        add(eng, GROUPS - 1, m)

                @block.tensor
                def _(eng):
                    weights_there(eng, 3)
                    first_front(eng, pe_front)
                    att.tensor(eng, around(pe_front, pe_back, pe_beyond))
                    for m in range(FC):
                        for part in range(2):
                            output(eng, GROUPS - 1, m, part)

    def feed_forward():
        TILES = MLP1 // P
        with ExitStack() as own:
            norm = ff_norm
            xn = [sb("xn_part", [P, FC, GT], F32R, own) for _ in range(2)]
            hid = sb("hid", [P, 2, GT], F32, own)
            hid_parts = [sb("hid_part", [P, 4, GT], F32R, own) for _ in range(2)]
            parts_1 = [sb("w_part", [P, FC, MLP1], F32R, own)[:] for _ in range(2)]
            parts_2 = [sb("w_part", [P, TILES, DIM], F32R, own)[:] for _ in range(2)]
            PIECES = 4
            for n, k in (("xnh_ready", 1), ("xnl_ready", 1), ("proj_ready", TILES), ("hid_ready", TILES),
                         ("high_ready", TILES), ("low_ready", TILES), ("hid_free", TILES), ("x_done", FC)):
                s[n].block(k)
            s["wh_ready"].block(2 * PIECES, 1)
            s["wl_ready"].block(2 * PIECES, 1)

            def pieces(n):
                cols = (slice(None), slice(None), slice(n * MLP1 // PIECES, (n + 1) * MLP1 // PIECES))
                rows = (slice(None), slice(n * TILES // PIECES, (n + 1) * TILES // PIECES), slice(None))
                for w, (hi, lo), at in ((w_ff1, parts_1, cols), (w_ff2, parts_2, rows)):
                    yield w[at], hi[at], lo[at]

            def part_free(eng, g, t):
                eng.wait_ge(s["hid_free"].sem, s["hid_free"].upto(g, max(t - 3, 0)))

            with nc.Block() as block:
                @block.sync
                def _(eng):
                    load_weights(eng, 5)

                @block.gpsimd
                def _(eng):
                    for n in range(PIECES):
                        eng.wait_ge(s["wh_ready"].sem, s["wh_ready"].upto(0, 2 * (n + 1)))
                        for w, hi, lo in pieces(n):
                            eng.tensor_tensor(lo, w, hi.bitcast(F32), ALU.subtract).then_inc(s["wl_ready"].sem, 1)

                @block.scalar
                def _(eng):
                    weights_there(eng, 4)

                    def normed_high(g):
                        norm.there(eng, g)
                        eng.wait_ge(s["proj_ready"].sem, s["proj_ready"].upto(g, 0))
                        eng.wait_ge(s["xnl_ready"].sem, s["xnl_ready"].upto(g, 0))
                        eng.activation(xn[0][:], norm.xn[:], ACT.Copy).then_inc(s["xnh_ready"].sem, 1)

                    def start():
                        normed_high(0)
                        for n in range(PIECES):
                            for w, hi, lo in pieces(n):
                                eng.activation(hi, w, ACT.Copy).then_inc(s["wh_ready"].sem, 1)

                    def body(g, more):
                        for t in range(TILES):
                            eng.wait_ge(s["proj_ready"].sem, s["proj_ready"].upto(g, t + 1))
                            eng.wait_ge(s["high_ready"].sem, s["high_ready"].upto(g, max(t - 1, 0)))
                            eng.wait_ge(s["low_ready"].sem, s["low_ready"].upto(g, max(t - 1, 0)))
                            eng.activation(hid[:, t % 2], bank[t % 4], ACT.Gelu).then_inc(s["hid_ready"].sem, 1)
                            eng.wait_ge(s["hid_ready"].sem, s["hid_ready"].upto(g, t + 1))
                            part_free(eng, g, t)
                            eng.activation(hid_parts[0][:, t % 4], hid[:, t % 2], ACT.Copy)\
                               .then_inc(s["high_ready"].sem, 1)
                            if t == 1 and more:
                                norm.square(eng, g + 1)
                                norm.root(eng, g + 1)
                        if more:
                            normed_high(g + 1)
                    ahead_over_groups(eng, start, body)

                @block.vector
                def _(eng):
                    def normed_low(g):
                        eng.wait_ge(s["xnh_ready"].sem, s["xnh_ready"].upto(g, 1))
                        eng.wait_ge(s["proj_ready"].sem, s["proj_ready"].upto(g, 0))
                        eng.tensor_tensor(xn[1][:], norm.xn[:], xn[0][:].bitcast(F32), ALU.subtract)\
                           .then_inc(s["xnl_ready"].sem, 1)

                    def start():
                        normed_low(0)

                    def body(g, more):
                        for t in range(TILES):
                            if t == 1 and more:
                                eng.wait_ge(s["xnl_ready"].sem, s["xnl_ready"].upto(g, 1))
                                norm.centre(eng, g + 1)
                            if t == 4 and more:
                                norm.vector(eng, g + 1)
                            eng.wait_ge(s["high_ready"].sem, s["high_ready"].upto(g, t + 1))
                            part_free(eng, g, t)
                            eng.tensor_tensor(hid_parts[1][:, t % 4], hid[:, t % 2], hid_parts[0][:, t % 4].bitcast(F32),
                                              ALU.subtract).then_inc(s["low_ready"].sem, 1)
                        if more:
                            norm.there(eng, g + 1)
                            normed_low(g + 1)
                        eng.wait_ge(s["hid_free"].sem, s["hid_free"].upto(g, TILES))
                        for m in range(FC):
                            xs = x_t[:, m, bass.ds(g * GT, GT)]
                            eng.scalar_tensor_tensor(out=xs, in0=bank[4 + m], scalar=gates[:, 1:2], in1=xs, op0=ALU.mult,
                                                     op1=ALU.add).then_inc(s["x_done"].sem, 1)
                    ahead_over_groups(eng, start, body)

                @block.tensor
                def _(eng):
                    def start():
                        pass

                    def project(g, t):
                        if t >= 4:
                            eng.wait_ge(s["hid_ready"].sem, s["hid_ready"].upto(g, t - 3))
                        if t % (TILES // PIECES) == 0:
                            n = t // (TILES // PIECES)
                            eng.wait_ge(s["wh_ready"].sem, s["wh_ready"].upto(0, 2 * (n + 1)))
                            eng.wait_ge(s["wl_ready"].sem, s["wl_ready"].upto(0, 2 * (n + 1)))
                        split_product(eng, bank[t % 4], [([part[:, c, t * P:(t + 1) * P] for part in parts_1],
                                                          [part[:, c, :] for part in xn]) for c in range(FC)])\
                            .then_inc(s["proj_ready"].sem, 1)

                    def down(g, t):
                        eng.wait_ge(s["high_ready"].sem, s["high_ready"].upto(g, t + 1))
                        eng.wait_ge(s["low_ready"].sem, s["low_ready"].upto(g, t + 1))
                        if t == 0:
                            eng.wait_ge(s["x_done"].sem, s["x_done"].upto(g, 0))
                        for m in range(FC):
                            mm = split_product(eng, bank[4 + m], [([part[:, t, m * P:(m + 1) * P] for part in parts_2],
                                                                   [part[:, t % 4] for part in hid_parts])],
                                               start=t == 0, stop=t == TILES - 1)
                        mm.then_inc(s["hid_free"].sem, 1)

                    def body(g, more):
                        eng.wait_ge(s["xnh_ready"].sem, s["xnh_ready"].upto(g, 1))
                        eng.wait_ge(s["xnl_ready"].sem, s["xnl_ready"].upto(g, 1))
                        for t in range(TILES + 2):
                            if t < TILES:
                                project(g, t)
                            if t >= 2:
                                down(g, t - 2)
                            if more and t == 0:
                                norm.mean(eng, g + 1)
                            if more and t == 3:
                                norm.tensor(eng, g + 1)
                    ahead_over_groups(eng, start, body)

    def memory_fusion():
        LAYERS = 2
        TURNS = LAYERS * GROUPS
        with ExitStack() as own:
            context = sb("context", [P, GT], F32, own)
            xq = sb("xq", [P, FC, GT], F32, own)
            mem_t = sb("mem_t", [P, FC, GT], F32, own)
            mem = sb("mem", [P, GROUP, DIM], F32, own)
            p = sb("p", [P, GROUP, SEQ], F32, own)
            pn = sb("pn", [P, GROUP, SEQ], F32, own)
            pt = sb("pt", [P, GROUP, SEQ], F32, own)
            nmax = sb("nmax", [P, GROUP], F32, own)
            sums = sb("sums", [P, GROUP], F32, own)
            recip = sb("recip", [P, GROUP], F32, own)
            mix = sb("mix", [P, FC, GT], F32, own)
            gate = sb("gate", [P, FC, GT], F32, own)
            fused = sb("fused", [P, FC, GT], F32, own)
            half_b = sb("half_b", [P, LAYERS, FC], F32, own)
            x_parts = [sb("x_part", [P, FC, GT], F32R, own) for _ in range(2)]
            mix_parts = [sb("mix_part", [P, FC, GT], F32R, own) for _ in range(2)]
            g_parts = [[sb("g_part", [P, 4, DIM], F32R, own) for _ in range(2)] for _ in range(LAYERS)]
            norm = Norm(NORM2, src=fused, groups=TURNS)
            for n, k in (("memt_ready", FC), ("mem_out", FC), ("v_ready", 2), ("v_out_d", 2), ("scores_ready", 1),
                         ("max_ready", 1), ("p_ready", GROUP), ("recip_ready", 1), ("norm_ready", 1), ("turned_ready", 1),
                         ("pt_ready", 1), ("ctx_ready", FC), ("mix_ready", FC), ("proj_ready", FC), ("act_ready", FC),
                         ("res_ready", 3 * FC), ("x_done", FC), ("rot_ready", 1), ("xnh_ready", 1), ("xnl_ready", 1), ("high_ready", 1),
                         ("low_ready", 1)):
                s[n].block(k, TURNS)
            s["ctx_loaded"].block(1, TURNS, 16)
            s["bias_half"].block(LAYERS, 1)
            s["wh_ready"].block(LAYERS, 1)
            s["wl_ready"].block(LAYERS, 1)

            def wait(eng, name, u, n):
                eng.wait_ge(s[name].sem, s[name].upto(u, n))

            def x(u, layer):
                return x_t[:, :, bass.ds((u - layer * GROUPS) * GT, GT)]

            def memory(eng, u, layer):
                weights_there(eng, 5 + layer)
                wait(eng, "ctx_loaded", u, 1)
                wait(eng, "mix_ready", u, 0)
                for c in range(FC):
                    product(eng, bank[c], [(fuse_w[layer][0][:, c * P:(c + 1) * P], context[:])])\
                        .then_inc(s["memt_ready"].sem, 1)
                for half in range(2):
                    for b in (2 * half, 2 * half + 1):
                        mm = product(eng, bank[2 + half][:, (b % 2) * DIM:(b % 2 + 1) * DIM],
                                     [(context[:, b * SEQ:(b + 1) * SEQ], fuse_w[layer][0])])
                    mm.then_inc(s["v_ready"].sem, 1)

            def scores(eng, u, layer):
                wait(eng, "mem_out", u, FC)
                wait(eng, "rot_ready", u, 1)
                for b in range(GROUP):
                    cols = slice(b * SEQ, (b + 1) * SEQ)
                    mm = product(eng, bank[6][:, cols], [(xq[:, c, cols], mem_t[:, c, cols]) for c in range(FC)])
                mm.then_inc(s["scores_ready"].sem, 1)

            def turned(eng, u, layer):
                wait(eng, "norm_ready", u, 1)
                wait(eng, "v_out_d", u, 1)
                for b in range(GROUP):
                    mm = eng.transpose(bank[2][:, b * SEQ:(b + 1) * SEQ], pn[:, b, :], ident[:])
                mm.then_inc(s["turned_ready"].sem, 1)

            def mixed(eng, u, layer):
                wait(eng, "pt_ready", u, 1)
                wait(eng, "v_out_d", u, 2)
                for m in range(FC):
                    for b in range(GROUP):
                        mm = eng.matmul(bank[m][:, b * SEQ:(b + 1) * SEQ], mem[:, b, m * P:(m + 1) * P],
                                        pt[:, b, :], start=True, stop=True)
                    mm.then_inc(s["ctx_ready"].sem, 1)

            def gate_from_x(eng, u, layer):
                eng.wait_ge(s["wh_ready"].sem, s["wh_ready"].upto(0, layer + 1))
                eng.wait_ge(s["wl_ready"].sem, s["wl_ready"].upto(0, layer + 1))
                wait(eng, "xnh_ready", u, 1)
                wait(eng, "xnl_ready", u, 1)
                wait(eng, "act_ready", u, 0)
                for m in range(FC):
                    split_product(eng, bank[4 + m], [([part[:, c, m * P:(m + 1) * P] for part in g_parts[layer]],
                                                      [part[:, c, :] for part in x_parts]) for c in range(FC)], stop=False)

            def gate_from_mix(eng, u, layer, m):
                wait(eng, "high_ready", u, 1)
                wait(eng, "low_ready", u, 1)
                split_product(eng, bank[4 + m], [([part[:, FC + c, m * P:(m + 1) * P] for part in g_parts[layer]],
                                                  [part[:, c, :] for part in mix_parts]) for c in range(FC)], start=False)\
                    .then_inc(s["proj_ready"].sem, 1)

            def queries(eng, u, layer):
                wait(eng, "xnh_ready", u, 0)
                wait(eng, "scores_ready", u, 0)
                eng.activation(xq[:], x(u, layer), ACT.Copy, scale=DIM ** -0.5).then_inc(s["rot_ready"].sem, 1)

            def take_memory(eng, u, layer):
                for c in range(FC):
                    wait(eng, "memt_ready", u, c + 1)
                    eng.activation(mem_t[:, c, :], bank[c], ACT.Copy).then_inc(s["mem_out"].sem, 1)

            def exps(eng, u, layer):
                wait(eng, "max_ready", u, 1)
                wait(eng, "norm_ready", u, 0)
                for b in range(GROUP):
                    eng.activation(p[:, b, :], bank[6][:, b * SEQ:(b + 1) * SEQ], ACT.Exp, bias=nmax[:, b:b + 1],
                                   accum_out=sums[:, b:b + 1]).then_inc(s["p_ready"].sem, 1)

            def tanh(eng, u, layer, m):
                wait(eng, "proj_ready", u, m + 1)
                if m == 0:
                    wait(eng, "res_ready", u, 0)
                eng.activation(gate[:, m, :], bank[4 + m], ACT.Tanh, bias=half_b[:, layer, m:m + 1], scale=0.5)\
                   .then_inc(s["act_ready"].sem, 1)

            def deviation(eng, u, layer):
                wait(eng, "res_ready", u, 3 * FC)
                norm.square(eng, u)
                norm.root(eng, u)

            def x_high(eng, u, layer):
                wait(eng, "proj_ready", u, 0)
                wait(eng, "xnl_ready", u, 0)
                wait(eng, "rot_ready", u, 1)
                eng.activation(x_parts[0][:], xq[:], ACT.Copy, scale=DIM ** 0.5).then_inc(s["xnh_ready"].sem, 1)

            def mix_high(eng, u):
                wait(eng, "mix_ready", u, FC)
                wait(eng, "proj_ready", u, 0)
                wait(eng, "low_ready", u, 0)
                eng.activation(mix_parts[0][:], mix[:], ACT.Copy).then_inc(s["high_ready"].sem, 1)

            def take_values(eng, u, layer):
                wait(eng, "ctx_ready", u, 0)
                for half in range(2):
                    wait(eng, "v_ready", u, half + 1)
                    eng.tensor_copy(mem[:, 2 * half:2 * half + 2, :].rearrange("p b n -> p (b n)"), bank[2 + half])\
                       .then_inc(s["v_out_d"].sem, 1)

            def maximum(eng, u, layer):
                wait(eng, "scores_ready", u, 1)
                wait(eng, "p_ready", u, 0)
                eng.tensor_reduce(nmax[:], bank[6].rearrange("p (b k) -> p b k", b=GROUP), AX_X, ALU.max,
                                  negate=True).then_inc(s["max_ready"].sem, 1)

            def divided(eng, u, layer):
                wait(eng, "p_ready", u, GROUP)
                eng.reciprocal(recip[:], sums[:]).then_inc(s["recip_ready"].sem, 1)
                wait(eng, "recip_ready", u, 1)
                wait(eng, "turned_ready", u, 0)
                eng.tensor_tensor(pn[:], p[:], recip[:].unsqueeze(2).to_broadcast([P, GROUP, SEQ]), ALU.mult)\
                   .then_inc(s["norm_ready"].sem, 1)

            def take_turned(eng, u, layer):
                wait(eng, "turned_ready", u, 1)
                wait(eng, "ctx_ready", u, 0)
                eng.tensor_copy(pt[:].rearrange("p b k -> p (b k)"), bank[2]).then_inc(s["pt_ready"].sem, 1)

            def take_mix(eng, u, layer):
                wait(eng, "proj_ready", u, 0)
                for m in range(FC):
                    wait(eng, "ctx_ready", u, m + 1)
                    eng.tensor_copy(mix[:, m, :], bank[m]).then_inc(s["mix_ready"].sem, 1)

            def fuse(eng, u, layer, m):
                wait(eng, "act_ready", u, m + 1)
                eng.tensor_scalar(gate[:, m, :], gate[:, m, :], 0.5, 0.5, ALU.mult, ALU.add).then_inc(s["res_ready"].sem, 1)
                wait(eng, "res_ready", u, 3 * m + 1)
                eng.tensor_tensor(gate[:, m, :], gate[:, m, :], mix[:, m, :], ALU.mult).then_inc(s["res_ready"].sem, 1)
                wait(eng, "res_ready", u, 3 * m + 2)
                eng.tensor_tensor(fused[:, m, :], gate[:, m, :], x(u, layer)[:, m], ALU.add)\
                   .then_inc(s["res_ready"].sem, 1)

            def finish(eng, u, layer):
                norm.reciprocal(eng, u)
                eng.wait_ge(norm.rstd_ready.sem, norm.rstd_ready.upto(u, 1))
                for m in range(FC):
                    eng.scalar_tensor_tensor(out=x(u, layer)[:, m], in0=fused[:, m, :],
                                             scalar=scales[:, NORM2 + layer, m:m + 1], in1=norm.rstd[:], op0=ALU.mult,
                                             op1=ALU.mult).then_inc(s["x_done"].sem, 1)

            def over_turns(eng, start, body):
                start()
                for layer in range(LAYERS):
                    with eng.Fori(layer * GROUPS, (layer + 1) * GROUPS - 1) as u:
                        body(u, layer, layer)
                    body((layer + 1) * GROUPS - 1, layer, layer + 1 if layer + 1 < LAYERS else None)

            with nc.Block() as block:
                @block.sync
                def _(eng):
                    def load(u, layer):
                        wait(eng, "v_ready", u, 0)
                        eng.dma_start(context[:], a["ctx"][:, bass.ds((u - layer * GROUPS) * GT, GT)])\
                           .then_inc(s["ctx_loaded"].sem, 16)

                    def start():
                        load(0, 0)
                        load_weights(eng, 6)

                    def body(u, layer, after):
                        if after is not None:
                            load(u + 1, after)
                    over_turns(eng, start, body)

                    for g in range(GROUPS):
                        wait(eng, "x_done", TURNS - GROUPS + g, FC)
                        eng.dma_start(out[:, :, g * GT:(g + 1) * GT], x_t[:, :, g * GT:(g + 1) * GT])\
                           .then_inc(s["stores"].sem, 16)
                    eng.wait_ge(s["stores"].sem, 16 * GROUPS)

                @block.gpsimd
                def _(eng):
                    def weights_low(layer):
                        eng.wait_ge(s["wh_ready"].sem, s["wh_ready"].upto(0, layer + 1))
                        eng.tensor_tensor(g_parts[layer][1][:], fuse_w[layer][1], g_parts[layer][0][:].bitcast(F32),
                                          ALU.subtract).then_inc(s["wl_ready"].sem, 1)

                    def x_low(u, layer):
                        wait(eng, "xnh_ready", u, 1)
                        wait(eng, "proj_ready", u, 0)
                        eng.tensor_tensor(x_parts[1][:], x(u, layer), x_parts[0][:].bitcast(F32), ALU.subtract)\
                           .then_inc(s["xnl_ready"].sem, 1)

                    def mix_low(u):
                        wait(eng, "high_ready", u, 1)
                        wait(eng, "proj_ready", u, 0)
                        eng.tensor_tensor(mix_parts[1][:], mix[:], mix_parts[0][:].bitcast(F32), ALU.subtract)\
                           .then_inc(s["low_ready"].sem, 1)

                    def start():
                        weights_low(0)
                        x_low(0, 0)
                        weights_low(1)
                        mix_low(0)

                    def body(u, layer, after):
                        if after is not None:
                            x_low(u + 1, after)
                            mix_low(u + 1)
                    over_turns(eng, start, body)

                @block.scalar
                def _(eng):
                    def weights_high(layer):
                        weights_there(eng, 5 + layer)
                        eng.activation(half_b[:, layer], fuse_w[layer][2], ACT.Copy, scale=0.5)\
                           .then_inc(s["bias_half"].sem, 1)
                        eng.activation(g_parts[layer][0][:], fuse_w[layer][1], ACT.Copy).then_inc(s["wh_ready"].sem, 1)

                    def start():
                        weights_high(0)
                        queries(eng, 0, 0)
                        x_high(eng, 0, 0)
                        take_memory(eng, 0, 0)
                        exps(eng, 0, 0)
                        weights_high(1)
                        eng.wait_ge(s["bias_half"].sem, s["bias_half"].upto(0, LAYERS))
                        mix_high(eng, 0)

                    def body(u, layer, after):
                        more = after is not None
                        if more:
                            queries(eng, u + 1, after)
                            take_memory(eng, u + 1, after)
                            exps(eng, u + 1, after)
                        tanh(eng, u, layer, 0)
                        tanh(eng, u, layer, 1)
                        if more:
                            x_high(eng, u + 1, after)
                        deviation(eng, u, layer)
                        if more:
                            mix_high(eng, u + 1)
                    over_turns(eng, start, body)

                @block.vector
                def _(eng):
                    def start():
                        take_values(eng, 0, 0)
                        maximum(eng, 0, 0)
                        divided(eng, 0, 0)
                        take_turned(eng, 0, 0)
                        take_mix(eng, 0, 0)

                    def body(u, layer, after):
                        more = after is not None
                        if more:
                            take_values(eng, u + 1, after)
                            maximum(eng, u + 1, after)
                            divided(eng, u + 1, after)
                        fuse(eng, u, layer, 0)
                        if more:
                            take_turned(eng, u + 1, after)
                        fuse(eng, u, layer, 1)
                        if more:
                            take_mix(eng, u + 1, after)
                        finish(eng, u, layer)
                    over_turns(eng, start, body)

                @block.tensor
                def _(eng):
                    weights_there(eng, 5)

                    def start():
                        memory(eng, 0, 0)
                        scores(eng, 0, 0)
                        turned(eng, 0, 0)
                        mixed(eng, 0, 0)

                    def body(u, layer, after):
                        more = after is not None
                        if more:
                            memory(eng, u + 1, after)
                        gate_from_x(eng, u, layer)
                        if more:
                            scores(eng, u + 1, after)
                        gate_from_mix(eng, u, layer, 0)
                        gate_from_mix(eng, u, layer, 1)
                        if more:
                            turned(eng, u + 1, after)
                            mixed(eng, u + 1, after)
                        norm.tensor(eng, u)
                    over_turns(eng, start, body)

    self_attention()
    cross_attention()
    expert_mlp()
    media_attention()
    feed_forward()
    memory_fusion()


def _laid_out(i):
    f = np.float32

    def chunks(w):
        return np.ascontiguousarray(w)

    def by_dim(w, hd):
        return w.reshape(w.shape[0], HEADS, hd).transpose(0, 2, 1).reshape(w.shape[0], HEADS * hd)

    def by_feature(v):
        return v.reshape(FC, P).T

    def hidden_columns(v, l):
        rest = np.zeros((v.shape[0], P), v.dtype)
        rest[:, 0:MREST] = v[:, MT * P:]
        rest[:, REST_AT:REST_AT + MREST] = l[:, MT * P:]
        return np.concatenate([rest, v[:, :MT * P], l[:, :MT * P]], axis=1)

    o = {}
    o["x"] = i["x"].reshape(TOKENS, FC, P).transpose(2, 1, 0)
    o["ctx"] = i["ctx_1024"].reshape(TOKENS, CTX).T
    o["tt"] = i["mask_BxS_ik0"].reshape(TOKENS)
    o["keys"] = i["mask_BxS2_bk0"].reshape(1, TOKENS).view(np.int32)
    o["pos"] = i["pos_1xS"].reshape(SEQ)
    for e in "vl":
        qkv = i[f"L0_xattn_{e}_qkv"]
        o[f"{e}_qk"] = np.concatenate([by_dim(qkv[:, :DIM], HD0), by_dim(qkv[:, DIM:2 * DIM], HD0)], axis=1)
        o[f"{e}_v"] = qkv[:, 2 * DIM:]
        o[f"{e}_dense"] = i[f"L0_xattn_{e}_dense"]
    o["cq"] = by_dim(i["L0_xattn_cq_w"], HD0C)
    o["ck"] = by_dim(i["L0_xattn_ckv_w"][:, :P], HD0C)
    o["cv"] = i["L0_xattn_ckv_w"][:, P:]
    o["cdense"] = i["L0_xattn_cdense_w"]
    o["gate0"] = hidden_columns(i["L0_xattn_v_gate"], i["L0_xattn_l_gate"])
    o["up0"] = hidden_columns(i["L0_xattn_v_up"], i["L0_xattn_l_up"])
    o["down0"] = hidden_columns(i["L0_xattn_v_down"].T, i["L0_xattn_l_down"].T).T
    o["wq"] = i["L1_xattn_Wq"]
    o["wo"] = i["L1_xattn_Wo"]
    o["wk"], o["wv"] = i["L1_xattn_Wkv"][:, :HEADS * HD1], i["L1_xattn_Wkv"][:, HEADS * HD1:]
    o["w1"], o["w2"] = i["L1_xattn_W1"], i["L1_xattn_W2"]
    for n in "23":
        o[f"mem{n}"] = i[f"L{n}_xattn_W_mem"].T
        o[f"g{n}"] = i[f"L{n}_xattn_W_gate"].T
        o[f"b{n}"] = by_feature(i[f"L{n}_xattn_b_gate"])
    o["scales"] = np.stack([by_feature(i[n]) for n in (
        "L0_xattn_ln_in_w", "L0_xattn_ln_post_cross_w", "L0_xattn_ln_post_attn_w", "L1_xattn_ln_q_g", "L1_xattn_ln_q_b",
        "L1_xattn_ln_ff_g", "L1_xattn_ln_ff_b", "L2_xattn_norm_w", "L3_xattn_norm_w")], axis=1)
    o["gates"] = np.concatenate([i["L1_xattn_attn_gate"], i["L1_xattn_ff_gate"]])

    inv = (1.0 / ROPE_BASE ** (np.arange(0, HD0, 2, dtype=f) / f(HD0))).astype(f)
    angle = np.outer(np.arange(SEQ, dtype=f), inv).astype(f)
    o["consts"] = np.concatenate([np.repeat(np.cos(angle), HEADS, axis=1), np.repeat(np.sin(angle), HEADS, axis=1),
                                  np.arange(P, dtype=f)[:, None]], axis=1).astype(f)
    o["ident"] = np.eye(P, dtype=f)
    above = np.arange(P)[None, :] > np.arange(P)[:, None]
    o["causal"] = np.where(above, MASKED, 0.0).astype(mybir.dt.np(BF16))
    return {n: np.ascontiguousarray(v) for n, v in o.items()}


def kernel(**inputs):
    import concourse.bacc as bacc
    from concourse.bass_utils import run_bass_kernel_spmd

    arrays = _laid_out({n: np.asarray(v) for n, v in inputs.items()})
    nc = bacc.Bacc("TRN2", target_bir_lowering=False, num_devices=1)
    aps = {n: nc.dram_tensor(f"in_{n}", v.shape, mybir.dt.from_np(v.dtype), kind="ExternalInput").ap()
           for n, v in arrays.items()}
    out = nc.dram_tensor("out_x", (P, FC, TOKENS), F32, kind="ExternalOutput").ap()
    build(nc, aps, out)
    got = run_bass_kernel_spmd(nc, [{f"in_{n}": v for n, v in arrays.items()}], core_ids=[0]).results[0]["out_x"]
    return got.transpose(2, 1, 0).reshape(BATCHES, SEQ, DIM)
```
